# Optimizing a Trainium2 kernel written in Bass

```python
import numpy as np
import jax
import jax.numpy as jnp

def _softmax(x, axis=-1):
    return jax.nn.softmax(x, axis=axis)

def _gelu(x):
    return jax.nn.gelu(x, approximate=True)

def _silu(x):
    return jax.nn.silu(x)

def _sigmoid(x):
    return jax.nn.sigmoid(x)

def _layernorm(x, axis=-1, eps=1e-05):
    m = jnp.mean(x, axis=axis, keepdims=True)
    v = jnp.var(x, axis=axis, keepdims=True)
    return (x - m) / jnp.sqrt(v + eps)

def _scatter_add(tgt, idx, src, axis=0):
    return tgt.at[idx].add(src)

def _segment_sum(src, seg, n):
    return jax.ops.segment_sum(src, seg, n)
kernel_name = 'mk_adaln_d1_jaxref_r8_dee7d3'

def setup_inputs(seed: int=0):
    np.random.seed(seed)
    _w = jnp.asarray

    def _L0_attn_setup():
        import jax, jax.numpy as jnp
        import numpy as np
        H = 256
        NH = 16
        Q_LORA = 192
        KV_LORA = 64
        D_NOPE = 128
        D_ROPE = 64
        D_QK = D_NOPE + D_ROPE
        D_V = 128
        EPS = 1e-06
        THETA = 10000.0
        SCALE = D_QK ** (-0.5)

        def rmsnorm(x, w):
            return x * jax.lax.rsqrt(jnp.mean(x * x, axis=-1, keepdims=True) + EPS) * w

        def rope_cos_sin(seq_len, dtype):
            inv_freq = 1.0 / THETA ** (jnp.arange(0, D_ROPE, 2, dtype=jnp.float32) / D_ROPE)
            pos = jnp.arange(seq_len, dtype=jnp.float32)
            freqs = pos[:, None] * inv_freq[None, :]
            emb = jnp.concatenate([freqs, freqs], axis=-1)
            return (jnp.cos(emb).astype(dtype), jnp.sin(emb).astype(dtype))

        def apply_rope(x, cos, sin):
            half = x.shape[-1] // 2
            x1, x2 = (x[..., :half], x[..., half:])
            rot = jnp.concatenate([-x2, x1], axis=-1)
            c = cos[None, :, None, :]
            s = sin[None, :, None, :]
            return x * c + rot * s
        key = jax.random.key(seed)
        ks = jax.random.split(key, 8)
        f = lambda k, shape: jax.random.normal(k, shape, dtype=jnp.float32) * 0.02
        return {'hidden_states': jax.random.normal(ks[0], (2, 256, H), dtype=jnp.float32), 'wq_a': f(ks[1], (Q_LORA, H)), 'q_norm_w': jnp.ones((Q_LORA,), jnp.float32), 'wq_b': f(ks[2], (NH * D_QK, Q_LORA)), 'wkv_a': f(ks[3], (KV_LORA + D_ROPE, H)), 'kv_norm_w': jnp.ones((KV_LORA,), jnp.float32), 'wkv_b': f(ks[4], (NH * (D_NOPE + D_V), KV_LORA)), 'wo': f(ks[5], (H, NH * D_V))}
    _L0_attn_in = _L0_attn_setup()

    def _L0_ffn_setup():
        import jax, jax.numpy as jnp
        import numpy as np
        B, S, D, DFF = (4, 512, 256, 1024)
        CAPACITY_FACTOR = 0.5
        K = int(CAPACITY_FACTOR * S)
        key = jax.random.key(seed)
        ks = jax.random.split(key, 5)
        hidden_states = jax.random.normal(ks[0], (B, S, D), dtype=jnp.float32)
        router_weight = jax.random.normal(ks[1], (D,), dtype=jnp.float32) * 0.02
        router_bias = jnp.zeros((1,), dtype=jnp.float32)
        w1 = jax.random.normal(ks[2], (D, DFF), dtype=jnp.float32) * (1.0 / np.sqrt(D))
        b1 = jnp.zeros((DFF,), dtype=jnp.float32)
        w2 = jax.random.normal(ks[3], (DFF, D), dtype=jnp.float32) * (1.0 / np.sqrt(DFF))
        b2 = jnp.zeros((D,), dtype=jnp.float32)
        return {'hidden_states': hidden_states, 'router_weight': router_weight, 'router_bias': router_bias, 'w1': w1, 'b1': b1, 'w2': w2, 'b2': b2}
    _L0_ffn_in = _L0_ffn_setup()
    _L0_c = _w((lambda *s: np.random.randn(*s).astype(np.float32) * 0.05)(16, 256))
    _L0_wmod = _w((lambda *s: np.random.randn(*s).astype(np.float32) * 0.05)(256, 6 * 256) * 256 ** (-0.5))
    _d = {'L0_attn_hidden_states': _L0_attn_in['hidden_states'], 'L0_attn_wq_a': _L0_attn_in['wq_a'], 'L0_attn_q_norm_w': _L0_attn_in['q_norm_w'], 'L0_attn_wq_b': _L0_attn_in['wq_b'], 'L0_attn_wkv_a': _L0_attn_in['wkv_a'], 'L0_attn_kv_norm_w': _L0_attn_in['kv_norm_w'], 'L0_attn_wkv_b': _L0_attn_in['wkv_b'], 'L0_attn_wo': _L0_attn_in['wo'], 'L0_ffn_router_weight': _L0_ffn_in['router_weight'], 'L0_ffn_router_bias': _L0_ffn_in['router_bias'], 'L0_ffn_w1': _L0_ffn_in['w1'], 'L0_ffn_b1': _L0_ffn_in['b1'], 'L0_ffn_w2': _L0_ffn_in['w2'], 'L0_ffn_b2': _L0_ffn_in['b2'], 'L0_c': _L0_c, 'L0_wmod': _L0_wmod}
    _x0 = _d['L0_attn_hidden_states']
    _d['L0_attn_hidden_states'] = jax.random.normal(jax.random.fold_in(jax.random.key(seed), 1), (16, 256, 256), dtype=_x0.dtype)
    del _x0
    return _d

def reference(L0_attn_hidden_states, L0_attn_wq_a, L0_attn_q_norm_w, L0_attn_wq_b, L0_attn_wkv_a, L0_attn_kv_norm_w, L0_attn_wkv_b, L0_attn_wo, L0_ffn_router_weight, L0_ffn_router_bias, L0_ffn_w1, L0_ffn_b1, L0_ffn_w2, L0_ffn_b2, L0_c, L0_wmod):

    def _L0_attn_ref(hidden_states, wq_a, q_norm_w, wq_b, wkv_a, kv_norm_w, wkv_b, wo):
        import jax, jax.numpy as jnp
        import numpy as np
        H = 256
        NH = 16
        Q_LORA = 192
        KV_LORA = 64
        D_NOPE = 128
        D_ROPE = 64
        D_QK = D_NOPE + D_ROPE
        D_V = 128
        EPS = 1e-06
        THETA = 10000.0
        SCALE = D_QK ** (-0.5)

        def rmsnorm(x, w):
            return x * jax.lax.rsqrt(jnp.mean(x * x, axis=-1, keepdims=True) + EPS) * w

        def rope_cos_sin(seq_len, dtype):
            inv_freq = 1.0 / THETA ** (jnp.arange(0, D_ROPE, 2, dtype=jnp.float32) / D_ROPE)
            pos = jnp.arange(seq_len, dtype=jnp.float32)
            freqs = pos[:, None] * inv_freq[None, :]
            emb = jnp.concatenate([freqs, freqs], axis=-1)
            return (jnp.cos(emb).astype(dtype), jnp.sin(emb).astype(dtype))

        def apply_rope(x, cos, sin):
            half = x.shape[-1] // 2
            x1, x2 = (x[..., :half], x[..., half:])
            rot = jnp.concatenate([-x2, x1], axis=-1)
            c = cos[None, :, None, :]
            s = sin[None, :, None, :]
            return x * c + rot * s
        B, S, _ = hidden_states.shape
        q = rmsnorm(hidden_states @ wq_a.T, q_norm_w) @ wq_b.T
        q = q.reshape(B, S, NH, D_QK)
        q_nope, q_pe = (q[..., :D_NOPE], q[..., D_NOPE:])
        kv = hidden_states @ wkv_a.T
        kv_c, k_pe = (kv[..., :KV_LORA], kv[..., KV_LORA:])
        cos, sin = rope_cos_sin(S, hidden_states.dtype)
        q_pe = apply_rope(q_pe, cos, sin)
        k_pe = apply_rope(k_pe[:, :, None, :], cos, sin)
        kv_dec = rmsnorm(kv_c, kv_norm_w) @ wkv_b.T
        kv_dec = kv_dec.reshape(B, S, NH, D_NOPE + D_V)
        k_nope, v = (kv_dec[..., :D_NOPE], kv_dec[..., D_NOPE:])
        qf = jnp.concatenate([q_nope, q_pe], axis=-1)
        kf = jnp.concatenate([k_nope, jnp.broadcast_to(k_pe, (B, S, NH, D_ROPE))], axis=-1)
        scores = jnp.einsum('bqhd,bkhd->bhqk', qf, kf) * SCALE
        causal = jnp.tril(jnp.ones((S, S), dtype=bool))
        scores = jnp.where(causal[None, None], scores, jnp.finfo(scores.dtype).min)
        probs = jax.nn.softmax(scores, axis=-1)
        attn = jnp.einsum('bhqk,bkhd->bqhd', probs, v)
        return attn.reshape(B, S, NH * D_V) @ wo.T

    def _L0_ffn_ref(hidden_states, router_weight, router_bias, w1, b1, w2, b2):
        import jax, jax.numpy as jnp
        import numpy as np
        B, S, D, DFF = (4, 512, 256, 1024)
        CAPACITY_FACTOR = 0.5
        K = int(CAPACITY_FACTOR * S)
        b, s, d = hidden_states.shape
        scores = jnp.einsum('bsd,d->bs', hidden_states, router_weight) + router_bias[0]
        top_scores, indices = jax.lax.top_k(scores, K)
        weights = jax.nn.sigmoid(top_scores)
        selected = jnp.take_along_axis(hidden_states, indices[:, :, None], axis=1)
        h = jax.nn.gelu(jnp.einsum('bkd,df->bkf', selected, w1) + b1)
        processed = jnp.einsum('bkf,fd->bkd', h, w2) + b2
        weighted = processed * weights[:, :, None]
        flat = hidden_states.reshape(b * s, d)
        flat_idx = (indices + jnp.arange(b)[:, None] * s).reshape(-1)
        out = flat.at[flat_idx].add(weighted.reshape(b * K, d))
        return out.reshape(b, s, d)
    x = L0_attn_hidden_states
    mod = (_silu(L0_c) @ L0_wmod).reshape(L0_c.shape[0], 6, 1, -1)
    sa, ca, ga, sb, cb, gb = (mod[:, 0], mod[:, 1], mod[:, 2], mod[:, 3], mod[:, 4], mod[:, 5])
    ga = (2 * (ga >= 0) - 1) * jnp.maximum(jnp.abs(ga), 0.25)
    gb = (2 * (gb >= 0) - 1) * jnp.maximum(jnp.abs(gb), 0.25)
    h = _layernorm(x, axis=-1) * (1 + ca) + sa
    x = x + ga * _L0_attn_ref(h, L0_attn_wq_a, L0_attn_q_norm_w, L0_attn_wq_b, L0_attn_wkv_a, L0_attn_kv_norm_w, L0_attn_wkv_b, L0_attn_wo)
    h = _layernorm(x, axis=-1) * (1 + cb) + sb
    x = x + gb * _L0_ffn_ref(h, L0_ffn_router_weight, L0_ffn_router_bias, L0_ffn_w1, L0_ffn_b1, L0_ffn_w2, L0_ffn_b2)
    return x

_drawn_inputs = setup_inputs


def setup_inputs(seed=0):
    import zlib

    import numpy as np

    out = dict(_drawn_inputs(seed))
    spreads = {'L0_attn_q_norm_w': (1.0, 0.6),
     'L0_attn_kv_norm_w': (1.0, 0.6),
     'L0_ffn_b1': (0.0, 2.0),
     'L0_ffn_b2': (0.0, 0.677)}
    factors = {'L0_attn_wq_a': 8.0,
     'L0_attn_wq_b': 8.0,
     'L0_attn_wkv_a': 8.0,
     'L0_attn_wkv_b': 8.0,
     'L0_attn_wo': 8.0,
     'L0_ffn_router_weight': 4.496}
    for name, (base, spread) in spreads.items():
        noise = np.random.default_rng([zlib.crc32(name.encode()), seed]).standard_normal(out[name].shape)
        drawn = base * np.exp(spread * noise) if base else spread * noise
        out[name] = jnp.asarray(drawn.astype(out[name].dtype))
    for name, factor in factors.items():
        out[name] = (out[name] * factor).astype(out[name].dtype)
    return out
```

```python
from contextlib import ExitStack

import numpy as np
import concourse.bass as bass
from concourse import mybir

F32 = mybir.dt.float32
F32R = mybir.dt.float32r
ACT = mybir.ActivationFunctionType
ALU = mybir.AluOpType

P = 128
B, S, D = 16, 256, 256
NH, QL, KL, DR, DN, DV = 16, 192, 64, 64, 128, 128
DFF = 1024
NT = S // P
KD = D // P
NP = NH // 2
WA = QL + KL + DR
KW1 = QL - P
SCORE = 3 * P
NF = DFF // P
SCALE = float(DN + DR) ** -0.5
LN_EPS, RMS_EPS = 1e-5, 1e-6
MASKED = -3.0e38
SWAP16 = [(i + 16) % 32 for i in range(32)]
RUNS = [(half, g) for g in range(2) for half in range(2)]


def adaln_layer(nc, x, wq_a, q_norm_w, wq_b, wkv_a, kv_norm_w, wkv_b, wo, router_w, router_b,
                w1, b1, w2, b2, c, wmod, ident_in, mask_in, rope_rows, rope_tokens, out):
    mod_rows = nc.dram_tensor("mod_rows", (B, 4 * D), F32, kind="Internal").ap()

    with ExitStack() as ctx:
        def sb(name, shape, dt=F32, own=ctx):
            return own.enter_context(nc.sbuf_tensor(name, shape, dt))

        def sem(name):
            return ctx.enter_context(nc.semaphore(name))

        bank = [ctx.enter_context(nc.psum_tensor(f"bank{i}", [P, 512], F32)) for i in range(8)]

        x_sb = sb("x_sb", [P, B * NT * D])
        ident = sb("ident", [P, P])
        mod_t = sb("mod_t", [P, 4 * B])
        tok_stat = sb("tok_stat", [P, B * NT, 2])
        tok_rstd = sb("tok_rstd", [P, B * NT])
        tok_shift = sb("tok_shift", [P, B * NT])
        bn_raw = sb("bn_raw", [P, NT, 6])
        spare = sb("spare", [P, 64])
        bn_tile = sb("bn_tile", [P, NT, 2])
        half_neg = sb("half_neg", [P, B * NT])

        a_ctx = ExitStack()
        wa_hi = sb("wa_hi", [P, KD * WA], F32R, a_ctx)
        wa_lo = sb("wa_lo", [P, KD * WA], F32R, a_ctx)
        wq_hi0 = sb("wq_hi0", [P, NP * 256], F32R, a_ctx)
        wq_lo0 = sb("wq_lo0", [P, NP * 256], F32R, a_ctx)
        wq_hi1 = sb("wq_hi1", [KW1, NP * 256], F32R, a_ctx)
        wq_lo1 = sb("wq_lo1", [KW1, NP * 256], F32R, a_ctx)
        wout_hi = sb("wout_hi", [P, NP * D], F32R, a_ctx)
        wout_lo = sb("wout_lo", [P, NP * D], F32R, a_ctx)
        mask_pad = sb("mask_pad", [P, 2 * P], F32, a_ctx)
        rope = sb("rope", [P, 2 * S], F32, a_ctx)
        rope_tok = sb("rope_tok", [P, NT, 2 * DR], F32, a_ctx)
        inv_n = sb("inv_n", [P, 2 * NT], F32, a_ctx)
        rms_eps = sb("rms_eps", [P, 2 * NT], F32, a_ctx)
        qn_t0 = sb("qn_t0", [P, (B + 1) * S], F32, a_ctx)
        qn_t1 = sb("qn_t1", [KW1, (B + 1) * S], F32, a_ctx)
        key_a = sb("key_a", [P, B * S], F32, a_ctx)
        key_b = sb("key_b", [P, B * S], F32, a_ctx)
        lat = sb("lat", [P, B * NT * KL], F32, a_ctx)

        s_ctx = ExitStack()
        wqa_nat = sb("wqa_nat", [P, 2, D], F32, s_ctx)
        wkva_nat = sb("wkva_nat", [P, D], F32, s_ctx)
        c_nat = sb("c_nat", [B, 4, D], F32, s_ctx)
        silu = sb("silu", [B, D], F32, s_ctx)
        silu_t = sb("silu_t", [P, KD * B], F32, s_ctx)
        mod_nat = sb("mod_nat", [B, 6 * D], F32, s_ctx)
        gate_sign = sb("gate_sign", [B, 2, 2 * D], F32, s_ctx)
        gate_abs = sb("gate_abs", [B, 2 * D], F32, s_ctx)
        mod_out = sb("mod_out", [B, 4 * D], F32, s_ctx)
        qw = sb("qw", [P, 2], F32, s_ctx)
        kw_col = sb("kw_col", [P, 1], F32, s_ctx)
        kw_row = sb("kw_row", [P, 256], F32, s_ctx)
        wq_tmp0 = sb("wq_tmp0", [P, 2, 256], F32, s_ctx)
        wq_tmp1 = sb("wq_tmp1", [KW1, 2, 256], F32, s_ctx)
        wmod_nat = x_sb[:, B * NT * D // 2:B * NT * D // 2 + KD * 6 * D].rearrange("p (k n) -> p k n", k=KD)
        wqn_nat = qn_t0[:, 0:NH * QL].rearrange("p (h r) -> p h r", h=NH)
        wqp_nat = lat[:, 0:NP * QL].rearrange("p (h r) -> p h r", h=NP)
        wkv_nat = sb("wkv_nat", [P, NH * 2, KL], F32, s_ctx)
        wo_nat = key_a[:, :].rearrange("p (t n) -> p t n", t=2)
        wo_t = key_b[:, :].rearrange("p (h o) -> p h o", h=NH)
        s_ctx.close()

        p_ctx = ExitStack()
        xhat = sb("xhat", [P, 2, NT * D], F32, p_ctx)
        mod_col = sb("mod_col", [P, 2, 4], F32, p_ctx)
        h_t = sb("h_t", [P, 2, KD * S], F32, p_ctx)
        h_hi = sb("h_hi", [P, 2, KD * S], F32R, p_ctx)
        h_lo = sb("h_lo", [P, 2, KD * S], F32R, p_ctx)
        sq_junk = sb("sq_junk", [P, 2, NT, QL + KL], F32, p_ctx)
        sumsq = sb("sumsq", [P, 2, 2 * NT], F32, p_ctx)
        rms_mid = sb("rms_mid", [P, 2, 2 * NT], F32, p_ctx)
        rms_var = sb("rms_var", [P, 2, 2 * NT], F32, p_ctx)
        rms_r = sb("rms_r", [P, 2, 2 * NT], F32, p_ctx)
        qn = sb("qn", [P, 2, NT * QL], F32, p_ctx)
        keys = sb("keys", [P, 2, NT * 192], F32, p_ctx)
        kr_cos = sb("kr_cos", [P, 2, NT * DR], F32, p_ctx)
        kr_sin = sb("kr_sin", [P, 2, NT * DR], F32, p_ctx)
        p_ctx.close()

        q_hi0 = sb("q_hi0", [P, S], F32R, a_ctx)
        q_lo0 = sb("q_lo0", [P, S], F32R, a_ctx)
        q_hi1 = sb("q_hi1", [KW1, S], F32R, a_ctx)
        q_lo1 = sb("q_lo1", [KW1, S], F32R, a_ctx)
        gate_a = sb("gate_a", [P, D], F32, a_ctx)
        query = sb("query", [P, 2, 2, S], F32, a_ctx)
        pe_cos = sb("pe_cos", [P, 2, S], F32, a_ctx)
        pe_rot = sb("pe_rot", [P, 2, S], F32, a_ctx)
        pe_sin = sb("pe_sin", [P, 2, S], F32, a_ctx)
        scored = sb("scored", [P, 2, 2, SCORE], F32, a_ctx)
        row_min = sb("row_min", [P, 2, 4], F32, a_ctx)
        probs = sb("probs", [P, 2, 2, SCORE], F32, a_ctx)
        row_sum = sb("row_sum", [P, 2, 4], F32, a_ctx)
        row_inv = sb("row_inv", [P, 2, 4], F32, a_ctx)
        probs_t = sb("probs_t", [P, 2, SCORE], F32, a_ctx)
        o_nat = sb("o_nat", [P, 2, 256], F32, a_ctx)
        o_hi = sb("o_hi", [P, 256], F32R, a_ctx)
        o_lo = sb("o_lo", [P, 256], F32R, a_ctx)
        gated = sb("gated", [P, NT * D], F32, a_ctx)
        a_ctx.close()

        w1_hi = sb("w1_hi", [P, KD * DFF], F32R)
        w1_lo = sb("w1_lo", [P, KD * DFF], F32R)
        w2_hi = sb("w2_hi", [P, NF * D], F32R)
        w2_lo = sb("w2_lo", [P, NF * D], F32R)
        w1_nat = sb("w1_nat", [P, KD * DFF])
        w2_nat = sb("w2_nat", [P, NF * D])
        b1_col = sb("b1_col", [P, NF])
        b2_row = sb("b2_row", [P, D])
        rw_row = sb("rw_row", [P, D])
        rb_col = sb("rb_col", [P, 2])
        mod_b = sb("mod_b", [P, 2, 3 * D])
        h2 = sb("h2", [P, 2, NT * D])
        h2_n = sb("h2_n", [P, NT * D])
        h2_m = sb("h2_m", [P, NT * D])
        h2_hi = sb("h2_hi", [P, KD * S], F32R)
        h2_lo = sb("h2_lo", [P, KD * S], F32R)
        f_bn = sb("f_bn", [P, NT, 6])
        f_stat = sb("f_stat", [P, NT, 2])
        f_var = sb("f_var", [P, NT])
        f_rstd = sb("f_rstd", [P, NT])
        f_shift = sb("f_shift", [P, NT])
        rout_junk = sb("rout_junk", [P, NT, D])
        rout = sb("rout", [P, 2, NT])
        rout_t = sb("rout_t", [P, 2, NT])
        rout_w = sb("rout_w", [P, 2, NT])
        act_hi = sb("act_hi", [P, NF * S], F32R)
        act_full = sb("act_full", [P, NF * S])
        act_lo = sb("act_lo", [P, NF * S], F32R)
        f_sum = sb("f_sum", [P, NT * D])
        f_mix = sb("f_mix", [P, NT * D])
        f_gate = sb("f_gate", [P, NT * D])
        f_out = sb("f_out", [P, 2, NT * D])

        ld_small = sem("ld_small")
        ld_first = sem("ld_first")
        ld_mod = sem("ld_mod")
        ld_wo = sem("ld_wo")
        ld_heads = sem("ld_heads")
        ld_x = sem("ld_x")
        mod_stored = sem("mod_stored")
        ld_c = sem("ld_c")
        ld_kwr = sem("ld_kwr")
        kwr_done = sem("kwr_done")
        exp_c = sem("exp_c")
        vec_step = sem("vec_step")
        pool_step = sem("pool_step")
        silu_done = sem("silu_done")
        s_wa_t = sem("s_wa_t")
        s_wa_hi = sem("s_wa_hi")
        s_silu_t = sem("s_silu_t")
        s_silu_sb = sem("s_silu_sb")
        s_mod = sem("s_mod")
        s_mod_sb = sem("s_mod_sb")
        mod_out_done = sem("mod_out_done")
        s_modt = sem("s_modt")
        s_modt_sb = sem("s_modt_sb")
        s_wo_t = sem("s_wo_t")
        s_wo_sb = sem("s_wo_sb")
        s_wout = sem("s_wout")
        s_wout_free = sem("s_wout_free")
        s_wq = sem("s_wq")
        s_wq_tmp = sem("s_wq_tmp")
        s_wq_hi = sem("s_wq_hi")
        s_wq_lo = sem("s_wq_lo")
        bn_kept = sem("bn_kept")
        var_done = sem("var_done")
        rstd_done = sem("rstd_done")
        pad_done = sem("pad_done")
        p_xhat = sem("p_xhat")
        p_ht = sem("p_ht")
        p_mod = sem("p_mod")
        p_hsb = sem("p_hsb")
        p_split = sem("p_split")
        p_proj = sem("p_proj")
        p_sq = sem("p_sq")
        p_rms = sem("p_rms")
        p_norm = sem("p_norm")
        p_t = sem("p_t")
        p_kept = sem("p_kept")
        gate_loaded = sem("gate_loaded")
        q_hi_done = sem("q_hi_done")
        q_split = sem("q_split")
        a_qgen = sem("a_qgen")
        a_rot = sem("a_rot")
        a_latq = sem("a_latq")
        a_query = sem("a_query")
        a_score = sem("a_score")
        a_masked = sem("a_masked")
        a_exp = sem("a_exp")
        a_ptr = sem("a_ptr")
        a_pt_a = sem("a_pt_a")
        a_pt_b = sem("a_pt_b")
        a_inv = sem("a_inv")
        a_pv = sem("a_pv")
        a_onat = sem("a_onat")
        a_otr = sem("a_otr")
        a_ohi = sem("a_ohi")
        a_olo = sem("a_olo")
        a_out = sem("a_out")
        a_batch = sem("a_batch")
        a_gated = sem("a_gated")
        a_added = sem("a_added")
        ld_ffn = sem("ld_ffn")
        ld_modb = sem("ld_modb")
        f_hi_w = sem("f_hi_w")
        f_w = sem("f_w")
        f_var_done = sem("f_var_done")
        f_rstd_done = sem("f_rstd_done")
        f_h2 = sem("f_h2")
        f_rout = sem("f_rout")
        f_tanh = sem("f_tanh")
        mix_step = sem("mix_step")
        f_ht = sem("f_ht")
        f_hhi = sem("f_hhi")
        f_hsplit = sem("f_hsplit")
        f_up = sem("f_up")
        f_act = sem("f_act")
        f_lo = sem("f_lo")
        f_down = sem("f_down")
        f_mixed = sem("f_mixed")
        f_gated = sem("f_gated")
        f_done = sem("f_done")
        stored = [sem("stored_even"), sem("stored_odd")]
        left = {e: sem(f"left_{e}") for e in ("tensor", "vector", "scalar", "gpsimd", "sync")}

        def leave(eng, own):
            eng.sem_inc(left[own], 1)

        def enter(eng, own, n):
            for e, s in left.items():
                if e != own:
                    eng.wait_ge(s, n)

        block = ctx.enter_context(nc.Block())

        @block.sync
        def _(sp):
            sp.dma_start(ident[:, :], ident_in).then_inc(ld_small, 16)
            sp.dma_start(wqa_nat[:, 0, :], wq_a[0:P, :]).then_inc(ld_first, 16)
            sp.dma_start(wqa_nat[0:KW1, 1, :], wq_a[P:QL, :]).then_inc(ld_first, 16)
            sp.dma_start(wkva_nat[:, :], wkv_a).then_inc(ld_first, 16)
            sp.dma_start(wmod_nat, wmod.rearrange("(k p) n -> p k n", p=P)).then_inc(ld_mod, 16)
            sp.dma_start(wo_nat, wo.rearrange("(t p) n -> p t n", p=P)).then_inc(ld_wo, 16)
            heads = wq_b.rearrange("(h d) r -> d h r", d=DN + DR)
            sp.dma_start(wqn_nat, heads[0:DN, :, :]).then_inc(ld_heads, 16)
            sp.dma_start(wkv_nat[:, :, :], wkv_b.rearrange("(h d) c -> d h c", d=P)).then_inc(ld_heads, 16)
            by_pair = wq_b.rearrange("(g t d) r -> d t g r", t=2, d=DN + DR)
            for place, head in enumerate((1, 0)):
                for n, (half, g) in enumerate(RUNS):
                    row, d = place * DR + n * 16, DN + half * 32 + g * 16
                    sp.dma_start(wqp_nat[row:row + 16, :, :], by_pair[d:d + 16, head, :, :]).then_inc(ld_heads, 16)
            x_rows = x.rearrange("b (t p) d -> p (b t) d", p=P)
            out_rows = out.rearrange("b (t p) d -> p (b t) d", p=P)
            x_tiles = x_sb[:, :].rearrange("p (n d) -> p n d", d=D)
            for i in range(4):
                n = B * NT // 4
                if i == 2:
                    sp.wait_ge(s_mod, 1)
                sp.dma_start(x_tiles[:, n * i:n * i + n, :], x_rows[:, n * i:n * i + n, :]).then_inc(ld_x, 16)
            sp.wait_ge(mod_out_done, 1)
            sp.dma_start(mod_rows, mod_out[:, :]).then_inc(mod_stored, 16)
            sp.wait_ge(mod_stored, 16)
            leave(sp, "sync")
            leave(sp, "sync")

            enter(sp, "sync", 2)
            sp.dma_start(gate_a[:, :], mod_rows[0:1, 0:D].broadcast_to([P, D])).then_inc(gate_loaded, 16)
            with sp.Fori(1, B) as b:
                sp.wait_ge(a_gated, b)
                sp.dma_start(gate_a[:, :], mod_rows[bass.ds(b, 1), 0:D].broadcast_to([P, D])).then_inc(gate_loaded, 16)

            leave(sp, "sync")

            enter(sp, "sync", 3)
            sp.dma_start(w1_nat[:, :].rearrange("p (k n) -> p k n", k=KD), w1.rearrange("(k p) n -> p k n", p=P)).then_inc(ld_ffn, 16)
            sp.dma_start(w2_nat[:, :].rearrange("p (k n) -> p k n", k=NF), w2.rearrange("(k p) n -> p k n", p=P)).then_inc(ld_ffn, 16)
            sp.dma_start(b1_col[:, :], b1).then_inc(ld_ffn, 16)
            sp.dma_start(b2_row[:, :], b2.rearrange("(a n) -> a n", a=1).broadcast_to([P, D])).then_inc(ld_ffn, 16)
            sp.dma_start(rw_row[:, :], router_w.rearrange("(a n) -> a n", a=1).broadcast_to([P, D])).then_inc(ld_ffn, 16)
            sp.dma_start(rb_col[:, 0:1], router_b.rearrange("(a n) -> a n", a=1).broadcast_to([P, 1])).then_inc(ld_ffn, 16)
            sp.dma_start(mod_b[:, 0, :], mod_rows[0:1, D:4 * D].broadcast_to([P, 3 * D])).then_inc(ld_modb, 16)
            sp.wait_ge(ld_modb, 16)
            sp.dma_start(mod_b[:, 1, :], mod_rows[1:2, D:4 * D].broadcast_to([P, 3 * D])).then_inc(ld_modb, 16)

            def store(b, slot):
                sp.wait_ge(f_done, b + 1)
                sp.dma_start(out_rows[:, bass.ds(b * NT, NT), :],
                             f_out[:, slot, :].rearrange("p (t d) -> p t d", d=D)).then_inc(stored[slot], 16)

            def next_mod(b, slot):
                sp.wait_ge(f_gated, b + 1)
                sp.wait_ge(ld_modb, 16 * (b + 2))
                sp.dma_start(mod_b[:, slot, :], mod_rows[bass.ds(b + 2, 1), D:4 * D].broadcast_to([P, 3 * D])).then_inc(ld_modb, 16)

            with sp.Fori(0, B // 2 - 1) as i:
                for slot in range(2):
                    next_mod(2 * i + slot, slot)
                    store(2 * i + slot, slot)
            for slot in range(2):
                store(B - 2 + slot, slot)
            for slot in range(2):
                sp.wait_ge(stored[slot], 16 * (B // 2))

        @block.tensor
        def _(pe):
            mm = nc.tensor.matmul

            def three(out_ap, left_hl, right_hl, start, stop, **kw):
                (lh, ll), (rh, rl) = left_hl, right_hl
                mm(out_ap, lh, rh, start=start, stop=False, **kw)
                mm(out_ap, ll, rh, start=False, stop=False, **kw)
                return mm(out_ap, lh, rl, start=False, stop=stop, **kw)

            pe.wait_ge(ld_small, 16 * 8)
            pe.wait_ge(ld_first, 48)
            for k in range(KD):
                cols = slice(k * P, k * P + P)
                nc.tensor.transpose(bank[k][:, 0:P], wqa_nat[:, 0, cols], ident[:, :])
                nc.tensor.transpose(bank[k][:, P:QL], wqa_nat[0:KW1, 1, cols], ident[0:KW1, 0:KW1])
                nc.tensor.transpose(bank[k][:, QL:WA], wkva_nat[:, cols], ident[:, :]).then_inc(s_wa_t, 1)
            pe.wait_ge(silu_done, 1)
            for k in range(KD):
                last = nc.tensor.transpose(bank[2][:, k * B:k * B + B], silu[:, k * P:k * P + P], ident[0:B, 0:B])
            last.then_inc(s_silu_t, 1)
            pe.wait_ge(s_silu_sb, 1)
            pe.wait_ge(ld_mod, 16)
            for n in range(3):
                for k in range(KD):
                    last = mm(bank[3 + n][0:B, :], silu_t[:, k * B:k * B + B], wmod_nat[:, k, n * 512:n * 512 + 512],
                              start=(k == 0), stop=(k == KD - 1))
            last.then_inc(s_mod, 1)
            pe.wait_ge(s_mod_sb, 1)
            for n in range(4):
                last = nc.tensor.transpose(bank[6][:, n * B:n * B + B], mod_nat[:, n * P:n * P + P], ident[0:B, 0:B])
            last.then_inc(s_modt, 1)
            pe.wait_ge(ld_wo, 16)
            pe.wait_ge(s_wa_hi, 2)
            for n in range(NP):
                if n >= 2:
                    pe.wait_ge(s_wo_sb, n - 1)
                for j in range(4):
                    h, t = 2 * n + j // 2, j % 2
                    last = nc.tensor.transpose(bank[n % 2][:, j * P:j * P + P], wo_nat[:, t, h * P:h * P + P], ident[:, :])
                last.then_inc(s_wo_t, 1)
            pe.wait_ge(ld_heads, 16 * 10)
            pe.wait_ge(s_mod_sb, 1)
            for n in range(NP):
                pe.wait_ge(s_wo_sb, n + 1)
                if n == 0:
                    pe.wait_ge(s_silu_sb, 1)
                if n >= 2:
                    pe.wait_ge(s_wout_free, n - 1)
                for j in range(2):
                    h = 2 * n + j
                    last = mm(bank[2 + n % 2][64 * j:64 * j + 64, 0:D], wkv_nat[:, 2 * h + 1, :], wo_t[:, h, :], start=True, stop=True)
                last.then_inc(s_wout, 1)
                if n >= 2:
                    pe.wait_ge(s_wq_tmp, n - 1)
                q = bank[4 + n % 2]
                for j in range(2):
                    h = 2 * n + j
                    mm(q[:, j * 64:j * 64 + 64], wqn_nat[:, h, 0:P], wkv_nat[:, 2 * h, :], start=True, stop=True)
                    mm(q[0:KW1, 256 + j * 64:320 + j * 64], wqn_nat[:, h, P:QL], wkv_nat[:, 2 * h, :], start=True, stop=True)
                nc.tensor.transpose(q[:, P:2 * P], wqp_nat[:, n, 0:P], ident[:, :])
                nc.tensor.transpose(q[0:KW1, 3 * P:4 * P], wqp_nat[:, n, P:QL], ident[:, :]).then_inc(s_wq, 1)
            leave(pe, "tensor")

            enter(pe, "tensor", 1)
            with pe.Fori(0, B // 2) as i:
                for s in range(2):
                    pe.wait_ge(p_xhat, 2 * i + s + 1)
                    for k in range(KD):
                        for t in range(NT):
                            last = nc.tensor.transpose(bank[s][:, k * S + t * P:k * S + t * P + P],
                                                       xhat[:, s, t * D + k * P:t * D + k * P + P], ident[:, :])
                    last.then_inc(p_ht, 1)
                for s in range(2):
                    pe.wait_ge(p_split, 2 * i + s + 1)
                    for t in range(NT):
                        for k in range(KD):
                            c0 = k * S + t * P
                            last = three(bank[2 + 2 * s + t][:, 0:WA], (h_hi[:, s, c0:c0 + P], h_lo[:, s, c0:c0 + P]),
                                         (wa_hi[:, k * WA:k * WA + WA], wa_lo[:, k * WA:k * WA + WA]), k == 0, k == KD - 1)
                    last.then_inc(p_proj, 1)
                for s in range(2):
                    pe.wait_ge(p_norm, 2 * i + s + 1)
                    if s == 1:
                        pe.wait_ge(p_kept, 2 * i + s)
                    for t in range(NT):
                        c0 = t * P
                        nc.tensor.transpose(bank[6][:, c0:c0 + P], qn[:, s, t * QL:t * QL + P], ident[:, :])
                        nc.tensor.transpose(bank[6][0:KW1, S + c0:S + c0 + P], qn[:, s, t * QL + P:t * QL + QL], ident[:, :])
                        nc.tensor.transpose(bank[7][:, c0:c0 + P], keys[:, s, t * 192:t * 192 + P], ident[:, :])
                        last = nc.tensor.transpose(bank[7][:, S + c0:S + c0 + P], keys[:, s, t * 192 + 64:t * 192 + 192], ident[:, :])
                    last.then_inc(p_t, 1)
            leave(pe, "tensor")

            enter(pe, "tensor", 2)

            def queries(b, p, first=False):
                if p == 0:
                    pe.wait_ge(q_split, b + 1)
                if not first:
                    pe.wait_ge(a_latq, NP * b + p)
                for tile in range(2):
                    w = slice(p * 256 + tile * P, p * 256 + tile * P + P)
                    dst = bank[0][:, tile * S:tile * S + S]
                    three(dst, (wq_hi0[:, w], wq_lo0[:, w]), (q_hi0[:, :], q_lo0[:, :]), True, False)
                    last = three(dst, (wq_hi1[:, w], wq_lo1[:, w]), (q_hi1[:, :], q_lo1[:, :]), False, True)
                last.then_inc(a_qgen, 1)

            def scores(b, p, first=False):
                pe.wait_ge(a_query, NP * b + p + 1)
                if not first:
                    pe.wait_ge(a_masked, 2 * (NP * b + p))
                for j, key in enumerate((key_a, key_b)):
                    q = query[:, p % 2, j, :]
                    mm(bank[1 + j][:, 0:P], q[:, 0:P], key[:, bass.ds(b * S, P)], start=True, stop=True)
                    mm(bank[1 + j][:, P:SCORE], q[:, P:S], key[:, bass.ds(b * S, S)], start=True, stop=True).then_inc(a_score, 1)

            def turn_probs(b, p, first=False):
                u = NP * b + p
                pe.wait_ge(a_exp, 2 * (u + 1))
                if not first:
                    pe.wait_ge(a_pt_a, u)
                    pe.wait_ge(a_pt_b, u)
                for j in range(2):
                    for n in range(3):
                        last = nc.tensor.transpose(bank[3 + j][:, n * P:n * P + P], probs[:, p % 2, j, n * P:n * P + P], ident[:, :])
                    last.then_inc(a_ptr, 1)

            def weigh(b, p, first=False):
                u = NP * b + p
                if not first:
                    pe.wait_ge(a_onat, u)
                for j in range(2):
                    pe.wait_ge((a_pt_a, a_pt_b)[j], u + 1)
                    for t in range(NT):
                        dst = bank[5][:, (j * NT + t) * KL:(j * NT + t) * KL + KL]
                        for k in range(t + 1):
                            src = probs_t[:, j, (t + k) * P:(t + k) * P + P]
                            last = mm(dst, src, lat[:, bass.ds((b * NT + k) * KL, KL)], start=(k == 0), stop=(k == t))
                last.then_inc(a_pv, 1)

            def turn_o(b, p, first=False):
                u = NP * b + p
                pe.wait_ge(a_onat, u + 1)
                if not first:
                    pe.wait_ge(a_olo, u)
                for t in range(NT):
                    last = nc.tensor.transpose(bank[6][:, t * P:t * P + P], o_nat[:, p % 2, t * P:t * P + P], ident[:, :])
                last.then_inc(a_otr, 1)

            def project(b, p, first=False):
                u = NP * b + p
                pe.wait_ge(a_olo, u + 1)
                if p == 0 and not first:
                    pe.wait_ge(a_gated, b)
                for t in range(NT):
                    dst = bank[7][:, t * D:t * D + D]
                    w = slice(p * D, p * D + D)
                    last = three(dst, (o_hi[:, t * P:t * P + P], o_lo[:, t * P:t * P + P]), (wout_hi[:, w], wout_lo[:, w]),
                                 p == 0 and t == 0, p == NP - 1, skip_group_check=True)
                last.then_inc(a_out, 1)

            def before(b, p, lag):
                return (b, p - lag) if p >= lag else (b - 1, p - lag + NP)

            def attention(b, first=False, last=False):
                for p in range(NP):
                    scores(b, p, first and p == 0)
                    if p + 2 < NP:
                        queries(b, p + 2)
                    elif not last:
                        queries(b + 1, p + 2 - NP)
                    if not first or p >= 1:
                        turn_probs(*before(b, p, 1), first and p == 1)
                    if not first or p >= 2:
                        turn_o(*before(b, p, 2), first and p == 2)
                    if not first or p >= 1:
                        weigh(*before(b, p, 1), first and p == 1)
                    if not first or p >= 2:
                        project(*before(b, p, 2), first and p == 2)

            queries(0, 0, True)
            queries(0, 1)
            attention(0, first=True)
            with pe.Fori(1, B - 1) as b:
                attention(b)
            attention(B - 1, last=True)
            turn_probs(B - 1, NP - 1)
            turn_o(B - 1, NP - 2)
            weigh(B - 1, NP - 1)
            project(B - 1, NP - 2)
            turn_o(B - 1, NP - 1)
            project(B - 1, NP - 1)
            leave(pe, "tensor")

            enter(pe, "tensor", 3)

            def turn_h(b, slot):
                pe.wait_ge(f_h2, b + 1)
                for k in range(KD):
                    for t in range(NT):
                        last = nc.tensor.transpose(bank[6][:, k * S + t * P:k * S + t * P + P],
                                                   h2[:, slot, t * D + k * P:t * D + k * P + P], ident[:, :])
                last.then_inc(f_ht, 1)

            def up(b, first=False):
                pe.wait_ge(f_hsplit, b + 1)
                for g in range(NF // 2):
                    if not first:
                        pe.wait_ge(f_act, (b - 1) * (NF // 2) + g + 1)
                    for j in range(2):
                        f = 2 * g + j
                        for k in range(KD):
                            w = slice(k * DFF + f * P, k * DFF + f * P + P)
                            last = three(bank[g][:, j * S:j * S + S], (w1_hi[:, w], w1_lo[:, w]),
                                         (h2_hi[:, k * S:k * S + S], h2_lo[:, k * S:k * S + S]), k == 0, k == KD - 1)
                    last.then_inc(f_up, 1)

            def down(b, first=False):
                if not first:
                    pe.wait_ge(f_mixed, b)
                pe.wait_ge(f_lo, (NF // 2) * (b + 1))
                for t in range(NT):
                    for f in range(NF):
                        a = slice(f * S + t * P, f * S + t * P + P)
                        last = three(bank[4 + t][:, 0:D], (act_hi[:, a], act_lo[:, a]),
                                     (w2_hi[:, f * D:f * D + D], w2_lo[:, f * D:f * D + D]), f == 0, f == NF - 1)
                last.then_inc(f_down, 1)

            pe.wait_ge(f_w, 1)
            turn_h(0, 0)
            up(0, True)
            turn_h(1, 1)
            down(0, True)
            with pe.Fori(0, (B - 2) // 2) as i:
                for slot in range(2):
                    up(2 * i + 1 + slot)
                    turn_h(2 * i + 2 + slot, slot)
                    down(2 * i + 1 + slot)
            up(B - 1)
            down(B - 1)

        @block.vector
        def _(dve):
            v = nc.vector
            step = [0]
            carried = [0]

            def link(ins):
                step[0] += 1
                ins.then_inc(vec_step, 1)
                dve.wait_ge(vec_step, step[0])

            def carry_wait():
                carried[0] = (carried[0] + 1) % 64
                v.memset(spare[:, carried[0]:carried[0] + 1], 0.0)

            dve.wait_ge(exp_c, 1)
            link(v.tensor_scalar_add(c_nat[:, 2, :], c_nat[:, 1, :], 1.0))
            link(v.reciprocal(c_nat[:, 3, :], c_nat[:, 2, :]))
            v.tensor_tensor(silu[:, :], c_nat[:, 0, :], c_nat[:, 3, :], ALU.mult).then_inc(silu_done, 1)
            for k in range(KD):
                dve.wait_ge(s_wa_hi, k + 1)
                w = slice(k * WA, k * WA + WA)
                v.tensor_tensor(wa_lo[:, w], bank[k][:, 0:WA], wa_hi[:, w].bitcast(F32), ALU.subtract)
            dve.wait_ge(s_silu_t, 1)
            v.tensor_copy(silu_t[:, :], bank[2][:, 0:KD * B]).then_inc(s_silu_sb, 1)
            dve.wait_ge(s_mod, 1)
            for n in range(3):
                last = v.tensor_copy(mod_nat[:, n * 512:n * 512 + 512], bank[3 + n][0:B, :])
            last.then_inc(s_mod_sb, 1)
            dve.wait_ge(s_mod_sb, 1)
            for n, part in enumerate((2, 5)):
                g = mod_nat[:, part * D:part * D + D]
                v.tensor_scalar(gate_sign[:, 0, n * D:n * D + D], g, 0.0, 2.0, ALU.is_ge, ALU.mult)
                last = v.scalar_tensor_tensor(out=gate_sign[:, 1, n * D:n * D + D], in0=g, scalar=-1.0, in1=g,
                                              op0=ALU.mult, op1=ALU.max)
            link(last)
            link(v.tensor_scalar_max(gate_abs[:, :], gate_sign[:, 1, :], 0.25))
            for n, part in enumerate((0, 3)):
                v.scalar_tensor_tensor(out=mod_out[:, part * D:part * D + D], in0=gate_sign[:, 0, n * D:n * D + D],
                                       scalar=-1.0, in1=gate_abs[:, n * D:n * D + D], op0=ALU.add, op1=ALU.mult)
            v.tensor_scalar_add(mod_out[:, D:2 * D], mod_nat[:, 4 * D:5 * D], 1.0)
            v.tensor_copy(mod_out[:, 2 * D:3 * D], mod_nat[:, 3 * D:4 * D]).then_inc(mod_out_done, 1)
            dve.wait_ge(s_modt, 1)
            v.tensor_copy(mod_t[:, 0:2 * B], bank[6][:, 0:2 * B])
            v.tensor_scalar_add(mod_t[:, 2 * B:4 * B], bank[6][:, 2 * B:4 * B], 1.0)
            dve.wait_ge(ld_small, 16 * 8)
            dve.wait_ge(ld_kwr, 32)
            dve.wait_ge(kwr_done, 1)
            for n in range(NP):
                dve.wait_ge(s_wout, n + 1)
                w = slice(n * D, n * D + D)
                link(v.tensor_scalar(wout_hi[:, w], bank[2 + n % 2][:, 0:D], kw_col[:, 0:1], None, ALU.mult))
                v.scalar_tensor_tensor(out=wout_lo[:, w], in0=bank[2 + n % 2][:, 0:D], scalar=kw_col[:, 0:1],
                                       in1=wout_hi[:, w].bitcast(F32), op0=ALU.mult, op1=ALU.subtract).then_inc(s_wout_free, 1)
                dve.wait_ge(s_wq, n + 1)
                if n >= 2:
                    dve.wait_ge(s_wq_lo, n - 1)
                q = bank[4 + n % 2]
                v.scalar_tensor_tensor(out=wq_tmp0[:, n % 2, :], in0=q[:, 0:256], scalar=qw[:, 0:1], in1=kw_row[:, :],
                                       op0=ALU.mult, op1=ALU.mult)
                v.scalar_tensor_tensor(out=wq_tmp1[:, n % 2, :], in0=q[0:KW1, 256:512], scalar=qw[0:KW1, 1:2],
                                       in1=kw_row[0:KW1, :], op0=ALU.mult, op1=ALU.mult).then_inc(s_wq_tmp, 1)
            leave(dve, "vector")

            enter(dve, "vector", 1)
            dve.wait_ge(ld_x, 64)
            base = step[0]
            with dve.Fori(0, B) as b:
                for t in range(NT):
                    last = v.bn_stats(bn_raw[:, t, :], x_sb[:, bass.ds((b * NT + t) * D, D)])
                last.then_inc(vec_step, 1)
                dve.wait_ge(vec_step, 2 * b + base + 1)
                for t in range(NT):
                    if t == 0:
                        carry_wait()
                    last = v.bn_aggr(bn_tile[:, t, :], bn_raw[:, t, :])
                last.then_inc(vec_step, 1)
                dve.wait_ge(vec_step, 2 * b + base + 2)
                v.tensor_copy(tok_stat[:, bass.ds(b * NT, NT), :], bn_tile[:, :, :]).then_inc(bn_kept, 1)
                dve.wait_ge(bn_kept, b + 1)
            step[0] += 2 * B
            v.tensor_scalar_add(tok_shift[:, :], tok_stat[:, :, 1], LN_EPS).then_inc(var_done, 1)
            dve.wait_ge(rstd_done, 1)
            link(v.scalar_tensor_tensor(out=tok_shift[:, :], in0=tok_stat[:, :, 0], scalar=-1.0, in1=tok_rstd[:, :],
                                        op0=ALU.mult, op1=ALU.mult))

            base = step[0]
            with dve.Fori(0, B // 2) as i:
                for s in range(2):
                    b = 2 * i + s
                    for t in range(NT):
                        g = b * NT + t
                        last = v.tensor_scalar(xhat[:, s, t * D:t * D + D], x_sb[:, bass.ds(g * D, D)],
                                               tok_rstd[:, bass.ds(g, 1)], tok_shift[:, bass.ds(g, 1)], ALU.mult, ALU.add)
                    last.then_inc(p_xhat, 1)
                    v.tensor_copy(mod_col[:, s, :], mod_t[:, :].rearrange("p (n b) -> p n b", b=B)[:, :, bass.ds(b, 1)]
                                  .rearrange("p n a -> p (n a)")).then_inc(p_mod, 1)
                for s in range(2):
                    dve.wait_ge(p_hsb, 2 * i + s + 1)
                    v.tensor_copy(h_hi[:, s, :], h_t[:, s, :]).then_inc(vec_step, 1)
                    dve.wait_ge(vec_step, 4 * i + base + s + 1)
                    v.tensor_tensor(h_lo[:, s, :], h_t[:, s, :], h_hi[:, s, :].bitcast(F32), ALU.subtract).then_inc(p_split, 1)
                for s in range(2):
                    dve.wait_ge(p_rms, 2 * i + s + 1)
                    for t in range(NT):
                        src = bank[2 + 2 * s + t]
                        rq, rk = rms_r[:, s, 2 * t:2 * t + 1], rms_r[:, s, 2 * t + 1:2 * t + 2]
                        k0 = t * 192
                        v.tensor_scalar(qn[:, s, t * QL:t * QL + QL], src[:, 0:QL], rq, None, ALU.mult)
                        v.tensor_scalar(keys[:, s, k0:k0 + KL], src[:, QL:QL + KL], rk, None, ALU.mult)
                        v.tensor_scalar(keys[:, s, k0 + P:k0 + 192], src[:, QL:QL + KL], rk, None, ALU.mult)
                        v.tensor_scalar(lat[:, bass.ds(((2 * i + s) * NT + t) * KL, KL)], src[:, QL:QL + KL], rk, None, ALU.mult)
                        r0, r1, r2 = QL + KL, QL + KL + DR // 2, WA
                        v.tensor_tensor(kr_cos[:, s, t * DR:t * DR + DR], src[:, r0:r2], rope_tok[:, t, 0:DR], ALU.mult)
                        v.tensor_tensor(kr_sin[:, s, t * DR:t * DR + DR // 2], src[:, r1:r2], rope_tok[:, t, DR:DR + DR // 2], ALU.mult)
                        last = v.tensor_tensor(kr_sin[:, s, t * DR + DR // 2:t * DR + DR], src[:, r0:r1],
                                               rope_tok[:, t, DR + DR // 2:2 * DR], ALU.mult)
                    last.then_inc(vec_step, 1)
                    dve.wait_ge(vec_step, 4 * i + base + 3 + s)
                    for t in range(NT):
                        def runs(a):
                            return a.rearrange("p (h g j) -> p h g j", h=2, g=2)
                        dst = keys[:, s, t * 192 + KL:t * 192 + P].rearrange("p (g h j) -> p h g j", g=2, h=2)
                        last = v.tensor_tensor(dst, runs(kr_cos[:, s, t * DR:t * DR + DR]), runs(kr_sin[:, s, t * DR:t * DR + DR]), ALU.add)
                    last.then_inc(p_norm, 1)
            step[0] += 4 * (B // 2)
            leave(dve, "vector")

            enter(dve, "vector", 2)

            def split_q(b):
                dve.wait_ge(q_hi_done, b + 1)
                v.tensor_tensor(q_lo0[:, :], qn_t0[:, bass.ds(b * S, S)], q_hi0[:, :].bitcast(F32), ALU.subtract)
                v.tensor_tensor(q_lo1[:, :], qn_t1[:, bass.ds(b * S, S)], q_hi1[:, :].bitcast(F32), ALU.subtract).then_inc(q_split, 1)

            def masked(b, p):
                u = NP * b + p
                if not isinstance(b, int) or u >= 2:
                    dve.wait_ge(a_exp, 2 * (u - 1))
                for j in range(2):
                    dve.wait_ge(a_score, 2 * u + j + 1)
                    carry_wait()
                    s, o, m = bank[1 + j], scored[:, p % 2, j, :], row_min[:, p % 2, :]
                    v.tensor_tensor_reduce(out=o[:, 0:P], in0=s[:, 0:P], in1=mask_pad[:, P:2 * P], scale=-SCALE, scalar=3.0e38,
                                           op0=ALU.add, op1=ALU.min, accum_out=m[:, 2 * j:2 * j + 1])
                    v.tensor_tensor_reduce(out=o[:, P:SCORE], in0=s[:, P:SCORE], in1=mask_pad[:, :], scale=-SCALE, scalar=3.0e38,
                                           op0=ALU.add, op1=ALU.min, accum_out=m[:, 2 * j + 1:2 * j + 2]).then_inc(a_masked, 1)

            def rotate(b, p):
                u = NP * b + p
                dve.wait_ge(a_qgen, u + 1)
                if not isinstance(b, int) or u >= 2:
                    dve.wait_ge(a_query, u - 1)
                v.tensor_tensor(pe_cos[:, p % 2, :], bank[0][:, S:2 * S], rope[:, 0:S], ALU.mult)
                v.stream_shuffle(pe_rot[:, p % 2, :], bank[0][:, S:2 * S], SWAP16).then_inc(a_rot, 1)

            def keep_pt(b, p):
                u = NP * b + p
                dve.wait_ge(a_ptr, 2 * u + 1)
                if not isinstance(b, int) or u >= 1:
                    dve.wait_ge(a_pv, u)
                v.tensor_copy(probs_t[:, 0, :], bank[3][:, 0:SCORE]).then_inc(a_pt_a, 1)

            def invert(b, p):
                dve.wait_ge(a_exp, 2 * (NP * b + p + 1))
                v.reciprocal(row_inv[:, p % 2, :], row_sum[:, p % 2, :]).then_inc(a_inv, 1)

            def norm_o(b, p):
                u = NP * b + p
                dve.wait_ge(a_pv, u + 1)
                dve.wait_ge(a_inv, u + 1)
                if not isinstance(b, int) or u >= 2:
                    dve.wait_ge(a_otr, u - 1)
                src = bank[5][:, 0:256].rearrange("p (h t c) -> p h t c", h=2, t=NT)
                dst = o_nat[:, p % 2, :].rearrange("p (t h c) -> p h t c", h=2, t=NT)
                inv = row_inv[:, p % 2, :].rearrange("p (h t a) -> p h t a", h=2, a=1).broadcast_to([P, 2, NT, KL])
                v.tensor_tensor(dst, src, inv, ALU.mult).then_inc(a_onat, 1)

            def split_o(b, p):
                u = NP * b + p
                dve.wait_ge(a_ohi, u + 1)
                v.tensor_tensor(o_lo[:, :], bank[6][:, 0:256], o_hi[:, :].bitcast(F32), ALU.subtract).then_inc(a_olo, 1)

            def gate(b):
                dve.wait_ge(a_out, NP * (b + 1))
                dve.wait_ge(gate_loaded, 16 * (b + 1))
                if not isinstance(b, int) or b >= 1:
                    dve.wait_ge(a_added, b)
                for t in range(NT):
                    last = v.tensor_tensor(gated[:, t * D:t * D + D], bank[7][:, t * D:t * D + D], gate_a[:, :], ALU.mult)
                last.then_inc(a_gated, 1)

            def before(b, p, lag):
                return (b, p - lag) if p >= lag else (b - 1, p - lag + NP)

            def attention(b, first=False, last=False):
                for p in range(NP):
                    masked(b, p)
                    if not first or p >= 1:
                        invert(*before(b, p, 1))
                    if p == NP - 2 and not last:
                        split_q(b + 1)
                    if p + 2 < NP:
                        rotate(b, p + 2)
                    elif not last:
                        rotate(b + 1, p + 2 - NP)
                    if not first or p >= 1:
                        keep_pt(*before(b, p, 1))
                    if not first or p >= 2:
                        split_o(*before(b, p, 2))
                    if not first or p >= 1:
                        norm_o(*before(b, p, 1))
                    if p == 1 and not first:
                        gate(b - 1)

            split_q(0)
            rotate(0, 0)
            rotate(0, 1)
            attention(0, first=True)
            with dve.Fori(1, B - 1) as b:
                attention(b)
            attention(B - 1, last=True)
            invert(B - 1, NP - 1)
            keep_pt(B - 1, NP - 1)
            split_o(B - 1, NP - 2)
            norm_o(B - 1, NP - 1)
            split_o(B - 1, NP - 1)
            gate(B - 1)
            leave(dve, "vector")

            enter(dve, "vector", 3)
            dve.wait_ge(ld_ffn, 16 * 6)
            dve.wait_ge(f_hi_w, 1)
            v.tensor_tensor(w1_lo[:, :], w1_nat[:, :], w1_hi[:, :].bitcast(F32), ALU.subtract)
            v.tensor_tensor(w2_lo[:, :], w2_nat[:, :], w2_hi[:, :].bitcast(F32), ALU.subtract).then_inc(f_w, 1)
            v.tensor_scalar(rb_col[:, 1:2], rb_col[:, 0:1], 0.5, None, ALU.mult)
            base = step[0]

            def chain(b, n, ins):
                ins.then_inc(vec_step, 1)
                dve.wait_ge(vec_step, 5 * b + base + n)

            def prepare(b, slot):
                dve.wait_ge(ld_modb, 16 * (b + 1))
                for t in range(NT):
                    last = v.bn_stats(f_bn[:, t, :], x_sb[:, bass.ds((b * NT + t) * D, D)])
                chain(b, 1, last)
                carry_wait()
                for t in range(NT):
                    last = v.bn_aggr(f_stat[:, t, :], f_bn[:, t, :])
                chain(b, 2, last)
                v.tensor_scalar_add(f_var[:, :], f_stat[:, :, 1], LN_EPS).then_inc(f_var_done, 1)
                dve.wait_ge(f_rstd_done, b + 1)
                chain(b, 3, v.scalar_tensor_tensor(out=f_shift[:, :], in0=f_stat[:, :, 0], scalar=-1.0, in1=f_rstd[:, :],
                                                   op0=ALU.mult, op1=ALU.mult))
                for t in range(NT):
                    last = v.tensor_scalar(h2_n[:, t * D:t * D + D], x_sb[:, bass.ds((b * NT + t) * D, D)],
                                           f_rstd[:, t:t + 1], f_shift[:, t:t + 1], ALU.mult, ALU.add)
                chain(b, 4, last)
                for t in range(NT):
                    last = v.tensor_tensor(h2_m[:, t * D:t * D + D], h2_n[:, t * D:t * D + D], mod_b[:, slot, 0:D], ALU.mult)
                chain(b, 5, last)
                for t in range(NT):
                    last = v.tensor_tensor(h2[:, slot, t * D:t * D + D], h2_m[:, t * D:t * D + D],
                                           mod_b[:, slot, D:2 * D], ALU.add)
                last.then_inc(f_h2, 1)
                dve.wait_ge(f_h2, b + 1)
                carry_wait()
                for t in range(NT):
                    last = v.tensor_tensor_reduce(out=rout_junk[:, t, :], in0=h2[:, slot, t * D:t * D + D], in1=rw_row[:, :],
                                                  scale=1.0, scalar=0.0, op0=ALU.mult, op1=ALU.add,
                                                  accum_out=rout[:, slot, t:t + 1])
                last.then_inc(f_rout, 1)

            def split_h(b):
                dve.wait_ge(f_hhi, b + 1)
                v.tensor_tensor(h2_lo[:, :], bank[6][:, :], h2_hi[:, :].bitcast(F32), ALU.subtract).then_inc(f_hsplit, 1)

            def split_act(b):
                for g in range(NF // 2):
                    dve.wait_ge(f_act, (NF // 2) * b + g + 1)
                    a = slice(g * 512, g * 512 + 512)
                    v.tensor_tensor(act_lo[:, a], act_full[:, a], act_hi[:, a].bitcast(F32), ALU.subtract).then_inc(f_lo, 1)

            def mix(b, slot):
                dve.wait_ge(f_down, b + 1)
                if not isinstance(b, int) or b >= 1:
                    dve.wait_ge(f_gated, b)
                for t in range(NT):
                    v.tensor_tensor(f_sum[:, t * D:t * D + D], bank[4 + t][:, 0:D], b2_row[:, :], ALU.add)
                dve.wait_ge(f_tanh, b + 1)
                last = v.tensor_scalar(rout_w[:, slot, :], rout_t[:, slot, :], 1.0, 0.5, ALU.add, ALU.mult)
                last.then_inc(mix_step, 1)
                dve.wait_ge(mix_step, b + 1)
                for t in range(NT):
                    last = v.scalar_tensor_tensor(out=f_mix[:, t * D:t * D + D], in0=f_sum[:, t * D:t * D + D],
                                                  scalar=rout_w[:, slot, t:t + 1], in1=h2[:, slot, t * D:t * D + D],
                                                  op0=ALU.mult, op1=ALU.add)
                last.then_inc(f_mixed, 1)

            def feed(b, slot, last=False):
                if not last:
                    prepare(b + 1, 1 - slot)
                split_act(b)
                if not last:
                    split_h(b + 1)
                mix(b, slot)

            prepare(0, 0)
            split_h(0)
            feed(0, 0)
            with dve.Fori(0, (B - 2) // 2) as i:
                feed(2 * i + 1, 1)
                feed(2 * i + 2, 0)
            feed(B - 1, 1, last=True)

        @block.scalar
        def _(act):
            a = nc.scalar.activation
            act.dma_start(c_nat[:, 0, :], c).then_inc(ld_c, 16)
            act.dma_start(mask_pad[:, :], mask_in).then_inc(ld_small, 16)
            act.dma_start(rope[:, :], rope_rows).then_inc(ld_small, 16)
            act.dma_start(rope_tok[:, :, :], rope_tokens.rearrange("(t p) n -> p t n", p=P)).then_inc(ld_small, 16)
            act.dma_start(qw[:, 0:1], q_norm_w[0:P].rearrange("(p a) -> p a", a=1)).then_inc(ld_small, 16)
            act.dma_start(qw[0:KW1, 1:2], q_norm_w[P:QL].rearrange("(p a) -> p a", a=1)).then_inc(ld_small, 16)
            for j in range(2):
                act.dma_start(kw_col[64 * j:64 * j + 64, :], kv_norm_w.rearrange("(p a) -> p a", a=1)).then_inc(ld_small, 16)
            act.wait_ge(ld_c, 16)
            a(c_nat[:, 1, :], c_nat[:, 0, :], ACT.Exp, scale=-1.0).then_inc(exp_c, 1)
            for k in range(KD):
                act.wait_ge(s_wa_t, k + 1)
                a(wa_hi[:, k * WA:k * WA + WA], bank[k][:, 0:WA], ACT.Copy).then_inc(s_wa_hi, 1)
            for n in range(NP):
                act.wait_ge(s_wo_t, n + 1)
                a(wo_t[:, 2 * n:2 * n + 2, :].rearrange("p h o -> p (h o)"), bank[n % 2][:, :], ACT.Copy).then_inc(s_wo_sb, 1)
            for n in range(NP):
                act.wait_ge(s_wq_tmp, n + 1)
                w = slice(n * 256, n * 256 + 256)
                a(wq_hi0[:, w], wq_tmp0[:, n % 2, :], ACT.Copy)
                a(wq_hi1[:, w], wq_tmp1[:, n % 2, :], ACT.Copy).then_inc(s_wq_hi, 1)
            leave(act, "scalar")

            enter(act, "scalar", 1)
            with act.Fori(0, B // 2) as i:
                for s in range(2):
                    act.wait_ge(p_ht, 2 * i + s + 1)
                    act.wait_ge(p_mod, 2 * i + s + 1)
                    for k in range(KD):
                        last = a(h_t[:, s, k * S:k * S + S], bank[s][:, k * S:k * S + S], ACT.Identity,
                                 bias=mod_col[:, s, k:k + 1], scale=mod_col[:, s, 2 + k:3 + k])
                    last.then_inc(p_hsb, 1)
                for s in range(2):
                    act.wait_ge(p_proj, 2 * i + s + 1)
                    for t in range(NT):
                        src = bank[2 + 2 * s + t]
                        a(sq_junk[:, s, t, 0:QL], src[:, 0:QL], ACT.Square, accum_out=sumsq[:, s, 2 * t:2 * t + 1])
                        last = a(sq_junk[:, s, t, QL:QL + KL], src[:, QL:QL + KL], ACT.Square, accum_out=sumsq[:, s, 2 * t + 1:2 * t + 2])
                    last.then_inc(p_sq, 1)
                for s in range(2):
                    act.wait_ge(p_t, 2 * i + s + 1)
                    cols = bass.ds((2 * i + s) * S, S)
                    a(qn_t0[:, cols], bank[6][:, 0:S], ACT.Copy)
                    a(qn_t1[:, cols], bank[6][0:KW1, S:2 * S], ACT.Copy)
                    a(key_a[:, cols], bank[7][:, 0:S], ACT.Copy)
                    a(key_b[:, cols], bank[7][:, S:2 * S], ACT.Copy).then_inc(p_kept, 1)
            leave(act, "scalar")

            enter(act, "scalar", 2)

            def round_q(b):
                if not isinstance(b, int) or b >= 1:
                    act.wait_ge(a_qgen, NP * b)
                a(q_hi0[:, :], qn_t0[:, bass.ds(b * S, S)], ACT.Copy)
                a(q_hi1[:, :], qn_t1[:, bass.ds(b * S, S)], ACT.Copy).then_inc(q_hi_done, 1)

            def latent_rows(b, p):
                u = NP * b + p
                act.wait_ge(a_rot, u + 1)
                if not isinstance(b, int) or u >= 2:
                    act.wait_ge(a_score, 2 * (u - 1))
                a(query[0:64, p % 2, 0, :], bank[0][0:64, 0:S], ACT.Copy)
                a(query[64:128, p % 2, 1, :], bank[0][64:128, 0:S], ACT.Copy).then_inc(a_latq, 1)

            def exps(b, p):
                u = NP * b + p
                if not isinstance(b, int) or u >= 2:
                    act.wait_ge(a_ptr, 2 * (u - 1))
                    act.wait_ge(a_inv, u - 1)
                for j in range(2):
                    act.wait_ge(a_masked, 2 * u + j + 1)
                    for t, c in enumerate((slice(0, P), slice(P, SCORE))):
                        n = 2 * j + t
                        last = a(probs[:, p % 2, j, c], scored[:, p % 2, j, c], ACT.Exp, scale=-1.0,
                                 bias=row_min[:, p % 2, n:n + 1], accum_out=row_sum[:, p % 2, n:n + 1])
                    last.then_inc(a_exp, 1)

            def keep_pt(b, p):
                u = NP * b + p
                act.wait_ge(a_ptr, 2 * u + 2)
                if not isinstance(b, int) or u >= 1:
                    act.wait_ge(a_pv, u)
                a(probs_t[:, 1, :], bank[4][:, 0:SCORE], ACT.Copy).then_inc(a_pt_b, 1)

            def round_o(b, p):
                u = NP * b + p
                act.wait_ge(a_otr, u + 1)
                if not isinstance(b, int) or u >= 1:
                    act.wait_ge(a_out, u)
                a(o_hi[:, :], bank[6][:, 0:256], ACT.Copy).then_inc(a_ohi, 1)

            def before(b, p, lag):
                return (b, p - lag) if p >= lag else (b - 1, p - lag + NP)

            def attention(b, first=False, last=False):
                for p in range(NP):
                    if p == NP - 2 and not last:
                        round_q(b + 1)
                    exps(b, p)
                    if p + 2 < NP:
                        latent_rows(b, p + 2)
                    elif not last:
                        latent_rows(b + 1, p + 2 - NP)
                    if not first or p >= 1:
                        keep_pt(*before(b, p, 1))
                    if not first or p >= 2:
                        round_o(*before(b, p, 2))

            round_q(0)
            latent_rows(0, 0)
            latent_rows(0, 1)
            attention(0, first=True)
            with act.Fori(1, B - 1) as b:
                attention(b)
            attention(B - 1, last=True)
            keep_pt(B - 1, NP - 1)
            round_o(B - 1, NP - 2)
            round_o(B - 1, NP - 1)
            leave(act, "scalar")

            enter(act, "scalar", 3)
            act.wait_ge(ld_ffn, 16 * 6)
            a(w1_hi[:, :], w1_nat[:, :], ACT.Copy)
            a(w2_hi[:, :], w2_nat[:, :], ACT.Copy).then_inc(f_hi_w, 1)

            def round_h(b, first=False):
                act.wait_ge(f_ht, b + 1)
                if not first:
                    act.wait_ge(f_up, (NF // 2) * b)
                a(h2_hi[:, :], bank[6][:, :], ACT.Copy).then_inc(f_hhi, 1)

            def gelus(b, first=False):
                if not first:
                    act.wait_ge(f_down, b)
                for g in range(NF // 2):
                    act.wait_ge(f_up, (NF // 2) * b + g + 1)
                    for j in range(2):
                        f = 2 * g + j
                        for dst in (act_hi, act_full):
                            last = a(dst[:, f * S:f * S + S], bank[g][:, j * S:j * S + S], ACT.Gelu_apprx_tanh, bias=b1_col[:, f:f + 1])
                    last.then_inc(f_act, 1)

            def router(b, slot):
                act.wait_ge(f_rout, b + 1)
                if not isinstance(b, int) or b >= 2:
                    act.wait_ge(f_mixed, b - 1)
                a(rout_t[:, slot, :], rout[:, slot, :], ACT.Tanh, bias=rb_col[:, 1:2], scale=0.5).then_inc(f_tanh, 1)

            router(0, 0)
            round_h(0, True)
            gelus(0, True)
            router(1, 1)
            round_h(1)
            with act.Fori(0, (B - 2) // 2) as i:
                for slot in range(2):
                    gelus(2 * i + 1 + slot)
                    router(2 * i + 2 + slot, slot)
                    round_h(2 * i + 2 + slot)
            gelus(B - 1)

        @block.gpsimd
        def _(pool):
            g = nc.gpsimd
            step = [0]

            def link(ins):
                step[0] += 1
                ins.then_inc(pool_step, 1)
                pool.wait_ge(pool_step, step[0])

            for j in range(2):
                pool.dma_start(kw_row[:, 64 * j:64 * j + 64], kv_norm_w.rearrange("(a n) -> a n", a=1).broadcast_to([P, KL])).then_inc(ld_kwr, 16)
            g.memset(half_neg[:, :], -0.5)
            g.memset(rms_eps[:, :], RMS_EPS)
            for t in range(NT):
                g.memset(inv_n[:, 2 * t:2 * t + 1], 1.0 / QL)
                g.memset(inv_n[:, 2 * t + 1:2 * t + 2], 1.0 / KL)
            link(g.memset(kw_row[:, P:2 * P], 1.0))
            pool.sem_inc(kwr_done, 1)
            for n in range(NP):
                pool.wait_ge(s_wq_hi, n + 1)
                w = slice(n * 256, n * 256 + 256)
                link(g.tensor_tensor(wq_lo0[:, w], wq_tmp0[:, n % 2, :], wq_hi0[:, w].bitcast(F32), ALU.subtract))
                g.tensor_tensor(wq_lo1[:, w], wq_tmp1[:, n % 2, :], wq_hi1[:, w].bitcast(F32), ALU.subtract).then_inc(s_wq_lo, 1)
            pool.wait_ge(s_wq_lo, NP)
            leave(pool, "gpsimd")

            enter(pool, "gpsimd", 1)
            pool.wait_ge(var_done, 1)
            g.tensor_tensor(tok_rstd[:, :], tok_shift[:, :], half_neg[:, :], ALU.pow).then_inc(rstd_done, 1)
            base = step[0]
            with pool.Fori(0, B // 2) as i:
                for s in range(2):
                    pool.wait_ge(p_sq, 2 * i + s + 1)
                    g.tensor_tensor(rms_mid[:, s, :], sumsq[:, s, :], inv_n[:, :], ALU.mult).then_inc(pool_step, 1)
                    pool.wait_ge(pool_step, 4 * i + base + 2 * s + 1)
                    g.tensor_tensor(rms_var[:, s, :], rms_mid[:, s, :], rms_eps[:, :], ALU.add).then_inc(pool_step, 1)
                    pool.wait_ge(pool_step, 4 * i + base + 2 * s + 2)
                    g.tensor_tensor(rms_r[:, s, :], rms_var[:, s, :], half_neg[:, 0:2 * NT], ALU.pow).then_inc(p_rms, 1)
            step[0] += 4 * (B // 2)
            pool.wait_ge(p_rms, B)
            leave(pool, "gpsimd")

            enter(pool, "gpsimd", 2)
            base_u = step[0]

            def finish_rope(b, p):
                u = NP * b + p
                pool.wait_ge(a_rot, u + 1)
                pool.wait_ge(a_latq, u + 1)
                g.tensor_tensor(pe_sin[:, p % 2, :], pe_rot[:, p % 2, :], rope[:, S:2 * S], ALU.mult).then_inc(pool_step, 1)
                pool.wait_ge(pool_step, 2 * u + base_u + 1)
                g.tensor_tensor(query[0:64, p % 2, 1, :], pe_sin[0:64, p % 2, :], pe_cos[0:64, p % 2, :], ALU.add).then_inc(pool_step, 1)
                pool.wait_ge(pool_step, 2 * u + base_u + 2)
                g.tensor_tensor(query[64:128, p % 2, 0, :], pe_sin[64:128, p % 2, :], pe_cos[64:128, p % 2, :], ALU.add).then_inc(a_query, 1)
                pool.wait_ge(a_query, u + 1)

            def add_out(b):
                pool.wait_ge(a_gated, b + 1)
                rows = x_sb[:, bass.ds(b * NT * D, NT * D)]
                g.tensor_tensor(rows, rows, gated[:, :], ALU.add).then_inc(a_added, 1)
                pool.wait_ge(a_added, b + 1)

            def attention(b, first=False, last=False):
                for p in range(NP):
                    if p + 2 < NP:
                        finish_rope(b, p + 2)
                    elif not last:
                        finish_rope(b + 1, p + 2 - NP)
                    if p == 1 and not first:
                        add_out(b - 1)

            finish_rope(0, 0)
            finish_rope(0, 1)
            attention(0, first=True)
            with pool.Fori(1, B - 1) as b:
                attention(b)
            attention(B - 1, last=True)
            add_out(B - 1)
            leave(pool, "gpsimd")

            enter(pool, "gpsimd", 3)

            def rstd(b):
                pool.wait_ge(f_var_done, b + 1)
                g.tensor_tensor(f_rstd[:, :], f_var[:, :], half_neg[:, 0:NT], ALU.pow).then_inc(f_rstd_done, 1)

            def finish(b, slot, before):
                pool.wait_ge(f_mixed, b + 1)
                if not isinstance(before, int) or before:
                    pool.wait_ge(stored[slot], 16 * before)
                for t in range(NT):
                    last = g.tensor_tensor(f_gate[:, t * D:t * D + D], f_mix[:, t * D:t * D + D], mod_b[:, slot, 2 * D:3 * D], ALU.mult)
                last.then_inc(f_gated, 1)
                pool.wait_ge(f_gated, b + 1)
                g.tensor_tensor(f_out[:, slot, :], f_gate[:, :], x_sb[:, bass.ds(b * NT * D, NT * D)], ALU.add).then_inc(f_done, 1)
                pool.wait_ge(f_done, b + 1)

            def feed(i, slot, last=False):
                b = 2 * i + slot
                if not last:
                    rstd(b + 1)
                finish(b, slot, i)

            rstd(0)
            feed(0, 0)
            feed(0, 1)
            with pool.Fori(1, B // 2 - 1) as i:
                feed(i, 0)
                feed(i, 1)
            feed(B // 2 - 1, 0)
            feed(B // 2 - 1, 1, last=True)


INS = ['L0_attn_hidden_states', 'L0_attn_wq_a', 'L0_attn_q_norm_w', 'L0_attn_wq_b', 'L0_attn_wkv_a', 'L0_attn_kv_norm_w',
       'L0_attn_wkv_b', 'L0_attn_wo', 'L0_ffn_router_weight', 'L0_ffn_router_bias', 'L0_ffn_w1', 'L0_ffn_b1', 'L0_ffn_w2',
       'L0_ffn_b2', 'L0_c', 'L0_wmod']


def shape_constants():
    f = np.float32
    inv = (f(1.0) / np.power(f(10000.0), np.arange(0, DR, 2, dtype=f) / f(DR))).astype(f)
    angle = (np.arange(S, dtype=f)[:, None] * inv[None, :]).astype(f)
    cos, sin = np.cos(angle).astype(f), np.sin(angle).astype(f)
    tokens = np.concatenate([cos, cos, -sin, sin], axis=1)
    row = [(half, g * 16 + j) for half, g in RUNS for j in range(16)] * 2
    rows = np.stack([np.concatenate([cos[:, d], sin[:, d] if half else -sin[:, d]]) for half, d in row])
    masks = np.zeros((P, 2 * P), f)
    masks[:, P:] = np.where(np.tril(np.ones((P, P), bool)), f(0), f(MASKED))
    return {"ident": np.eye(P, dtype=f), "mask": masks, "rope_rows": rows.astype(f), "rope_tokens": tokens.astype(f)}


def kernel(**inputs):
    import concourse.bacc as _bacc
    from concourse.bass_utils import run_bass_kernel_spmd as _run

    nc = _bacc.Bacc("TRN2", target_bir_lowering=False, num_devices=1)
    arrays, args = {}, []
    given = {n: np.asarray(inputs[n]) for n in INS}
    given["L0_ffn_b1"] = given["L0_ffn_b1"].reshape(NF, P).T
    given = [(n, np.ascontiguousarray(a)) for n, a in given.items()] + list(shape_constants().items())
    for name, a in given:
        arrays[f"in_{name}"] = a
        args.append(nc.dram_tensor(f"in_{name}", a.shape, mybir.dt.from_np(a.dtype), kind="ExternalInput").ap())
    result = nc.dram_tensor("out_x", (B, S, D), F32, kind="ExternalOutput").ap()
    adaln_layer(nc, *args, result)
    return _run(nc, [arrays], core_ids=[0]).results[0]["out_x"]
```

```python
from contextlib import ExitStack

import numpy as np
import concourse.bass as bass
from concourse import mybir

F32 = mybir.dt.float32
F32R = mybir.dt.float32r
ACT = mybir.ActivationFunctionType
ALU = mybir.AluOpType

P = 128
B, S, D = 16, 256, 256
NH, QL, KL, DR, DN, DV = 16, 192, 64, 64, 128, 128
DFF = 1024
NT = S // P
KD = D // P
NP = NH // 2
WA = QL + KL + DR
KW1 = QL - P
SCORE = 3 * P
NF = DFF // P
SCALE = float(DN + DR) ** -0.5
LN_EPS, RMS_EPS = 1e-5, 1e-6
MASKED = -3.0e38
SWAP16 = [(i + 16) % 32 for i in range(32)]
RUNS = [(half, g) for g in range(2) for half in range(2)]


def adaln_layer(nc, x, wq_a, q_norm_w, wq_b, wkv_a, kv_norm_w, wkv_b, wo, router_w, router_b,
                w1, b1, w2, b2, c, wmod, ident_in, mask_in, rope_rows, rope_tokens, out):
    mod_rows = nc.dram_tensor("mod_rows", (B, 4 * D), F32, kind="Internal").ap()

    with ExitStack() as ctx:
        def sb(name, shape, dt=F32, own=ctx):
            return own.enter_context(nc.sbuf_tensor(name, shape, dt))

        def sem(name):
            return ctx.enter_context(nc.semaphore(name))

        bank = [ctx.enter_context(nc.psum_tensor(f"bank{i}", [P, 512], F32)) for i in range(8)]

        x_sb = sb("x_sb", [P, B * NT * D])
        ident = sb("ident", [P, P])
        mod_t = sb("mod_t", [P, 4 * B])
        bn_raw = sb("bn_raw", [P, B * NT, 6])
        tok_mean = sb("tok_mean", [P, B * NT])
        tok_gap = sb("tok_gap", [P, B * NT])
        tok_m2 = sb("tok_m2", [P, B * NT])
        tok_gap2 = sb("tok_gap2", [P, B * NT])
        tok_var = sb("tok_var", [P, B * NT])
        tok_rstd = sb("tok_rstd", [P, B * NT])
        tok_shift = sb("tok_shift", [P, B * NT])
        half_neg = sb("half_neg", [P, B * NT])
        spare = sb("spare", [P, 64])
        b1_col = sb("b1_col", [P, NF])
        b2_row = sb("b2_row", [P, D])
        rw_row = sb("rw_row", [P, D])
        rb_col = sb("rb_col", [P, 2])
        mod_h = sb("mod_h", [P, 2, 2 * D])
        mod_g = sb("mod_g", [P, 2, D])
        qn_t0 = sb("qn_t0", [P, B * S])

        a_ctx = ExitStack()
        wq_hi0 = sb("wq_hi0", [P, NP * 256], F32R, a_ctx)
        wq_lo0 = sb("wq_lo0", [P, NP * 256], F32R, a_ctx)
        wq_hl1 = sb("wq_hl1", [P, NP * 256], F32R, a_ctx)
        wout_hi = sb("wout_hi", [P, NP * D], F32R, a_ctx)
        wout_lo = sb("wout_lo", [P, NP * D], F32R, a_ctx)
        mask_pad = sb("mask_pad", [P, 2 * P], F32, a_ctx)
        rope = sb("rope", [P, 2 * S], F32, a_ctx)
        rope_tok = sb("rope_tok", [P, NT, 2 * DR], F32, a_ctx)
        inv_n = sb("inv_n", [P, 2 * NT], F32, a_ctx)
        rms_eps = sb("rms_eps", [P, 2 * NT], F32, a_ctx)
        qn_t1 = sb("qn_t1", [P, B * S], F32, a_ctx)
        key_t = sb("key_t", [P, B * S], F32, a_ctx)
        lat = sb("lat", [P, B * NT * KL], F32, a_ctx)

        w_ctx = ExitStack()
        wa_hi = sb("wa_hi", [P, KD * WA], F32R, w_ctx)
        wa_lo = sb("wa_lo", [P, KD * WA], F32R, w_ctx)

        s_ctx = ExitStack()
        wqa_nat = sb("wqa_nat", [P, 2, D], F32, s_ctx)
        wkva_nat = sb("wkva_nat", [P, D], F32, s_ctx)
        c_nat = sb("c_nat", [B, 4, D], F32, s_ctx)
        silu = sb("silu", [B, D], F32, s_ctx)
        silu_t = sb("silu_t", [P, KD * B], F32, s_ctx)
        mod_nat = sb("mod_nat", [B, 6 * D], F32, s_ctx)
        gate_sign = sb("gate_sign", [B, 2, 2 * D], F32, s_ctx)
        gate_abs = sb("gate_abs", [B, 2 * D], F32, s_ctx)
        mod_out = sb("mod_out", [B, 4 * D], F32, s_ctx)
        qw = sb("qw", [P, 2], F32, s_ctx)
        kw_col = sb("kw_col", [P, 1], F32, s_ctx)
        kw_row = sb("kw_row", [P, 256], F32, s_ctx)
        wq_tmp0 = sb("wq_tmp0", [P, 2, 256], F32, s_ctx)
        wq_tmp1 = sb("wq_tmp1", [KW1, 2, 256], F32, s_ctx)
        wkv_nat = sb("wkv_nat", [P, NH * 2, KL], F32, s_ctx)
        wo_t = sb("wo_t", [P, NH, D], F32, s_ctx)
        wqn_nat = qn_t0[:, 0:NH * QL].rearrange("p (h r) -> p h r", h=NH)
        wqp_nat = lat[:, 0:NP * QL].rearrange("p (h r) -> p h r", h=NP)
        wo_nat = key_t[:, :].rearrange("p (t n) -> p t n", t=2)
        wmod_nat = qn_t1[:, 0:KD * 6 * D].rearrange("p (k n) -> p k n", k=KD)
        s_ctx.close()

        p_ctx = ExitStack()
        xhat = sb("xhat", [P, 2, NT * D], F32, p_ctx)
        mod_col = sb("mod_col", [P, 2, 4], F32, p_ctx)
        h_t = sb("h_t", [P, 2, KD * S], F32, p_ctx)
        h_hi = sb("h_hi", [P, 2, KD * S], F32R, p_ctx)
        h_lo = sb("h_lo", [P, 2, KD * S], F32R, p_ctx)
        sq_junk = sb("sq_junk", [P, 2, NT, QL + KL], F32, p_ctx)
        sumsq = sb("sumsq", [P, 2, 2 * NT], F32, p_ctx)
        rms_mid = sb("rms_mid", [P, 2, 2 * NT], F32, p_ctx)
        rms_var = sb("rms_var", [P, 2, 2 * NT], F32, p_ctx)
        rms_r = sb("rms_r", [P, 2, 2 * NT], F32, p_ctx)
        qn = sb("qn", [P, 2, NT * QL], F32, p_ctx)
        keys = sb("keys", [P, 2, NT * P], F32, p_ctx)
        kr_cos = sb("kr_cos", [P, 2, NT * DR], F32, p_ctx)
        kr_sin = sb("kr_sin", [P, 2, NT * DR], F32, p_ctx)
        p_ctx.close()
        w_ctx.close()

        q_hi0 = sb("q_hi0", [P, S], F32R, a_ctx)
        q_lo0 = sb("q_lo0", [P, S], F32R, a_ctx)
        q_hi1 = sb("q_hi1", [P, S], F32R, a_ctx)
        q_lo1 = sb("q_lo1", [KW1, S], F32R, a_ctx)
        key_hi = sb("key_hi", [P, 2, 2 * S], F32R, a_ctx)
        key_lo = sb("key_lo", [P, 2, 2 * S], F32R, a_ctx)
        gate_a = sb("gate_a", [P, D], F32, a_ctx)
        query = sb("query", [P, 2, 2 * S], F32, a_ctx)
        query_hi = sb("query_hi", [P, 2, 2 * S], F32R, a_ctx)
        query_lo = sb("query_lo", [P, 2, 2 * S], F32R, a_ctx)
        pe_cos = sb("pe_cos", [P, 2, S], F32, a_ctx)
        pe_rot = sb("pe_rot", [P, 2, S], F32, a_ctx)
        scored = sb("scored", [P, 2, 2, SCORE], F32, a_ctx)
        row_min = sb("row_min", [P, 2, 4], F32, a_ctx)
        probs = sb("probs", [P, 2, 2, SCORE], F32, a_ctx)
        row_sum = sb("row_sum", [P, 2, 4], F32, a_ctx)
        row_inv = sb("row_inv", [P, 2, 4], F32, a_ctx)
        probs_t = sb("probs_t", [P, 2, SCORE], F32, a_ctx)
        o_nat = sb("o_nat", [P, 2, 256], F32, a_ctx)
        o_hi = sb("o_hi", [P, 256], F32R, a_ctx)
        o_lo = sb("o_lo", [P, 256], F32R, a_ctx)
        gated = sb("gated", [P, NT * D], F32, a_ctx)
        a_ctx.close()

        w1_nat = qn_t0[:, 0:KD * DFF]
        w2_nat = qn_t0[:, KD * DFF:KD * DFF + NF * D]
        w1_hi = sb("w1_hi", [P, KD * DFF], F32R)
        w1_lo = sb("w1_lo", [P, KD * DFF], F32R)
        w2_hi = sb("w2_hi", [P, NF * D], F32R)
        w2_lo = sb("w2_lo", [P, NF * D], F32R)
        h2 = sb("h2", [P, 2, NT * D])
        h2_n = sb("h2_n", [P, NT * D])
        h2_m = sb("h2_m", [P, NT * D])
        h2_hi = sb("h2_hi", [P, KD * S], F32R)
        h2_lo = sb("h2_lo", [P, KD * S], F32R)
        f_bn = sb("f_bn", [P, NT, 6])
        f_stat = sb("f_stat", [P, NT, 2])
        f_var = sb("f_var", [P, NT])
        f_rstd = sb("f_rstd", [P, NT])
        f_shift = sb("f_shift", [P, NT])
        rout_junk = sb("rout_junk", [P, NT, D])
        rout = sb("rout", [P, 2, NT])
        rout_t = sb("rout_t", [P, 2, NT])
        rout_w = sb("rout_w", [P, 2, NT])
        act_hi = sb("act_hi", [P, NF * S], F32R)
        act_full = sb("act_full", [P, NF * S])
        act_lo = sb("act_lo", [P, NF * S], F32R)
        f_sum = sb("f_sum", [P, NT * D])
        f_mix = sb("f_mix", [P, NT * D])
        f_gate = sb("f_gate", [P, NT * D])
        f_out = sb("f_out", [P, 2, NT * D])

        ld_ident = sem("ld_ident")
        ld_small = sem("ld_small")
        ld_first = sem("ld_first")
        ld_mod = sem("ld_mod")
        ld_wo = sem("ld_wo")
        ld_heads = sem("ld_heads")
        ld_x = [sem(f"ld_x{n}") for n in range(4)]
        mod_stored = sem("mod_stored")
        ld_c = sem("ld_c")
        ld_kwr = sem("ld_kwr")
        kwr_done = sem("kwr_done")
        exp_c = sem("exp_c")
        vec_step = sem("vec_step")
        pool_step = sem("pool_step")
        silu_done = sem("silu_done")
        s_wa_t = sem("s_wa_t")
        s_wa_hi = sem("s_wa_hi")
        s_silu_t = sem("s_silu_t")
        s_silu_sb = sem("s_silu_sb")
        s_mod = sem("s_mod")
        s_mod_sb = sem("s_mod_sb")
        mod_out_done = sem("mod_out_done")
        s_modt = sem("s_modt")
        s_modt_sb = sem("s_modt_sb")
        s_wo_t = sem("s_wo_t")
        s_wo_sb = sem("s_wo_sb")
        s_wout = sem("s_wout")
        s_wout_hi = sem("s_wout_hi")
        s_wout_free = sem("s_wout_free")
        s_wq = sem("s_wq")
        s_wq_tmp = sem("s_wq_tmp")
        s_wq_hi = sem("s_wq_hi")
        s_wq_lo0 = sem("s_wq_lo0")
        s_wq_lo1 = sem("s_wq_lo1")
        var_done = sem("var_done")
        rstd_done = sem("rstd_done")
        pad_done = sem("pad_done")
        p_xhat = sem("p_xhat")
        p_ht = sem("p_ht")
        p_mod = sem("p_mod")
        p_hsb = sem("p_hsb")
        p_split = sem("p_split")
        p_proj = sem("p_proj")
        p_sq = sem("p_sq")
        p_rms = sem("p_rms")
        rope_step = sem("rope_step")
        p_norm = sem("p_norm")
        p_t = sem("p_t")
        p_kept = sem("p_kept")
        gate_loaded = sem("gate_loaded")
        q_hi_done = sem("q_hi_done")
        q_split = sem("q_split")
        a_qgen = sem("a_qgen")
        a_rot = sem("a_rot")
        a_latq = sem("a_latq")
        a_query = sem("a_query")
        a_qhi = sem("a_qhi")
        a_qlo = sem("a_qlo")
        k_hi_done = sem("k_hi_done")
        k_split = sem("k_split")
        a_score = sem("a_score")
        a_masked = sem("a_masked")
        a_exp = sem("a_exp")
        a_ptr = sem("a_ptr")
        a_pt_a = sem("a_pt_a")
        a_pt_b = sem("a_pt_b")
        a_inv = sem("a_inv")
        a_pv = sem("a_pv")
        a_onat = sem("a_onat")
        a_otr = sem("a_otr")
        a_ohi = sem("a_ohi")
        a_olo = sem("a_olo")
        a_out = sem("a_out")
        a_batch = sem("a_batch")
        a_gated = sem("a_gated")
        a_added = sem("a_added")
        ld_ffn = [sem("ld_w1"), sem("ld_w2")]
        ld_ffn_small = sem("ld_ffn_small")
        ld_modh = [sem("ld_modh_even"), sem("ld_modh_odd")]
        ld_modg = [sem("ld_modg_even"), sem("ld_modg_odd")]
        f_hi_w = sem("f_hi_w")
        f_w = sem("f_w")
        f_var_done = sem("f_var_done")
        f_rstd_done = sem("f_rstd_done")
        f_shifted = sem("f_shifted")
        f_xhat = sem("f_xhat")
        f_scaled = sem("f_scaled")
        f_h2 = sem("f_h2")
        f_rout = sem("f_rout")
        f_tanh = sem("f_tanh")
        f_summed = sem("f_summed")
        f_ht = sem("f_ht")
        f_hhi = sem("f_hhi")
        f_hsplit = sem("f_hsplit")
        f_up = sem("f_up")
        f_act = sem("f_act")
        f_lo = sem("f_lo")
        f_down = sem("f_down")
        f_mixed = sem("f_mixed")
        f_gated = sem("f_gated")
        f_done = sem("f_done")
        stored = [sem("stored_even"), sem("stored_odd")]
        left = {e: sem(f"left_{e}") for e in ("tensor", "vector", "scalar", "gpsimd", "sync")}

        def leave(eng, own):
            eng.sem_inc(left[own], 1)

        def enter(eng, own, n):
            for e, s in left.items():
                if e != own:
                    eng.wait_ge(s, n)

        block = ctx.enter_context(nc.Block())

        @block.sync
        def _(sp):
            sp.dma_start(ident[:, :], ident_in).then_inc(ld_ident, 16)
            sp.dma_start(wqa_nat[:, 0, :], wq_a[0:P, :]).then_inc(ld_first, 16)
            sp.dma_start(wqa_nat[0:KW1, 1, :], wq_a[P:QL, :]).then_inc(ld_first, 16)
            sp.dma_start(wkva_nat[:, :], wkv_a).then_inc(ld_first, 16)
            x_rows = x.rearrange("b (t p) d -> p (b t) d", p=P)
            out_rows = out.rearrange("b (t p) d -> p (b t) d", p=P)
            x_tiles = x_sb[:, :].rearrange("p (n d) -> p n d", d=D)

            def load_x(i):
                n = B * NT // 4
                sp.dma_start(x_tiles[:, n * i:n * i + n, :], x_rows[:, n * i:n * i + n, :]).then_inc(ld_x[i], 16)

            load_x(0)
            sp.dma_start(wmod_nat, wmod.rearrange("(k p) n -> p k n", p=P)).then_inc(ld_mod, 16)
            load_x(1)
            sp.dma_start(wo_nat, wo.rearrange("(t p) n -> p t n", p=P)).then_inc(ld_wo, 16)
            heads = wq_b.rearrange("(h d) r -> d h r", d=DN + DR)
            sp.dma_start(wkv_nat[:, :, :], wkv_b.rearrange("(h d) c -> d h c", d=P)).then_inc(ld_heads, 16)
            sp.dma_start(wqn_nat, heads[0:DN, :, :]).then_inc(ld_heads, 16)
            by_pair = wq_b.rearrange("(g t d) r -> d t g r", t=2, d=DN + DR)
            for place, head in enumerate((1, 0)):
                for n, (half, g) in enumerate(RUNS):
                    row, d = place * DR + n * 16, DN + half * 32 + g * 16
                    sp.dma_start(wqp_nat[row:row + 16, :, :], by_pair[d:d + 16, head, :, :]).then_inc(ld_heads, 16)
            load_x(2)
            load_x(3)
            sp.dma_start(b1_col[:, :], b1).then_inc(ld_ffn_small, 16)
            sp.dma_start(b2_row[:, :], b2.rearrange("(a n) -> a n", a=1).broadcast_to([P, D])).then_inc(ld_ffn_small, 16)
            sp.dma_start(rw_row[:, :], router_w.rearrange("(a n) -> a n", a=1).broadcast_to([P, D])).then_inc(ld_ffn_small, 16)
            sp.dma_start(rb_col[:, 0:1], router_b.rearrange("(a n) -> a n", a=1).broadcast_to([P, 1])).then_inc(ld_ffn_small, 16)
            sp.wait_ge(mod_out_done, 1)
            sp.dma_start(mod_rows, mod_out[:, :]).then_inc(mod_stored, 16)
            sp.wait_ge(mod_stored, 16)
            leave(sp, "sync")
            leave(sp, "sync")

            enter(sp, "sync", 2)
            sp.dma_start(gate_a[:, :], mod_rows[0:1, 0:D].broadcast_to([P, D])).then_inc(gate_loaded, 16)
            with sp.Fori(1, B) as b:
                sp.wait_ge(a_gated, b)
                sp.dma_start(gate_a[:, :], mod_rows[bass.ds(b, 1), 0:D].broadcast_to([P, D])).then_inc(gate_loaded, 16)

            leave(sp, "sync")

            sp.wait_ge(q_split, B)
            sp.dma_start(w1_nat.rearrange("p (k n) -> p k n", k=KD), w1.rearrange("(k p) n -> p k n", p=P)).then_inc(ld_ffn[0], 16)
            sp.dma_start(w2_nat.rearrange("p (k n) -> p k n", k=NF), w2.rearrange("(k p) n -> p k n", p=P)).then_inc(ld_ffn[1], 16)

            def load_h(b, slot):
                sp.dma_start(mod_h[:, slot, :], mod_rows[bass.ds(b, 1), D:3 * D].broadcast_to([P, 2 * D])).then_inc(ld_modh[slot], 16)

            def load_g(b, slot):
                sp.dma_start(mod_g[:, slot, :], mod_rows[bass.ds(b, 1), 3 * D:4 * D].broadcast_to([P, D])).then_inc(ld_modg[slot], 16)

            def next_h(b, slot):
                sp.wait_ge(f_h2, b + 1)
                load_h(b + 2, slot)

            def next_g(b, slot):
                sp.wait_ge(f_gated, b + 1)
                load_g(b + 2, slot)

            def store(b, slot):
                sp.wait_ge(f_done, b + 1)
                sp.dma_start(out_rows[:, bass.ds(b * NT, NT), :],
                             f_out[:, slot, :].rearrange("p (t d) -> p t d", d=D)).then_inc(stored[slot], 16)

            for slot in range(2):
                load_h(slot, slot)
                load_g(slot, slot)
            next_h(0, 0)
            with sp.Fori(0, B // 2 - 2) as i:
                for slot in range(2):
                    next_h(2 * i + slot + 1, 1 - slot)
                    next_g(2 * i + slot, slot)
                    store(2 * i + slot, slot)
            next_h(B - 3, 1)
            for b in range(B - 4, B):
                if b < B - 2:
                    next_g(b, b % 2)
                store(b, b % 2)
            for slot in range(2):
                sp.wait_ge(stored[slot], 16 * (B // 2))

        @block.tensor
        def _(pe):
            mm = nc.tensor.matmul

            def three(out_ap, left_hl, right_hl, start, stop, **kw):
                (lh, ll), (rh, rl) = left_hl, right_hl
                mm(out_ap, lh, rh, start=start, stop=False, **kw)
                mm(out_ap, ll, rh, start=False, stop=False, **kw)
                return mm(out_ap, lh, rl, start=False, stop=stop, **kw)

            pe.wait_ge(ld_ident, 16)
            pe.wait_ge(ld_first, 48)
            for k in range(KD):
                cols = slice(k * P, k * P + P)
                nc.tensor.transpose(bank[k][:, 0:P], wqa_nat[:, 0, cols], ident[:, :])
                nc.tensor.transpose(bank[k][:, P:QL], wqa_nat[0:KW1, 1, cols], ident[0:KW1, 0:KW1])
                nc.tensor.transpose(bank[k][:, QL:WA], wkva_nat[:, cols], ident[:, :]).then_inc(s_wa_t, 1)
            pe.wait_ge(silu_done, 1)
            for k in range(KD):
                last = nc.tensor.transpose(bank[2][:, k * B:k * B + B], silu[:, k * P:k * P + P], ident[0:B, 0:B])
            last.then_inc(s_silu_t, 1)
            pe.wait_ge(s_silu_sb, 1)
            pe.wait_ge(ld_mod, 16)
            for n in range(3):
                for k in range(KD):
                    last = mm(bank[3 + n][0:B, :], silu_t[:, k * B:k * B + B], wmod_nat[:, k, n * 512:n * 512 + 512],
                              start=(k == 0), stop=(k == KD - 1))
            last.then_inc(s_mod, 1)
            pe.wait_ge(s_mod_sb, 1)
            for n in range(4):
                last = nc.tensor.transpose(bank[6][:, n * B:n * B + B], mod_nat[:, n * P:n * P + P], ident[0:B, 0:B])
            last.then_inc(s_modt, 1)
            pe.wait_ge(ld_wo, 16)
            pe.wait_ge(s_wa_hi, 2)
            for n in range(NP):
                if n >= 2:
                    pe.wait_ge(s_wo_sb, n - 1)
                for j in range(4):
                    h, t = 2 * n + j // 2, j % 2
                    last = nc.tensor.transpose(bank[n % 2][:, j * P:j * P + P], wo_nat[:, t, h * P:h * P + P], ident[:, :])
                last.then_inc(s_wo_t, 1)
            pe.wait_ge(ld_heads, 16 * 10)
            pe.wait_ge(s_mod_sb, 1)
            for n in range(NP):
                pe.wait_ge(s_wo_sb, n + 1)
                if n == 0:
                    pe.wait_ge(s_silu_sb, 1)
                if n >= 2:
                    pe.wait_ge(s_wout_free, n - 1)
                for j in range(2):
                    h = 2 * n + j
                    last = mm(bank[2 + n % 2][64 * j:64 * j + 64, 0:D], wkv_nat[:, 2 * h + 1, :], wo_t[:, h, :], start=True, stop=True)
                last.then_inc(s_wout, 1)
                if n >= 2:
                    pe.wait_ge(s_wq_tmp, n - 1)
                q = bank[4 + n % 2]
                for j in range(2):
                    h = 2 * n + j
                    mm(q[:, j * 64:j * 64 + 64], wqn_nat[:, h, 0:P], wkv_nat[:, 2 * h, :], start=True, stop=True)
                    mm(q[0:KW1, 256 + j * 64:320 + j * 64], wqn_nat[:, h, P:QL], wkv_nat[:, 2 * h, :], start=True, stop=True)
                nc.tensor.transpose(q[:, P:2 * P], wqp_nat[:, n, 0:P], ident[:, :])
                nc.tensor.transpose(q[0:KW1, 3 * P:4 * P], wqp_nat[:, n, P:QL], ident[:, :]).then_inc(s_wq, 1)
            leave(pe, "tensor")

            enter(pe, "tensor", 1)

            def turn_x(i, first=False):
                for s in range(2):
                    pe.wait_ge(p_xhat, 2 * i + s + 1)
                    if not first:
                        pe.wait_ge(p_hsb, 2 * i + s - 1)
                    for k in range(KD):
                        for t in range(NT):
                            last = nc.tensor.transpose(bank[s][:, k * S + t * P:k * S + t * P + P],
                                                       xhat[:, s, t * D + k * P:t * D + k * P + P], ident[:, :])
                    last.then_inc(p_ht, 1)

            def project_x(i, s, first=False):
                pe.wait_ge(p_split, 2 * i + s + 1)
                if not first:
                    pe.wait_ge(p_norm, 2 * i + s - 1)
                for t in range(NT):
                    for k in range(KD):
                        c0 = k * S + t * P
                        last = three(bank[2 + 2 * s + t][:, 0:WA], (h_hi[:, s, c0:c0 + P], h_lo[:, s, c0:c0 + P]),
                                     (wa_hi[:, k * WA:k * WA + WA], wa_lo[:, k * WA:k * WA + WA]), k == 0, k == KD - 1)
                last.then_inc(p_proj, 1)

            def turn_rows(i, s, first=False):
                pe.wait_ge(p_norm, 2 * i + s + 1)
                if not (first and s == 0):
                    pe.wait_ge(p_kept, 2 * i + s)
                for t in range(NT):
                    c0 = t * P
                    nc.tensor.transpose(bank[6][:, c0:c0 + P], qn[:, s, t * QL:t * QL + P], ident[:, :])
                    nc.tensor.transpose(bank[6][0:KW1, S + c0:S + c0 + P], qn[:, s, t * QL + P:t * QL + QL], ident[:, :])
                    last = nc.tensor.transpose(bank[7][:, c0:c0 + P], keys[:, s, t * P:t * P + P], ident[:, :])
                last.then_inc(p_t, 1)

            def two_batches(i, first=False, last=False):
                project_x(i, 0, first)
                if not last:
                    turn_x(i + 1)
                project_x(i, 1, first)
                turn_rows(i, 0, first)
                turn_rows(i, 1)

            turn_x(0, True)
            two_batches(0, first=True)
            with pe.Fori(1, B // 2 - 1) as i:
                two_batches(i)
            two_batches(B // 2 - 1, last=True)
            leave(pe, "tensor")

            enter(pe, "tensor", 2)

            def queries(b, p, first=False):
                if p == 0:
                    pe.wait_ge(q_split, b + 1)
                if not first:
                    pe.wait_ge(a_latq, NP * b + p)
                for tile in range(2):
                    w = slice(p * 256 + tile * P, p * 256 + tile * P + P)
                    dst = bank[0][:, tile * S:tile * S + S]
                    three(dst, (wq_hi0[:, w], wq_lo0[:, w]), (q_hi0[:, :], q_lo0[:, :]), True, False)
                    mm(dst, wq_hl1[:, w], q_hi1[:, :], start=False, stop=False)
                    last = mm(dst, wq_hl1[0:KW1, w], q_lo1[:, :], start=False, stop=True)
                last.then_inc(a_qgen, 1)

            def scores(b, p, first=False):
                pe.wait_ge(a_qlo, NP * b + p + 1)
                if p == 0:
                    pe.wait_ge(k_split, b + 1)
                if not first:
                    pe.wait_ge(a_masked, 2 * (NP * b + p))
                for j in range(2):
                    for t, (q0, n) in enumerate(((0, P), (P, S))):
                        qs = slice(j * S + q0, j * S + q0 + P)
                        ks = bass.ds((b % 2) * S, n)
                        last = three(bank[1 + j][:, q0:q0 + n], (query_hi[:, p % 2, qs], query_lo[:, p % 2, qs]),
                                     (key_hi[:, j, ks], key_lo[:, j, ks]), True, True)
                    last.then_inc(a_score, 1)

            def turn_probs(b, p, first=False):
                u = NP * b + p
                pe.wait_ge(a_exp, 2 * (u + 1))
                if not first:
                    pe.wait_ge(a_pt_a, u)
                    pe.wait_ge(a_pt_b, u)
                for j in range(2):
                    for n in range(3):
                        last = nc.tensor.transpose(bank[3 + j][:, n * P:n * P + P], probs[:, p % 2, j, n * P:n * P + P], ident[:, :])
                    last.then_inc(a_ptr, 1)

            def weigh(b, p, first=False):
                u = NP * b + p
                if not first:
                    pe.wait_ge(a_onat, u)
                for j in range(2):
                    pe.wait_ge((a_pt_a, a_pt_b)[j], u + 1)
                    for t in range(NT):
                        dst = bank[5][:, (j * NT + t) * KL:(j * NT + t) * KL + KL]
                        for k in range(t + 1):
                            src = probs_t[:, j, (t + k) * P:(t + k) * P + P]
                            last = mm(dst, src, lat[:, bass.ds((b * NT + k) * KL, KL)], start=(k == 0), stop=(k == t))
                last.then_inc(a_pv, 1)

            def turn_o(b, p, first=False):
                u = NP * b + p
                pe.wait_ge(a_onat, u + 1)
                if not first:
                    pe.wait_ge(a_olo, u)
                for t in range(NT):
                    last = nc.tensor.transpose(bank[6][:, t * P:t * P + P], o_nat[:, p % 2, t * P:t * P + P], ident[:, :])
                last.then_inc(a_otr, 1)

            def project(b, p, first=False):
                u = NP * b + p
                pe.wait_ge(a_olo, u + 1)
                if p == 0 and not first:
                    pe.wait_ge(a_gated, b)
                for t in range(NT):
                    dst = bank[7][:, t * D:t * D + D]
                    w = slice(p * D, p * D + D)
                    last = three(dst, (o_hi[:, t * P:t * P + P], o_lo[:, t * P:t * P + P]), (wout_hi[:, w], wout_lo[:, w]),
                                 p == 0 and t == 0, p == NP - 1, skip_group_check=True)
                last.then_inc(a_out, 1)

            def before(b, p, lag):
                return (b, p - lag) if p >= lag else (b - 1, p - lag + NP)

            def attention(b, first=False, last=False):
                for p in range(NP):
                    if not first or p >= 1:
                        turn_probs(*before(b, p, 1), first and p == 1)
                    scores(b, p, first and p == 0)
                    if not first or p >= 1:
                        weigh(*before(b, p, 1), first and p == 1)
                    if not first or p >= 2:
                        turn_o(*before(b, p, 2), first and p == 2)
                    if p + 2 < NP:
                        queries(b, p + 2)
                    elif not last:
                        queries(b + 1, p + 2 - NP)
                    if not first or p >= 2:
                        project(*before(b, p, 2), first and p == 2)

            queries(0, 0, True)
            queries(0, 1)
            attention(0, first=True)
            with pe.Fori(1, B - 1) as b:
                attention(b)
            attention(B - 1, last=True)
            turn_probs(B - 1, NP - 1)
            turn_o(B - 1, NP - 2)
            weigh(B - 1, NP - 1)
            project(B - 1, NP - 2)
            turn_o(B - 1, NP - 1)
            project(B - 1, NP - 1)
            leave(pe, "tensor")

            enter(pe, "tensor", 3)

            def turn_h(b, slot):
                pe.wait_ge(f_h2, b + 1)
                for k in range(KD):
                    for t in range(NT):
                        last = nc.tensor.transpose(bank[6][:, k * S + t * P:k * S + t * P + P],
                                                   h2[:, slot, t * D + k * P:t * D + k * P + P], ident[:, :])
                last.then_inc(f_ht, 1)

            def up(b, first=False):
                pe.wait_ge(f_hsplit, b + 1)
                for g in range(NF // 2):
                    if not first:
                        pe.wait_ge(f_act, (b - 1) * (NF // 2) + g + 1)
                    for j in range(2):
                        f = 2 * g + j
                        for k in range(KD):
                            w = slice(k * DFF + f * P, k * DFF + f * P + P)
                            last = three(bank[g][:, j * S:j * S + S], (w1_hi[:, w], w1_lo[:, w]),
                                         (h2_hi[:, k * S:k * S + S], h2_lo[:, k * S:k * S + S]), k == 0, k == KD - 1)
                    last.then_inc(f_up, 1)

            def down(b, slot, first=False, last=False):
                if not first:
                    pe.wait_ge(f_summed, b)
                for g in range(NF // 2):
                    pe.wait_ge(f_lo, (NF // 2) * b + g + 1)
                    for f in (2 * g, 2 * g + 1):
                        for t in range(NT):
                            a = slice(f * S + t * P, f * S + t * P + P)
                            done = three(bank[4 + t][:, 0:D], (act_hi[:, a], act_lo[:, a]),
                                         (w2_hi[:, f * D:f * D + D], w2_lo[:, f * D:f * D + D]), f == 0, f == NF - 1)
                    if g == 1 and not last:
                        turn_h(b + 1, 1 - slot)
                done.then_inc(f_down, 1)

            turn_h(0, 0)
            pe.wait_ge(f_w, 1)
            up(0, True)
            pe.wait_ge(f_w, 2)
            down(0, 0, first=True)
            with pe.Fori(0, (B - 2) // 2) as i:
                for slot in range(2):
                    up(2 * i + 1 + slot)
                    down(2 * i + 1 + slot, 1 - slot)
            up(B - 1)
            down(B - 1, 1, last=True)

        @block.vector
        def _(dve):
            v = nc.vector
            step = [0]
            carried = [0]

            def link(ins):
                step[0] += 1
                ins.then_inc(vec_step, 1)
                dve.wait_ge(vec_step, step[0])

            def carry_wait():
                carried[0] = (carried[0] + 1) % 64
                v.memset(spare[:, carried[0]:carried[0] + 1], 0.0)

            dve.wait_ge(exp_c, 1)
            link(v.tensor_scalar_add(c_nat[:, 2, :], c_nat[:, 1, :], 1.0))
            link(v.reciprocal(c_nat[:, 3, :], c_nat[:, 2, :]))
            v.tensor_tensor(silu[:, :], c_nat[:, 0, :], c_nat[:, 3, :], ALU.mult).then_inc(silu_done, 1)

            def statistics(i):
                dve.wait_ge(ld_x[i], 16)
                for n in range(B * NT // 4 * i, B * NT // 4 * (i + 1)):
                    last = v.bn_stats(bn_raw[:, n, :], x_sb[:, n * D:n * D + D])
                return last

            statistics(0)
            for k in range(KD):
                dve.wait_ge(s_wa_hi, k + 1)
                w = slice(k * WA, k * WA + WA)
                v.tensor_tensor(wa_lo[:, w], bank[k][:, 0:WA], wa_hi[:, w].bitcast(F32), ALU.subtract)
            dve.wait_ge(s_silu_t, 1)
            v.tensor_copy(silu_t[:, :], bank[2][:, 0:KD * B]).then_inc(s_silu_sb, 1)
            statistics(1)
            dve.wait_ge(s_mod, 1)
            for n in range(3):
                last = v.tensor_copy(mod_nat[:, n * 512:n * 512 + 512], bank[3 + n][0:B, :])
            last.then_inc(s_mod_sb, 1)
            dve.wait_ge(s_mod_sb, 1)
            for n, part in enumerate((2, 5)):
                g = mod_nat[:, part * D:part * D + D]
                v.tensor_scalar(gate_sign[:, 0, n * D:n * D + D], g, 0.0, 2.0, ALU.is_ge, ALU.mult)
                last = v.scalar_tensor_tensor(out=gate_sign[:, 1, n * D:n * D + D], in0=g, scalar=-1.0, in1=g,
                                              op0=ALU.mult, op1=ALU.max)
            link(last)
            link(v.tensor_scalar_max(gate_abs[:, :], gate_sign[:, 1, :], 0.25))
            for n, part in enumerate((0, 3)):
                v.scalar_tensor_tensor(out=mod_out[:, part * D:part * D + D], in0=gate_sign[:, 0, n * D:n * D + D],
                                       scalar=-1.0, in1=gate_abs[:, n * D:n * D + D], op0=ALU.add, op1=ALU.mult)
            v.tensor_scalar_add(mod_out[:, D:2 * D], mod_nat[:, 4 * D:5 * D], 1.0)
            v.tensor_copy(mod_out[:, 2 * D:3 * D], mod_nat[:, 3 * D:4 * D]).then_inc(mod_out_done, 1)
            dve.wait_ge(s_modt, 1)
            v.tensor_copy(mod_t[:, 0:2 * B], bank[6][:, 0:2 * B])
            v.tensor_scalar_add(mod_t[:, 2 * B:4 * B], bank[6][:, 2 * B:4 * B], 1.0)
            statistics(2)
            link(statistics(3))
            even, odd = bn_raw[:, :, 0:3], bn_raw[:, :, 3:6]
            v.tensor_tensor(tok_mean[:, :], even[:, :, 1], odd[:, :, 1], ALU.add)
            v.tensor_tensor(tok_gap[:, :], even[:, :, 1], odd[:, :, 1], ALU.subtract)
            link(v.tensor_tensor(tok_m2[:, :], even[:, :, 2], odd[:, :, 2], ALU.add))
            link(v.scalar_tensor_tensor(out=tok_gap2[:, :], in0=tok_gap[:, :], scalar=0.25, in1=tok_gap[:, :],
                                        op0=ALU.mult, op1=ALU.mult))
            link(v.scalar_tensor_tensor(out=tok_shift[:, :], in0=tok_m2[:, :], scalar=1.0 / D, in1=tok_gap2[:, :],
                                        op0=ALU.mult, op1=ALU.add))
            v.tensor_scalar_add(tok_var[:, :], tok_shift[:, :], LN_EPS).then_inc(var_done, 1)
            dve.wait_ge(ld_small, 16 * 7)
            dve.wait_ge(ld_kwr, 32)
            dve.wait_ge(kwr_done, 1)

            def rest(n):
                dve.wait_ge(s_wq_hi, n + 1)
                w = slice(n * 256, n * 256 + 256)
                v.tensor_tensor(wq_hl1[KW1:P, w], wq_tmp1[:, n % 2, :], wq_hl1[0:KW1, w].bitcast(F32), ALU.subtract).then_inc(s_wq_lo1, 1)

            for n in range(NP):
                dve.wait_ge(s_wq, n + 1)
                if n >= 2:
                    dve.wait_ge(s_wq_lo0, n - 1)
                    dve.wait_ge(s_wq_lo1, n - 1)
                q = bank[4 + n % 2]
                v.scalar_tensor_tensor(out=wq_tmp0[:, n % 2, :], in0=q[:, 0:256], scalar=qw[:, 0:1], in1=kw_row[:, :],
                                       op0=ALU.mult, op1=ALU.mult)
                v.scalar_tensor_tensor(out=wq_tmp1[:, n % 2, :], in0=q[0:KW1, 256:512], scalar=qw[0:KW1, 1:2],
                                       in1=kw_row[0:KW1, :], op0=ALU.mult, op1=ALU.mult).then_inc(s_wq_tmp, 1)
                dve.wait_ge(s_wout_hi, n + 1)
                w = slice(n * D, n * D + D)
                v.scalar_tensor_tensor(out=wout_lo[:, w], in0=bank[2 + n % 2][:, 0:D], scalar=kw_col[:, 0:1],
                                       in1=wout_hi[:, w].bitcast(F32), op0=ALU.mult, op1=ALU.subtract).then_inc(s_wout_free, 1)
                if n:
                    rest(n - 1)
            rest(NP - 1)
            dve.wait_ge(rstd_done, 1)
            link(v.scalar_tensor_tensor(out=tok_shift[:, :], in0=tok_mean[:, :], scalar=-0.5, in1=tok_rstd[:, :],
                                        op0=ALU.mult, op1=ALU.mult))
            leave(dve, "vector")

            enter(dve, "vector", 1)
            base = step[0]

            def normed(i, first=False):
                for s in range(2):
                    b = 2 * i + s
                    if not first:
                        dve.wait_ge(p_ht, 2 * i + s - 1)
                    for t in range(NT):
                        g = b * NT + t
                        last = v.tensor_scalar(xhat[:, s, t * D:t * D + D], x_sb[:, bass.ds(g * D, D)],
                                               tok_rstd[:, bass.ds(g, 1)], tok_shift[:, bass.ds(g, 1)], ALU.mult, ALU.add)
                    last.then_inc(p_xhat, 1)
                    if not first:
                        dve.wait_ge(p_hsb, 2 * i + s - 1)
                    v.tensor_copy(mod_col[:, s, :], mod_t[:, :].rearrange("p (n b) -> p n b", b=B)[:, :, bass.ds(b, 1)]
                                  .rearrange("p n a -> p (n a)")).then_inc(p_mod, 1)

            def split_x(i, s, first=False):
                dve.wait_ge(p_hsb, 2 * i + s + 1)
                if not first:
                    dve.wait_ge(p_proj, 2 * i + s - 1)
                v.tensor_copy(h_hi[:, s, :], h_t[:, s, :]).then_inc(vec_step, 1)
                dve.wait_ge(vec_step, 2 * i + base + s + 1)
                v.tensor_tensor(h_lo[:, s, :], h_t[:, s, :], h_hi[:, s, :].bitcast(F32), ALU.subtract).then_inc(p_split, 1)

            def rows(i, s, first=False):
                dve.wait_ge(p_rms, 2 * i + s + 1)
                if not first:
                    dve.wait_ge(p_t, 2 * i + s - 1)
                for t in range(NT):
                    src = bank[2 + 2 * s + t]
                    rq, rk = rms_r[:, s, 2 * t:2 * t + 1], rms_r[:, s, 2 * t + 1:2 * t + 2]
                    v.tensor_scalar(qn[:, s, t * QL:t * QL + QL], src[:, 0:QL], rq, None, ALU.mult)
                    v.tensor_scalar(keys[:, s, t * P:t * P + KL], src[:, QL:QL + KL], rk, None, ALU.mult)
                    v.tensor_scalar(lat[:, bass.ds(((2 * i + s) * NT + t) * KL, KL)], src[:, QL:QL + KL], rk, None, ALU.mult)
                    r0, r1, r2 = QL + KL, QL + KL + DR // 2, WA
                    v.tensor_tensor(kr_cos[:, s, t * DR:t * DR + DR], src[:, r0:r2], rope_tok[:, t, 0:DR], ALU.mult)
                    v.tensor_tensor(kr_sin[:, s, t * DR:t * DR + DR // 2], src[:, r1:r2], rope_tok[:, t, DR:DR + DR // 2], ALU.mult)
                    last = v.tensor_tensor(kr_sin[:, s, t * DR + DR // 2:t * DR + DR], src[:, r0:r1],
                                           rope_tok[:, t, DR + DR // 2:2 * DR], ALU.mult)
                last.then_inc(rope_step, 1)
                dve.wait_ge(rope_step, 2 * i + s + 1)
                for t in range(NT):
                    def runs(a):
                        return a.rearrange("p (h g j) -> p h g j", h=2, g=2)
                    dst = keys[:, s, t * P + KL:t * P + P].rearrange("p (g h j) -> p h g j", g=2, h=2)
                    last = v.tensor_tensor(dst, runs(kr_cos[:, s, t * DR:t * DR + DR]), runs(kr_sin[:, s, t * DR:t * DR + DR]), ALU.add)
                last.then_inc(p_norm, 1)

            def two_batches(i, first=False, last=False):
                if not last:
                    normed(i + 1)
                rows(i, 0, first)
                if not last:
                    split_x(i + 1, 0)
                    split_x(i + 1, 1)
                rows(i, 1, first)

            normed(0, True)
            split_x(0, 0, True)
            split_x(0, 1, True)
            two_batches(0, first=True)
            with dve.Fori(1, B // 2 - 1) as i:
                two_batches(i)
            two_batches(B // 2 - 1, last=True)
            step[0] += B
            leave(dve, "vector")

            enter(dve, "vector", 2)

            def split_key(b):
                dve.wait_ge(k_hi_done, b + 1)
                src, dst, lo, hi = key_t[:, bass.ds(b * S, S)], bass.ds((b % 2) * S, S), slice(0, 64), slice(64, P)
                rounded = key_hi[:, 0, :].bitcast(F32)
                v.tensor_tensor(key_lo[:, 0, dst], src, rounded[:, dst], ALU.subtract)
                v.tensor_tensor(key_lo[lo, 1, dst], src[hi, :], rounded[hi, dst], ALU.subtract)
                v.tensor_tensor(key_lo[hi, 1, dst], src[lo, :], rounded[lo, dst], ALU.subtract).then_inc(k_split, 1)

            def split_query(b, p):
                dve.wait_ge(a_qhi, NP * b + p + 1)
                v.tensor_tensor(query_lo[:, p % 2, :], query[:, p % 2, :], query_hi[:, p % 2, :].bitcast(F32),
                                ALU.subtract).then_inc(a_qlo, 1)


            def split_q(b):
                dve.wait_ge(q_hi_done, b + 1)
                v.tensor_tensor(q_lo0[:, :], qn_t0[:, bass.ds(b * S, S)], q_hi0[:, :].bitcast(F32), ALU.subtract)
                v.tensor_tensor(q_lo1[:, :], qn_t1[0:KW1, bass.ds(b * S, S)], q_hi1[0:KW1, :].bitcast(F32), ALU.subtract).then_inc(q_split, 1)

            def masked(b, p):
                u = NP * b + p
                if not isinstance(b, int) or u >= 2:
                    dve.wait_ge(a_exp, 2 * (u - 1))
                for j in range(2):
                    dve.wait_ge(a_score, 2 * u + j + 1)
                    carry_wait()
                    s, o, m = bank[1 + j], scored[:, p % 2, j, :], row_min[:, p % 2, :]
                    v.tensor_tensor_reduce(out=o[:, 0:P], in0=s[:, 0:P], in1=mask_pad[:, P:2 * P], scale=-SCALE, scalar=3.0e38,
                                           op0=ALU.add, op1=ALU.min, accum_out=m[:, 2 * j:2 * j + 1])
                    v.tensor_tensor_reduce(out=o[:, P:SCORE], in0=s[:, P:SCORE], in1=mask_pad[:, :], scale=-SCALE, scalar=3.0e38,
                                           op0=ALU.add, op1=ALU.min, accum_out=m[:, 2 * j + 1:2 * j + 2]).then_inc(a_masked, 1)

            def rotate(b, p):
                u = NP * b + p
                dve.wait_ge(a_qgen, u + 1)
                if not isinstance(b, int) or u >= 2:
                    dve.wait_ge(a_query, u - 1)
                v.tensor_tensor(pe_cos[:, p % 2, :], bank[0][:, S:2 * S], rope[:, 0:S], ALU.mult)
                v.stream_shuffle(pe_rot[:, p % 2, :], bank[0][:, S:2 * S], SWAP16).then_inc(a_rot, 1)

            def keep_pt(b, p):
                u = NP * b + p
                dve.wait_ge(a_ptr, 2 * u + 1)
                if not isinstance(b, int) or u >= 1:
                    dve.wait_ge(a_pv, u)
                v.tensor_copy(probs_t[:, 0, :], bank[3][:, 0:SCORE]).then_inc(a_pt_a, 1)

            def invert(b, p):
                dve.wait_ge(a_exp, 2 * (NP * b + p + 1))
                v.reciprocal(row_inv[:, p % 2, :], row_sum[:, p % 2, :]).then_inc(a_inv, 1)

            def norm_o(b, p):
                u = NP * b + p
                dve.wait_ge(a_pv, u + 1)
                dve.wait_ge(a_inv, u + 1)
                if not isinstance(b, int) or u >= 2:
                    dve.wait_ge(a_otr, u - 1)
                src = bank[5][:, 0:256].rearrange("p (h t c) -> p h t c", h=2, t=NT)
                dst = o_nat[:, p % 2, :].rearrange("p (t h c) -> p h t c", h=2, t=NT)
                inv = row_inv[:, p % 2, :].rearrange("p (h t a) -> p h t a", h=2, a=1).broadcast_to([P, 2, NT, KL])
                v.tensor_tensor(dst, src, inv, ALU.mult).then_inc(a_onat, 1)

            def split_o(b, p):
                u = NP * b + p
                dve.wait_ge(a_ohi, u + 1)
                v.tensor_tensor(o_lo[:, :], bank[6][:, 0:256], o_hi[:, :].bitcast(F32), ALU.subtract).then_inc(a_olo, 1)

            def gate(b):
                dve.wait_ge(a_out, NP * (b + 1))
                dve.wait_ge(gate_loaded, 16 * (b + 1))
                if not isinstance(b, int) or b >= 1:
                    dve.wait_ge(a_added, b)
                for t in range(NT):
                    last = v.tensor_tensor(gated[:, t * D:t * D + D], bank[7][:, t * D:t * D + D], gate_a[:, :], ALU.mult)
                last.then_inc(a_gated, 1)

            def before(b, p, lag):
                return (b, p - lag) if p >= lag else (b - 1, p - lag + NP)

            def attention(b, first=False, last=False):
                for p in range(NP):
                    if not first or p >= 1:
                        keep_pt(*before(b, p, 1))
                    masked(b, p)
                    if not first or p >= 1:
                        invert(*before(b, p, 1))
                    if p == NP - 2 and not last:
                        split_q(b + 1)
                    if not first or p >= 1:
                        norm_o(*before(b, p, 1))
                    if not first or p >= 2:
                        split_o(*before(b, p, 2))
                    if p == NP - 3 and not last:
                        split_key(b + 1)
                    if p + 1 < NP:
                        split_query(b, p + 1)
                    elif not last:
                        split_query(b + 1, 0)
                    if p + 2 < NP:
                        rotate(b, p + 2)
                    elif not last:
                        rotate(b + 1, p + 2 - NP)
                    if p == 1 and not first:
                        gate(b - 1)

            split_q(0)
            split_key(0)
            rotate(0, 0)
            rotate(0, 1)
            split_query(0, 0)
            attention(0, first=True)
            with dve.Fori(1, B - 1) as b:
                attention(b)
            attention(B - 1, last=True)
            keep_pt(B - 1, NP - 1)
            invert(B - 1, NP - 1)
            norm_o(B - 1, NP - 1)
            split_o(B - 1, NP - 2)
            split_o(B - 1, NP - 1)
            gate(B - 1)
            leave(dve, "vector")

            enter(dve, "vector", 3)
            dve.wait_ge(ld_ffn_small, 16 * 4)
            v.tensor_scalar(rb_col[:, 1:2], rb_col[:, 0:1], 0.5, None, ALU.mult)
            base = step[0]

            def chain(b, n, ins):
                ins.then_inc(vec_step, 1)
                dve.wait_ge(vec_step, 2 * b + base + n)

            def variance(b):
                for t in range(NT):
                    last = v.bn_stats(f_bn[:, t, :], x_sb[:, bass.ds((b * NT + t) * D, D)])
                chain(b, 1, last)
                carry_wait()
                for t in range(NT):
                    last = v.bn_aggr(f_stat[:, t, :], f_bn[:, t, :])
                chain(b, 2, last)
                v.tensor_scalar_add(f_var[:, :], f_stat[:, :, 1], LN_EPS).then_inc(f_var_done, 1)

            def normed2(b, first=False):
                dve.wait_ge(f_rstd_done, b + 1)
                v.scalar_tensor_tensor(out=f_shift[:, :], in0=f_stat[:, :, 0], scalar=-1.0, in1=f_rstd[:, :],
                                       op0=ALU.mult, op1=ALU.mult).then_inc(f_shifted, 1)
                if not first:
                    dve.wait_ge(f_scaled, b)
                dve.wait_ge(f_shifted, b + 1)
                for t in range(NT):
                    last = v.tensor_scalar(h2_n[:, t * D:t * D + D], x_sb[:, bass.ds((b * NT + t) * D, D)],
                                           f_rstd[:, t:t + 1], f_shift[:, t:t + 1], ALU.mult, ALU.add)
                last.then_inc(f_xhat, 1)

            def score(b, slot):
                dve.wait_ge(f_h2, b + 1)
                if not isinstance(b, int) or b >= 2:
                    dve.wait_ge(f_tanh, b - 1)
                carry_wait()
                for t in range(NT):
                    last = v.tensor_tensor_reduce(out=rout_junk[:, t, :], in0=h2[:, slot, t * D:t * D + D], in1=rw_row[:, :],
                                                  scale=1.0, scalar=0.0, op0=ALU.mult, op1=ALU.add,
                                                  accum_out=rout[:, slot, t:t + 1])
                last.then_inc(f_rout, 1)

            def split_h(b):
                dve.wait_ge(f_hhi, b + 1)
                v.tensor_tensor(h2_lo[:, :], bank[6][:, :], h2_hi[:, :].bitcast(F32), ALU.subtract).then_inc(f_hsplit, 1)

            def split_act(b, g):
                dve.wait_ge(f_act, (NF // 2) * b + g + 1)
                a = slice(g * 512, g * 512 + 512)
                v.tensor_tensor(act_lo[:, a], act_full[:, a], act_hi[:, a].bitcast(F32), ALU.subtract).then_inc(f_lo, 1)

            def mix(b, slot):
                dve.wait_ge(f_down, b + 1)
                if not isinstance(b, int) or b >= 1:
                    dve.wait_ge(f_gated, b)
                for t in range(NT):
                    v.tensor_tensor(f_sum[:, t * D:t * D + D], bank[4 + t][:, 0:D], b2_row[:, :], ALU.add)
                dve.wait_ge(f_tanh, b + 1)
                last = v.tensor_scalar(rout_w[:, slot, :], rout_t[:, slot, :], 1.0, 0.5, ALU.add, ALU.mult)
                last.then_inc(f_summed, 1)
                dve.wait_ge(f_summed, b + 1)
                for t in range(NT):
                    last = v.scalar_tensor_tensor(out=f_mix[:, t * D:t * D + D], in0=f_sum[:, t * D:t * D + D],
                                                  scalar=rout_w[:, slot, t:t + 1], in1=h2[:, slot, t * D:t * D + D],
                                                  op0=ALU.mult, op1=ALU.add)
                last.then_inc(f_mixed, 1)

            def feed(b, slot, first=False, last=False):
                if not first:
                    mix(b - 1, 1 - slot)
                if not last:
                    variance(b + 1)
                split_act(b, 0)
                if not last:
                    normed2(b + 1)
                split_act(b, 1)
                split_act(b, 2)
                split_act(b, 3)
                if not last:
                    score(b + 1, 1 - slot)
                    split_h(b + 1)

            variance(0)
            normed2(0, True)
            score(0, 0)
            split_h(0)
            dve.wait_ge(f_hi_w, 1)
            v.tensor_tensor(w1_lo[:, :], w1_nat, w1_hi[:, :].bitcast(F32), ALU.subtract).then_inc(f_w, 1)
            dve.wait_ge(f_hi_w, 2)
            v.tensor_tensor(w2_lo[:, :], w2_nat, w2_hi[:, :].bitcast(F32), ALU.subtract).then_inc(f_w, 1)
            feed(0, 0, first=True)
            with dve.Fori(0, (B - 2) // 2) as i:
                feed(2 * i + 1, 1)
                feed(2 * i + 2, 0)
            feed(B - 1, 1, last=True)
            mix(B - 1, 1)

        @block.scalar
        def _(act):
            a = nc.scalar.activation
            act.dma_start(c_nat[:, 0, :], c).then_inc(ld_c, 16)
            act.dma_start(mask_pad[:, :], mask_in).then_inc(ld_small, 16)
            act.dma_start(rope[:, :], rope_rows).then_inc(ld_small, 16)
            act.dma_start(rope_tok[:, :, :], rope_tokens.rearrange("(t p) n -> p t n", p=P)).then_inc(ld_small, 16)
            act.dma_start(qw[:, 0:1], q_norm_w[0:P].rearrange("(p a) -> p a", a=1)).then_inc(ld_small, 16)
            act.dma_start(qw[0:KW1, 1:2], q_norm_w[P:QL].rearrange("(p a) -> p a", a=1)).then_inc(ld_small, 16)
            for j in range(2):
                act.dma_start(kw_col[64 * j:64 * j + 64, :], kv_norm_w.rearrange("(p a) -> p a", a=1)).then_inc(ld_small, 16)
            act.wait_ge(ld_c, 16)
            a(c_nat[:, 1, :], c_nat[:, 0, :], ACT.Exp, scale=-1.0).then_inc(exp_c, 1)
            for k in range(KD):
                act.wait_ge(s_wa_t, k + 1)
                a(wa_hi[:, k * WA:k * WA + WA], bank[k][:, 0:WA], ACT.Copy).then_inc(s_wa_hi, 1)
            for n in range(NP):
                act.wait_ge(s_wo_t, n + 1)
                a(wo_t[:, 2 * n:2 * n + 2, :].rearrange("p h o -> p (h o)"), bank[n % 2][:, :], ACT.Copy).then_inc(s_wo_sb, 1)
            act.wait_ge(ld_small, 16 * 7)
            for n in range(NP):
                act.wait_ge(s_wout, n + 1)
                a(wout_hi[:, n * D:n * D + D], bank[2 + n % 2][:, 0:D], ACT.Copy, scale=kw_col[:, 0:1]).then_inc(s_wout_hi, 1)
                act.wait_ge(s_wq_tmp, n + 1)
                w = slice(n * 256, n * 256 + 256)
                a(wq_hi0[:, w], wq_tmp0[:, n % 2, :], ACT.Copy)
                a(wq_hl1[0:KW1, w], wq_tmp1[:, n % 2, :], ACT.Copy).then_inc(s_wq_hi, 1)
            leave(act, "scalar")

            enter(act, "scalar", 1)

            def modulated(i, s, first=False):
                act.wait_ge(p_ht, 2 * i + s + 1)
                act.wait_ge(p_mod, 2 * i + s + 1)
                if not first:
                    act.wait_ge(p_split, 2 * i + s - 1)
                for k in range(KD):
                    last = a(h_t[:, s, k * S:k * S + S], bank[s][:, k * S:k * S + S], ACT.Identity,
                             bias=mod_col[:, s, k:k + 1], scale=mod_col[:, s, 2 + k:3 + k])
                last.then_inc(p_hsb, 1)

            def squares(i, s, first=False):
                act.wait_ge(p_proj, 2 * i + s + 1)
                if not first:
                    act.wait_ge(p_rms, 2 * i + s - 1)
                for t in range(NT):
                    src = bank[2 + 2 * s + t]
                    a(sq_junk[:, s, t, 0:QL], src[:, 0:QL], ACT.Square, accum_out=sumsq[:, s, 2 * t:2 * t + 1])
                    last = a(sq_junk[:, s, t, QL:QL + KL], src[:, QL:QL + KL], ACT.Square, accum_out=sumsq[:, s, 2 * t + 1:2 * t + 2])
                last.then_inc(p_sq, 1)

            def keep_rows(i, s):
                act.wait_ge(p_t, 2 * i + s + 1)
                cols = bass.ds((2 * i + s) * S, S)
                a(qn_t0[:, cols], bank[6][:, 0:S], ACT.Copy)
                a(qn_t1[0:KW1, cols], bank[6][0:KW1, S:2 * S], ACT.Copy)
                a(key_t[:, cols], bank[7][:, 0:S], ACT.Copy).then_inc(p_kept, 1)

            def two_batches(i, first=False, last=False):
                squares(i, 0, first)
                if not last:
                    modulated(i + 1, 0)
                    modulated(i + 1, 1)
                squares(i, 1, first)
                keep_rows(i, 0)
                keep_rows(i, 1)

            modulated(0, 0, True)
            modulated(0, 1, True)
            two_batches(0, first=True)
            with act.Fori(1, B // 2 - 1) as i:
                two_batches(i)
            two_batches(B // 2 - 1, last=True)
            leave(act, "scalar")

            enter(act, "scalar", 2)

            def round_q(b):
                if not isinstance(b, int) or b >= 1:
                    act.wait_ge(a_qgen, NP * b)
                a(q_hi0[:, :], qn_t0[:, bass.ds(b * S, S)], ACT.Copy)
                a(q_hi1[0:KW1, :], qn_t1[0:KW1, bass.ds(b * S, S)], ACT.Copy)
                a(q_hi1[KW1:P, :], qn_t1[0:KW1, bass.ds(b * S, S)], ACT.Copy).then_inc(q_hi_done, 1)

            def round_key(b):
                if not isinstance(b, int) or b >= 2:
                    act.wait_ge(a_score, 2 * NP * (b - 1))
                src, dst = bass.ds(b * S, S), bass.ds((b % 2) * S, S)
                a(key_hi[:, 0, dst], key_t[:, src], ACT.Copy)
                a(key_hi[0:64, 1, dst], key_t[64:128, src], ACT.Copy)
                a(key_hi[64:128, 1, dst], key_t[0:64, src], ACT.Copy).then_inc(k_hi_done, 1)

            def round_query(b, p):
                u = NP * b + p
                act.wait_ge(a_query, u + 1)
                if not isinstance(b, int) or u >= 2:
                    act.wait_ge(a_score, 2 * (u - 1))
                a(query_hi[:, p % 2, :], query[:, p % 2, :], ACT.Copy).then_inc(a_qhi, 1)

            def latent_rows(b, p):
                u = NP * b + p
                act.wait_ge(a_rot, u + 1)
                if not isinstance(b, int) or u >= 2:
                    act.wait_ge(a_qlo, u - 1)
                a(query[0:64, p % 2, 0:S], bank[0][0:64, 0:S], ACT.Copy)
                a(query[64:128, p % 2, S:2 * S], bank[0][64:128, 0:S], ACT.Copy).then_inc(a_latq, 1)

            def exps(b, p, j):
                u = NP * b + p
                if j == 0 and (not isinstance(b, int) or u >= 2):
                    act.wait_ge(a_ptr, 2 * (u - 1))
                    act.wait_ge(a_inv, u - 1)
                act.wait_ge(a_masked, 2 * u + j + 1)
                for t, c in enumerate((slice(0, P), slice(P, SCORE))):
                    n = 2 * j + t
                    last = a(probs[:, p % 2, j, c], scored[:, p % 2, j, c], ACT.Exp, scale=-1.0,
                             bias=row_min[:, p % 2, n:n + 1], accum_out=row_sum[:, p % 2, n:n + 1])
                last.then_inc(a_exp, 1)

            def keep_pt(b, p):
                u = NP * b + p
                act.wait_ge(a_ptr, 2 * u + 2)
                if not isinstance(b, int) or u >= 1:
                    act.wait_ge(a_pv, u)
                a(probs_t[:, 1, :], bank[4][:, 0:SCORE], ACT.Copy).then_inc(a_pt_b, 1)

            def round_o(b, p):
                u = NP * b + p
                act.wait_ge(a_otr, u + 1)
                if not isinstance(b, int) or u >= 1:
                    act.wait_ge(a_out, u)
                a(o_hi[:, :], bank[6][:, 0:256], ACT.Copy).then_inc(a_ohi, 1)

            def before(b, p, lag):
                return (b, p - lag) if p >= lag else (b - 1, p - lag + NP)

            def attention(b, first=False, last=False):
                for p in range(NP):
                    if not first or p >= 1:
                        keep_pt(*before(b, p, 1))
                    if p == NP - 2 and not last:
                        round_q(b + 1)
                    if p == NP - 3 and not last:
                        round_key(b + 1)
                    exps(b, p, 0)
                    if not first or p >= 2:
                        round_o(*before(b, p, 2))
                    if p + 1 < NP:
                        round_query(b, p + 1)
                    elif not last:
                        round_query(b + 1, 0)
                    exps(b, p, 1)
                    if p + 2 < NP:
                        latent_rows(b, p + 2)
                    elif not last:
                        latent_rows(b + 1, p + 2 - NP)

            round_q(0)
            round_key(0)
            latent_rows(0, 0)
            latent_rows(0, 1)
            round_query(0, 0)
            attention(0, first=True)
            with act.Fori(1, B - 1) as b:
                attention(b)
            attention(B - 1, last=True)
            keep_pt(B - 1, NP - 1)
            round_o(B - 1, NP - 2)
            round_o(B - 1, NP - 1)
            leave(act, "scalar")

            enter(act, "scalar", 3)
            act.wait_ge(ld_ffn[0], 16)
            a(w1_hi[:, :], w1_nat, ACT.Copy).then_inc(f_hi_w, 1)
            act.wait_ge(ld_ffn[1], 16)
            a(w2_hi[:, :], w2_nat, ACT.Copy).then_inc(f_hi_w, 1)

            def round_h(b, first=False):
                act.wait_ge(f_ht, b + 1)
                if not first:
                    act.wait_ge(f_up, (NF // 2) * b)
                a(h2_hi[:, :], bank[6][:, :], ACT.Copy).then_inc(f_hhi, 1)

            def gelus(b, first=False):
                if not first:
                    act.wait_ge(f_down, b)
                for g in range(NF // 2):
                    act.wait_ge(f_up, (NF // 2) * b + g + 1)
                    for j in range(2):
                        f = 2 * g + j
                        for dst in (act_hi, act_full):
                            last = a(dst[:, f * S:f * S + S], bank[g][:, j * S:j * S + S], ACT.Gelu_apprx_tanh, bias=b1_col[:, f:f + 1])
                    last.then_inc(f_act, 1)

            def router(b, slot):
                act.wait_ge(f_rout, b + 1)
                if not isinstance(b, int) or b >= 2:
                    act.wait_ge(f_mixed, b - 1)
                a(rout_t[:, slot, :], rout[:, slot, :], ACT.Tanh, bias=rb_col[:, 1:2], scale=0.5).then_inc(f_tanh, 1)

            router(0, 0)
            round_h(0, True)
            gelus(0, True)
            router(1, 1)
            round_h(1)
            with act.Fori(0, (B - 2) // 2) as i:
                for slot in range(2):
                    gelus(2 * i + 1 + slot)
                    router(2 * i + 2 + slot, slot)
                    round_h(2 * i + 2 + slot)
            gelus(B - 1)

        @block.gpsimd
        def _(pool):
            g = nc.gpsimd
            step = [0]

            def link(ins):
                step[0] += 1
                ins.then_inc(pool_step, 1)
                pool.wait_ge(pool_step, step[0])

            for j in range(2):
                pool.dma_start(kw_row[:, 64 * j:64 * j + 64], kv_norm_w.rearrange("(a n) -> a n", a=1).broadcast_to([P, KL])).then_inc(ld_kwr, 16)
            g.memset(half_neg[:, :], -0.5)
            g.memset(rms_eps[:, :], RMS_EPS)
            for t in range(NT):
                g.memset(inv_n[:, 2 * t:2 * t + 1], 1.0 / QL)
                g.memset(inv_n[:, 2 * t + 1:2 * t + 2], 1.0 / KL)
            link(g.memset(kw_row[:, P:2 * P], 1.0))
            pool.sem_inc(kwr_done, 1)
            pool.wait_ge(var_done, 1)
            g.tensor_tensor(tok_rstd[:, :], tok_var[:, :], half_neg[:, :], ALU.pow).then_inc(rstd_done, 1)
            for n in range(NP):
                pool.wait_ge(s_wq_hi, n + 1)
                w = slice(n * 256, n * 256 + 256)
                g.tensor_tensor(wq_lo0[:, w], wq_tmp0[:, n % 2, :], wq_hi0[:, w].bitcast(F32), ALU.subtract).then_inc(s_wq_lo0, 1)
            pool.wait_ge(s_wq_lo0, NP)
            leave(pool, "gpsimd")

            enter(pool, "gpsimd", 1)
            base = step[0]

            def rms(i, first=False):
                for s in range(2):
                    pool.wait_ge(p_sq, 2 * i + s + 1)
                    g.tensor_tensor(rms_mid[:, s, :], sumsq[:, s, :], inv_n[:, :], ALU.mult).then_inc(pool_step, 1)
                    pool.wait_ge(pool_step, 4 * i + base + 2 * s + 1)
                    g.tensor_tensor(rms_var[:, s, :], rms_mid[:, s, :], rms_eps[:, :], ALU.add).then_inc(pool_step, 1)
                    pool.wait_ge(pool_step, 4 * i + base + 2 * s + 2)
                    if not first:
                        pool.wait_ge(p_norm, 2 * i + s - 1)
                    g.tensor_tensor(rms_r[:, s, :], rms_var[:, s, :], half_neg[:, 0:2 * NT], ALU.pow).then_inc(p_rms, 1)

            rms(0, True)
            with pool.Fori(1, B // 2) as i:
                rms(i)
            step[0] += 4 * (B // 2)
            pool.wait_ge(p_rms, B)
            leave(pool, "gpsimd")

            enter(pool, "gpsimd", 2)
            base_u = step[0]

            def finish_rope(b, p):
                u = NP * b + p
                pool.wait_ge(a_rot, u + 1)
                pool.wait_ge(a_latq, u + 1)
                g.tensor_tensor(pe_rot[:, p % 2, :], pe_rot[:, p % 2, :], rope[:, S:2 * S], ALU.mult).then_inc(pool_step, 1)
                pool.wait_ge(pool_step, 2 * u + base_u + 1)
                g.tensor_tensor(query[0:64, p % 2, S:2 * S], pe_rot[0:64, p % 2, :], pe_cos[0:64, p % 2, :], ALU.add).then_inc(pool_step, 1)
                pool.wait_ge(pool_step, 2 * u + base_u + 2)
                g.tensor_tensor(query[64:128, p % 2, 0:S], pe_rot[64:128, p % 2, :], pe_cos[64:128, p % 2, :], ALU.add).then_inc(a_query, 1)
                pool.wait_ge(a_query, u + 1)

            def add_out(b):
                pool.wait_ge(a_gated, b + 1)
                rows = x_sb[:, bass.ds(b * NT * D, NT * D)]
                g.tensor_tensor(rows, rows, gated[:, :], ALU.add).then_inc(a_added, 1)
                pool.wait_ge(a_added, b + 1)

            def attention(b, first=False, last=False):
                for p in range(NP):
                    if p + 2 < NP:
                        finish_rope(b, p + 2)
                    elif not last:
                        finish_rope(b + 1, p + 2 - NP)
                    if p == 1 and not first:
                        add_out(b - 1)

            finish_rope(0, 0)
            finish_rope(0, 1)
            attention(0, first=True)
            with pool.Fori(1, B - 1) as b:
                attention(b)
            attention(B - 1, last=True)
            add_out(B - 1)
            leave(pool, "gpsimd")

            enter(pool, "gpsimd", 3)

            def rstd(b):
                pool.wait_ge(f_var_done, b + 1)
                g.tensor_tensor(f_rstd[:, :], f_var[:, :], half_neg[:, 0:NT], ALU.pow).then_inc(f_rstd_done, 1)

            def modulate(b, slot, nth):
                pool.wait_ge(ld_modh[slot], 16 * nth)
                pool.wait_ge(f_xhat, b + 1)
                for t in range(NT):
                    last = g.tensor_tensor(h2_m[:, t * D:t * D + D], h2_n[:, t * D:t * D + D], mod_h[:, slot, 0:D], ALU.mult)
                last.then_inc(f_scaled, 1)
                pool.wait_ge(f_scaled, b + 1)
                if not isinstance(b, int) or b >= 2:
                    pool.wait_ge(f_mixed, b - 1)
                for t in range(NT):
                    last = g.tensor_tensor(h2[:, slot, t * D:t * D + D], h2_m[:, t * D:t * D + D], mod_h[:, slot, D:2 * D], ALU.add)
                last.then_inc(f_h2, 1)
                pool.wait_ge(f_h2, b + 1)

            def finish(b, slot, before):
                pool.wait_ge(f_mixed, b + 1)
                pool.wait_ge(ld_modg[slot], 16 * (before + 1))
                if not isinstance(before, int) or before:
                    pool.wait_ge(stored[slot], 16 * before)
                for t in range(NT):
                    last = g.tensor_tensor(f_gate[:, t * D:t * D + D], f_mix[:, t * D:t * D + D], mod_g[:, slot, :], ALU.mult)
                last.then_inc(f_gated, 1)
                pool.wait_ge(f_gated, b + 1)
                g.tensor_tensor(f_out[:, slot, :], f_gate[:, :], x_sb[:, bass.ds(b * NT * D, NT * D)], ALU.add).then_inc(f_done, 1)
                pool.wait_ge(f_done, b + 1)

            def feed(i, slot, last=False):
                b = 2 * i + slot
                if not last:
                    rstd(b + 2)
                    modulate(b + 2, slot, i + 2)
                finish(b, slot, i)

            for b in range(2):
                rstd(b)
                modulate(b, b, 1)
            feed(0, 0)
            feed(0, 1)
            with pool.Fori(1, B // 2 - 1) as i:
                feed(i, 0)
                feed(i, 1)
            feed(B // 2 - 1, 0, last=True)
            feed(B // 2 - 1, 1, last=True)


INS = ['L0_attn_hidden_states', 'L0_attn_wq_a', 'L0_attn_q_norm_w', 'L0_attn_wq_b', 'L0_attn_wkv_a', 'L0_attn_kv_norm_w',
       'L0_attn_wkv_b', 'L0_attn_wo', 'L0_ffn_router_weight', 'L0_ffn_router_bias', 'L0_ffn_w1', 'L0_ffn_b1', 'L0_ffn_w2',
       'L0_ffn_b2', 'L0_c', 'L0_wmod']


def shape_constants():
    f = np.float32
    inv = (f(1.0) / np.power(f(10000.0), np.arange(0, DR, 2, dtype=f) / f(DR))).astype(f)
    angle = (np.arange(S, dtype=f)[:, None] * inv[None, :]).astype(f)
    cos, sin = np.cos(angle).astype(f), np.sin(angle).astype(f)
    tokens = np.concatenate([cos, cos, -sin, sin], axis=1)
    row = [(half, g * 16 + j) for half, g in RUNS for j in range(16)] * 2
    rows = np.stack([np.concatenate([cos[:, d], sin[:, d] if half else -sin[:, d]]) for half, d in row])
    masks = np.zeros((P, 2 * P), f)
    masks[:, P:] = np.where(np.tril(np.ones((P, P), bool)), f(0), f(MASKED))
    return {"ident": np.eye(P, dtype=f), "mask": masks, "rope_rows": rows.astype(f), "rope_tokens": tokens.astype(f)}


def kernel(**inputs):
    import concourse.bacc as _bacc
    from concourse.bass_utils import run_bass_kernel_spmd as _run

    nc = _bacc.Bacc("TRN2", target_bir_lowering=False, num_devices=1)
    arrays, args = {}, []
    given = {n: np.asarray(inputs[n]) for n in INS}
    given["L0_ffn_b1"] = given["L0_ffn_b1"].reshape(NF, P).T
    given = [(n, np.ascontiguousarray(a)) for n, a in given.items()] + list(shape_constants().items())
    for name, a in given:
        arrays[f"in_{name}"] = a
        args.append(nc.dram_tensor(f"in_{name}", a.shape, mybir.dt.from_np(a.dtype), kind="ExternalInput").ap())
    result = nc.dram_tensor("out_x", (B, S, D), F32, kind="ExternalOutput").ap()
    adaln_layer(nc, *args, result)
    return _run(nc, [arrays], core_ids=[0]).results[0]["out_x"]
```

```python
from contextlib import ExitStack

import numpy as np
import concourse.bass as bass
from concourse import mybir

F32 = mybir.dt.float32
F32R = mybir.dt.float32r
ACT = mybir.ActivationFunctionType
ALU = mybir.AluOpType

P = 128
B, S, D = 16, 256, 256
NH, QL, KL, DR, DN, DV = 16, 192, 64, 64, 128, 128
DFF = 1024
NT = S // P
KD = D // P
NP = NH // 2
WA = QL + KL + DR
KW1 = QL - P
SCORE = 3 * P
NF = DFF // P
SCALE = float(DN + DR) ** -0.5
LN_EPS, RMS_EPS = 1e-5, 1e-6
MASKED = -3.0e38
SWAP16 = [(i + 16) % 32 for i in range(32)]
RUNS = [(half, g) for g in range(2) for half in range(2)]


def adaln_layer(nc, x, wq_a, q_norm_w, wq_b, wkv_a, kv_norm_w, wkv_b, wo, router_w, router_b,
                w1, b1, w2, b2, c, wmod, ident_in, mask_in, rope_rows, rope_tokens, out):
    mod_rows = nc.dram_tensor("mod_rows", (B, 4 * D), F32, kind="Internal").ap()

    with ExitStack() as ctx:
        def sb(name, shape, dt=F32, own=ctx):
            return own.enter_context(nc.sbuf_tensor(name, shape, dt))

        def sem(name):
            return ctx.enter_context(nc.semaphore(name))

        bank = [ctx.enter_context(nc.psum_tensor(f"bank{i}", [P, 512], F32)) for i in range(8)]

        x_sb = sb("x_sb", [P, B * NT * D])
        ident = sb("ident", [P, P])
        mod_t = sb("mod_t", [P, 4 * B])
        bn_raw = sb("bn_raw", [P, B * NT, 6])
        tok_mean = sb("tok_mean", [P, B * NT])
        tok_gap = sb("tok_gap", [P, B * NT])
        tok_m2 = sb("tok_m2", [P, B * NT])
        tok_gap2 = sb("tok_gap2", [P, B * NT])
        tok_var = sb("tok_var", [P, B * NT])
        tok_rstd = sb("tok_rstd", [P, B * NT])
        tok_shift = sb("tok_shift", [P, B * NT])
        half_neg = sb("half_neg", [P, B * NT])
        spare = sb("spare", [P, 64])
        b1_col = sb("b1_col", [P, NF])
        b2_row = sb("b2_row", [P, D])
        rw_row = sb("rw_row", [P, D])
        rb_col = sb("rb_col", [P, 2])
        mod_h = sb("mod_h", [P, 2, 2 * D])
        mod_g = sb("mod_g", [P, 2, D])
        qn_t0 = sb("qn_t0", [P, B * S])

        wq_hi0 = sb("wq_hi0", [P, NP * 256], F32R)
        wq_lo0 = sb("wq_lo0", [P, NP * 256], F32R)
        wq_hl1 = sb("wq_hl1", [P, NP * 256], F32R)
        h2 = sb("h2", [P, 2, NT * D])
        h2_n = sb("h2_n", [P, NT * D])
        h2_m = sb("h2_m", [P, NT * D])
        f_bn = sb("f_bn", [P, NT, 6])
        f_stat = sb("f_stat", [P, NT, 2])
        f_var = sb("f_var", [P, NT])
        f_rstd = sb("f_rstd", [P, NT])
        f_shift = sb("f_shift", [P, NT])

        a_ctx = ExitStack()
        wout_hi = sb("wout_hi", [P, NP * D], F32R, a_ctx)
        wout_lo = sb("wout_lo", [P, NP * D], F32R, a_ctx)
        mask_pad = sb("mask_pad", [P, 2 * P], F32, a_ctx)
        rope = sb("rope", [P, 2 * S], F32, a_ctx)
        rope_tok = sb("rope_tok", [P, NT, 2 * DR], F32, a_ctx)
        inv_n = sb("inv_n", [P, 2 * NT], F32, a_ctx)
        rms_eps = sb("rms_eps", [P, 2 * NT], F32, a_ctx)
        qn_t1 = sb("qn_t1", [P, B * S], F32, a_ctx)
        key_t = sb("key_t", [P, B * S], F32, a_ctx)
        lat = sb("lat", [P, B * NT * KL], F32, a_ctx)

        w_ctx = ExitStack()
        wa_hi = sb("wa_hi", [P, KD * WA], F32R, w_ctx)
        wa_lo = sb("wa_lo", [P, KD * WA], F32R, w_ctx)

        s_ctx = ExitStack()
        wqa_nat = sb("wqa_nat", [P, 2, D], F32, s_ctx)
        wkva_nat = sb("wkva_nat", [P, D], F32, s_ctx)
        c_nat = sb("c_nat", [B, 4, D], F32, s_ctx)
        silu = sb("silu", [B, D], F32, s_ctx)
        silu_t = sb("silu_t", [P, KD * B], F32, s_ctx)
        mod_nat = sb("mod_nat", [B, 6 * D], F32, s_ctx)
        gate_sign = sb("gate_sign", [B, 2, 2 * D], F32, s_ctx)
        gate_abs = sb("gate_abs", [B, 2 * D], F32, s_ctx)
        mod_out = sb("mod_out", [B, 4 * D], F32, s_ctx)
        qw = sb("qw", [P, 2], F32, s_ctx)
        kw_row = sb("kw_row", [P, KL], F32, s_ctx)
        wkv_nat = sb("wkv_nat", [P, NH * 2, KL], F32, s_ctx)
        wo_t = sb("wo_t", [P, NH, D], F32, s_ctx)
        wqn_nat = qn_t0[:, 0:NH * QL].rearrange("p (h r) -> p h r", h=NH)
        wqp_nat = lat[:, 0:NP * QL].rearrange("p (h r) -> p h r", h=NP)
        wo_nat = key_t[:, :].rearrange("p (t n) -> p t n", t=2)
        wmod_nat = qn_t1[:, 0:KD * 6 * D].rearrange("p (k n) -> p k n", k=KD)
        s_ctx.close()

        p_ctx = ExitStack()
        xhat = sb("xhat", [P, 2, NT * D], F32, p_ctx)
        mod_col = sb("mod_col", [P, 2, 4], F32, p_ctx)
        h_t = sb("h_t", [P, 2, KD * S], F32, p_ctx)
        h_hi = sb("h_hi", [P, 2, KD * S], F32R, p_ctx)
        h_lo = sb("h_lo", [P, 2, KD * S], F32R, p_ctx)
        sq_junk = sb("sq_junk", [P, 2, NT, QL + KL], F32, p_ctx)
        sumsq = sb("sumsq", [P, 2, 2 * NT], F32, p_ctx)
        rms_mid = sb("rms_mid", [P, 2, 2 * NT], F32, p_ctx)
        rms_var = sb("rms_var", [P, 2, 2 * NT], F32, p_ctx)
        rms_r = sb("rms_r", [P, 2, 2 * NT], F32, p_ctx)
        qn = sb("qn", [P, 2, NT * QL], F32, p_ctx)
        keys = sb("keys", [P, 2, NT * P], F32, p_ctx)
        kr_cos = sb("kr_cos", [P, 2, NT * DR], F32, p_ctx)
        kr_sin = sb("kr_sin", [P, 2, NT * DR], F32, p_ctx)
        p_ctx.close()
        w_ctx.close()

        q_hi0 = sb("q_hi0", [P, S], F32R, a_ctx)
        q_lo0 = sb("q_lo0", [P, S], F32R, a_ctx)
        q_hi1 = sb("q_hi1", [P, S], F32R, a_ctx)
        q_lo1 = sb("q_lo1", [KW1, S], F32R, a_ctx)
        key_hi = sb("key_hi", [P, 2, 2 * S], F32R, a_ctx)
        key_lo = sb("key_lo", [P, 2, 2 * S], F32R, a_ctx)
        gate_a = sb("gate_a", [P, D], F32, a_ctx)
        query = sb("query", [P, 2, 2 * S], F32, a_ctx)
        query_hi = sb("query_hi", [P, 2, 2 * S], F32R, a_ctx)
        query_lo = sb("query_lo", [P, 2, 2 * S], F32R, a_ctx)
        pe_cos = sb("pe_cos", [P, 2, S], F32, a_ctx)
        pe_rot = sb("pe_rot", [P, 2, S], F32, a_ctx)
        scored = sb("scored", [P, 2, 2, SCORE], F32, a_ctx)
        row_min = sb("row_min", [P, 2, 4], F32, a_ctx)
        probs = sb("probs", [P, 2, 2, SCORE], F32, a_ctx)
        row_sum = sb("row_sum", [P, 2, 4], F32, a_ctx)
        row_inv = sb("row_inv", [P, 2, 4], F32, a_ctx)
        pt_hi = sb("pt_hi", [P, 2, SCORE], F32R, a_ctx)
        pt_lo = sb("pt_lo", [P, 2, SCORE], F32R, a_ctx)
        lat_hi = sb("lat_hi", [P, NT * KL], F32R, a_ctx)
        lat_lo = sb("lat_lo", [P, NT * KL], F32R, a_ctx)
        o_hi = sb("o_hi", [P, 256], F32R, a_ctx)
        o_lo = sb("o_lo", [P, 256], F32R, a_ctx)
        gated = sb("gated", [P, NT * D], F32, a_ctx)
        a_ctx.close()

        w1_nat = qn_t0[:, 0:KD * DFF]
        w2_nat = qn_t0[:, KD * DFF:KD * DFF + NF * D]
        w1_hi, w1_lo, w2_hi = wq_hi0, wq_lo0, wq_hl1
        w2_lo = sb("w2_lo", [P, NF * D], F32R)
        h2_hi = sb("h2_hi", [P, KD * S], F32R)
        h2_lo = sb("h2_lo", [P, KD * S], F32R)
        rout_junk = sb("rout_junk", [P, NT, D])
        rout = sb("rout", [P, 2, NT])
        rout_t = sb("rout_t", [P, 2, NT])
        rout_w = sb("rout_w", [P, 2, NT])
        act_hi = sb("act_hi", [P, NF * S], F32R)
        act_full = sb("act_full", [P, NF * S])
        act_lo = sb("act_lo", [P, NF * S], F32R)
        f_sum = sb("f_sum", [P, NT * D])
        f_mix = sb("f_mix", [P, NT * D])
        f_gate = sb("f_gate", [P, NT * D])
        f_out = sb("f_out", [P, 2, NT * D])

        ld_ident = sem("ld_ident")
        ld_small = sem("ld_small")
        ld_first = sem("ld_first")
        ld_mod = sem("ld_mod")
        ld_wo = sem("ld_wo")
        ld_heads = sem("ld_heads")
        ld_x = [sem(f"ld_x{n}") for n in range(4)]
        mod_stored = sem("mod_stored")
        ld_c = sem("ld_c")
        ld_kwr = sem("ld_kwr")
        kv_scaled = sem("kv_scaled")
        ld_kv = sem("ld_kv")
        exp_c = sem("exp_c")
        vec_step = sem("vec_step")
        pool_step = sem("pool_step")
        silu_done = sem("silu_done")
        s_wa_t = sem("s_wa_t")
        s_wa_hi = sem("s_wa_hi")
        s_silu_t = sem("s_silu_t")
        s_silu_sb = sem("s_silu_sb")
        s_mod = sem("s_mod")
        s_mod_sb = sem("s_mod_sb")
        mod_out_done = sem("mod_out_done")
        s_modt = sem("s_modt")
        mod_t_done = sem("mod_t_done")
        s_wo_t = sem("s_wo_t")
        s_wo_sb = sem("s_wo_sb")
        s_wout = sem("s_wout")
        s_wout_hi = sem("s_wout_hi")
        s_wout_free = sem("s_wout_free")
        s_wq = sem("s_wq")
        s_wq_hi = sem("s_wq_hi")
        s_wq_lo = sem("s_wq_lo")
        var_done = sem("var_done")
        rstd_done = sem("rstd_done")
        p_xhat = sem("p_xhat")
        p_ht = sem("p_ht")
        p_mod = sem("p_mod")
        p_hsb = sem("p_hsb")
        p_split = sem("p_split")
        p_proj = sem("p_proj")
        p_sq = sem("p_sq")
        p_rms = sem("p_rms")
        p_rows = sem("p_rows")
        p_norm = sem("p_norm")
        p_t = sem("p_t")
        p_kept = sem("p_kept")
        gate_loaded = sem("gate_loaded")
        q_hi_done = sem("q_hi_done")
        q_split = sem("q_split")
        a_qgen = sem("a_qgen")
        a_rot = sem("a_rot")
        a_latq = sem("a_latq")
        a_query = sem("a_query")
        a_qhi = sem("a_qhi")
        a_qlo = sem("a_qlo")
        k_hi_done = sem("k_hi_done")
        k_split = sem("k_split")
        a_score = sem("a_score")
        a_masked = sem("a_masked")
        a_exp = sem("a_exp")
        a_ptr = sem("a_ptr")
        a_pthi = sem("a_pthi")
        a_ptlo = sem("a_ptlo")
        l_hi_done = sem("l_hi_done")
        l_split = sem("l_split")
        a_norm = sem("a_norm")
        a_inv = sem("a_inv")
        a_pv = sem("a_pv")
        a_ohi = sem("a_ohi")
        a_olo = sem("a_olo")
        a_out = sem("a_out")
        a_gated = sem("a_gated")
        gated_free = sem("gated_free")
        ld_ffn = [sem("ld_w1"), sem("ld_w2")]
        ld_ffn_small = sem("ld_ffn_small")
        ld_modh = [sem("ld_modh_even"), sem("ld_modh_odd")]
        ld_modg = [sem("ld_modg_even"), sem("ld_modg_odd")]
        f_hi_w = sem("f_hi_w")
        f_w = sem("f_w")
        f_var_done = sem("f_var_done")
        f_rstd_done = sem("f_rstd_done")
        f_shifted = sem("f_shifted")
        f_xhat = sem("f_xhat")
        f_scaled = sem("f_scaled")
        f_h2 = sem("f_h2")
        f_rout = sem("f_rout")
        f_tanh = sem("f_tanh")
        f_summed = sem("f_summed")
        f_ht = sem("f_ht")
        f_hhi = sem("f_hhi")
        f_hsplit = sem("f_hsplit")
        f_up = sem("f_up")
        f_act = sem("f_act")
        f_lo = sem("f_lo")
        f_down = sem("f_down")
        f_mixed = sem("f_mixed")
        f_gated = sem("f_gated")
        f_done = sem("f_done")
        stored = [sem("stored_even"), sem("stored_odd")]
        left = {e: sem(f"left_{e}") for e in ("tensor", "vector", "scalar", "gpsimd", "sync")}

        def leave(eng, own):
            eng.sem_inc(left[own], 1)

        def enter(eng, own, n):
            for e, s in left.items():
                if e != own:
                    eng.wait_ge(s, n)

        def last_batches(b, n):
            return isinstance(b, int) and b + n >= B

        block = ctx.enter_context(nc.Block())

        @block.sync
        def _(sp):
            sp.dma_start(ident[:, :], ident_in).then_inc(ld_ident, 16)
            sp.dma_start(wqa_nat[:, 0, :], wq_a[0:P, :]).then_inc(ld_first, 16)
            sp.dma_start(wqa_nat[0:KW1, 1, :], wq_a[P:QL, :]).then_inc(ld_first, 16)
            sp.dma_start(wkva_nat[:, :], wkv_a).then_inc(ld_first, 16)
            x_rows = x.rearrange("b (t p) d -> p (b t) d", p=P)
            out_rows = out.rearrange("b (t p) d -> p (b t) d", p=P)
            x_tiles = x_sb[:, :].rearrange("p (n d) -> p n d", d=D)

            def load_x(i):
                n = B * NT // 4
                sp.dma_start(x_tiles[:, n * i:n * i + n, :], x_rows[:, n * i:n * i + n, :]).then_inc(ld_x[i], 16)

            sp.dma_start(wmod_nat, wmod.rearrange("(k p) n -> p k n", p=P)).then_inc(ld_mod, 16)
            heads = wq_b.rearrange("(h d) r -> d h r", d=DN + DR)
            sp.dma_start(wkv_nat[:, :, :], wkv_b.rearrange("(h d) c -> d h c", d=P)).then_inc(ld_kv, 16)
            sp.dma_start(wo_nat, wo.rearrange("(t p) n -> p t n", p=P)).then_inc(ld_wo, 16)
            sp.dma_start(wqn_nat, heads[0:DN, :, :]).then_inc(ld_heads, 16)
            by_pair = wq_b.rearrange("(g t d) r -> d t g r", t=2, d=DN + DR)
            for place, head in enumerate((1, 0)):
                for n, (half, g) in enumerate(RUNS):
                    row, d = place * DR + n * 16, DN + half * 32 + g * 16
                    sp.dma_start(wqp_nat[row:row + 16, :, :], by_pair[d:d + 16, head, :, :]).then_inc(ld_heads, 16)
            for i in range(4):
                load_x(i)
            sp.dma_start(b1_col[:, :], b1).then_inc(ld_ffn_small, 16)
            sp.dma_start(b2_row[:, :], b2.rearrange("(a n) -> a n", a=1).broadcast_to([P, D])).then_inc(ld_ffn_small, 16)
            sp.dma_start(rw_row[:, :], router_w.rearrange("(a n) -> a n", a=1).broadcast_to([P, D])).then_inc(ld_ffn_small, 16)
            sp.dma_start(rb_col[:, 0:1], router_b.rearrange("(a n) -> a n", a=1).broadcast_to([P, 1])).then_inc(ld_ffn_small, 16)
            sp.wait_ge(mod_out_done, 1)
            sp.dma_start(mod_rows, mod_out[:, :]).then_inc(mod_stored, 16)
            sp.wait_ge(mod_stored, 16)
            leave(sp, "sync")
            leave(sp, "sync")

            enter(sp, "sync", 2)
            sp.dma_start(gate_a[:, :], mod_rows[0:1, 0:D].broadcast_to([P, D])).then_inc(gate_loaded, 16)
            with sp.Fori(1, B) as b:
                sp.wait_ge(a_gated, b)
                sp.dma_start(gate_a[:, :], mod_rows[bass.ds(b, 1), 0:D].broadcast_to([P, D])).then_inc(gate_loaded, 16)

            leave(sp, "sync")

            sp.wait_ge(q_split, 2 * B)
            sp.dma_start(w1_nat.rearrange("p (k n) -> p k n", k=KD), w1.rearrange("(k p) n -> p k n", p=P)).then_inc(ld_ffn[0], 16)
            sp.dma_start(w2_nat.rearrange("p (k n) -> p k n", k=NF), w2.rearrange("(k p) n -> p k n", p=P)).then_inc(ld_ffn[1], 16)

            def load_h(b, slot):
                sp.dma_start(mod_h[:, slot, :], mod_rows[bass.ds(b, 1), D:3 * D].broadcast_to([P, 2 * D])).then_inc(ld_modh[slot], 16)

            def load_g(b, slot):
                sp.dma_start(mod_g[:, slot, :], mod_rows[bass.ds(b, 1), 3 * D:4 * D].broadcast_to([P, D])).then_inc(ld_modg[slot], 16)

            def next_h(b, slot):
                sp.wait_ge(f_h2, b + 1)
                load_h(b + 2, slot)

            def next_g(b, slot):
                sp.wait_ge(f_gated, b + 1)
                load_g(b + 2, slot)

            def store(b, slot):
                sp.wait_ge(f_done, b + 1)
                sp.dma_start(out_rows[:, bass.ds(b * NT, NT), :],
                             f_out[:, slot, :].rearrange("p (t d) -> p t d", d=D)).then_inc(stored[slot], 16)

            for slot in range(2):
                load_h(slot, slot)
                load_g(slot, slot)
            next_h(0, 0)
            with sp.Fori(0, B // 2 - 2) as i:
                for slot in range(2):
                    next_h(2 * i + slot + 1, 1 - slot)
                    next_g(2 * i + slot, slot)
                    store(2 * i + slot, slot)
            next_h(B - 3, 1)
            for b in range(B - 4, B):
                if b < B - 2:
                    next_g(b, b % 2)
                store(b, b % 2)
            for slot in range(2):
                sp.wait_ge(stored[slot], 16 * (B // 2))

        @block.tensor
        def _(pe):
            mm = nc.tensor.matmul

            def three(out_ap, left_hl, right_hl, start, stop, **kw):
                (lh, ll), (rh, rl) = left_hl, right_hl
                mm(out_ap, lh, rh, start=start, stop=False, **kw)
                mm(out_ap, ll, rh, start=False, stop=False, **kw)
                return mm(out_ap, lh, rl, start=False, stop=stop, **kw)

            pe.wait_ge(ld_ident, 16)
            pe.wait_ge(ld_first, 48)
            for k in range(KD):
                cols = slice(k * P, k * P + P)
                nc.tensor.transpose(bank[k][:, 0:P], wqa_nat[:, 0, cols], ident[:, :])
                nc.tensor.transpose(bank[k][:, P:QL], wqa_nat[0:KW1, 1, cols], ident[0:KW1, 0:KW1])
                nc.tensor.transpose(bank[k][:, QL:WA], wkva_nat[:, cols], ident[:, :]).then_inc(s_wa_t, 1)
            pe.wait_ge(silu_done, 1)
            for k in range(KD):
                last = nc.tensor.transpose(bank[2][:, k * B:k * B + B], silu[:, k * P:k * P + P], ident[0:B, 0:B])
            last.then_inc(s_silu_t, 1)
            pe.wait_ge(s_silu_sb, 1)
            pe.wait_ge(ld_mod, 16)
            for n in range(3):
                for k in range(KD):
                    last = mm(bank[5 + n][0:B, :], silu_t[:, k * B:k * B + B], wmod_nat[:, k, n * 512:n * 512 + 512],
                              start=(k == 0), stop=(k == KD - 1))
            last.then_inc(s_mod, 1)
            pe.wait_ge(s_mod_sb, 1)
            for n in range(4):
                last = nc.tensor.transpose(bank[2][:, n * B:n * B + B], mod_nat[:, n * P:n * P + P], ident[0:B, 0:B])
            last.then_inc(s_modt, 1)
            pe.wait_ge(ld_wo, 16)
            pe.wait_ge(s_wa_hi, 2)
            for n in range(NP):
                if n >= 2:
                    pe.wait_ge(s_wo_sb, n - 1)
                for j in range(4):
                    h, t = 2 * n + j // 2, j % 2
                    last = nc.tensor.transpose(bank[n % 2][:, j * P:j * P + P], wo_nat[:, t, h * P:h * P + P], ident[:, :])
                last.then_inc(s_wo_t, 1)
            pe.wait_ge(ld_heads, 16 * 9)
            pe.wait_ge(kv_scaled, 1)
            for n in range(NP):
                pe.wait_ge(s_wo_sb, n + 1)
                if n == 0:
                    pe.wait_ge(mod_t_done, 1)
                if n >= 2:
                    pe.wait_ge(s_wout_free, n - 1)
                for j in range(2):
                    h = 2 * n + j
                    last = mm(bank[2 + n % 2][64 * j:64 * j + 64, 0:D], wkv_nat[:, 2 * h + 1, :], wo_t[:, h, :], start=True, stop=True)
                last.then_inc(s_wout, 1)
                if n >= 2:
                    pe.wait_ge(s_wq_lo, n - 1)
                q = bank[4 + n % 2]
                for j in range(2):
                    h = 2 * n + j
                    mm(q[:, j * 64:j * 64 + 64], wqn_nat[:, h, 0:P], wkv_nat[:, 2 * h, :], start=True, stop=True)
                    mm(q[0:KW1, 256 + j * 64:320 + j * 64], wqn_nat[:, h, P:QL], wkv_nat[:, 2 * h, :], start=True, stop=True)
                nc.tensor.transpose(q[:, P:2 * P], wqp_nat[:, n, 0:P], ident[:, :])
                nc.tensor.transpose(q[0:KW1, 3 * P:4 * P], wqp_nat[:, n, P:QL], ident[:, :]).then_inc(s_wq, 1)
            leave(pe, "tensor")

            enter(pe, "tensor", 1)

            def later(b, n):
                return not isinstance(b, int) or b >= n

            def turn_x(b, s):
                pe.wait_ge(p_xhat, b + 1)
                if later(b, 2):
                    pe.wait_ge(p_hsb, b - 1)
                for k in range(KD):
                    for t in range(NT):
                        last = nc.tensor.transpose(bank[s][:, k * S + t * P:k * S + t * P + P],
                                                   xhat[:, s, t * D + k * P:t * D + k * P + P], ident[:, :])
                last.then_inc(p_ht, 1)

            def project_x(b, s):
                pe.wait_ge(p_split, b + 1)
                if later(b, 2):
                    pe.wait_ge(p_rows, b - 1)
                for t in range(NT):
                    for k in range(KD):
                        c0 = k * S + t * P
                        last = three(bank[2 + 2 * s + t][:, 0:WA], (h_hi[:, s, c0:c0 + P], h_lo[:, s, c0:c0 + P]),
                                     (wa_hi[:, k * WA:k * WA + WA], wa_lo[:, k * WA:k * WA + WA]), k == 0, k == KD - 1)
                last.then_inc(p_proj, 1)

            def turn_rows(b, s):
                pe.wait_ge(p_norm, b + 1)
                if later(b, 1):
                    pe.wait_ge(p_kept, b)
                for t in range(NT):
                    c0 = t * P
                    nc.tensor.transpose(bank[6][:, c0:c0 + P], qn[:, s, t * QL:t * QL + P], ident[:, :])
                    nc.tensor.transpose(bank[6][0:KW1, S + c0:S + c0 + P], qn[:, s, t * QL + P:t * QL + QL], ident[:, :])
                    last = nc.tensor.transpose(bank[7][:, c0:c0 + P], keys[:, s, t * P:t * P + P], ident[:, :])
                last.then_inc(p_t, 1)

            def two_batches(i):
                for s in range(2):
                    b = 2 * i + s
                    if not last_batches(b, 2):
                        turn_x(b + 2, s)
                    if not last_batches(b, 1):
                        project_x(b + 1, 1 - s)
                    if later(b, 1):
                        turn_rows(b - 1, 1 - s)

            turn_x(0, 0)
            turn_x(1, 1)
            project_x(0, 0)
            two_batches(0)
            with pe.Fori(1, B // 2 - 2) as i:
                two_batches(i)
            two_batches(B // 2 - 2)
            two_batches(B // 2 - 1)
            turn_rows(B - 1, 1)
            leave(pe, "tensor")

            enter(pe, "tensor", 2)

            def queries(b, p):
                if p == 0:
                    pe.wait_ge(q_hi_done, 2 * (b + 1))
                if later(b, 1) or p >= 2:
                    pe.wait_ge(a_latq, NP * b + p - 1)
                w = [slice(p * 256 + tile * P, p * 256 + tile * P + P) for tile in range(2)]
                dst = [bank[(0, 6)[p % 2]][:, tile * S:tile * S + S] for tile in range(2)]
                for tile in range(2):
                    mm(dst[tile], wq_hi0[:, w[tile]], q_hi0[:, :], start=(tile == 0), stop=False, skip_group_check=True)
                    mm(dst[tile], wq_lo0[:, w[tile]], q_hi0[:, :], start=False, stop=False, skip_group_check=True)
                    mm(dst[tile], wq_hl1[:, w[tile]], q_hi1[:, :], start=False, stop=False, skip_group_check=True)
                if p == 0:
                    pe.wait_ge(q_split, 2 * (b + 1))
                for tile in range(2):
                    mm(dst[tile], wq_hi0[:, w[tile]], q_lo0[:, :], start=False, stop=False, skip_group_check=True)
                    last = mm(dst[tile], wq_hl1[0:KW1, w[tile]], q_lo1[:, :], start=False, stop=True, skip_group_check=True)
                last.then_inc(a_qgen, 1)

            def scores(b, p, first=False):
                u = NP * b + p
                pe.wait_ge(a_qhi, u + 1)
                if p == 0:
                    pe.wait_ge(k_split, 3 * (b + 1))
                if not first:
                    pe.wait_ge(a_masked, 2 * u)
                for j in range(2):
                    part = []
                    for q0, n in ((0, P), (P, S)):
                        part.append((bank[1 + j][:, q0:q0 + n], slice(j * S + q0, j * S + q0 + P), bass.ds((b % 2) * S, n)))
                    for t, (dst, qs, ks) in enumerate(part):
                        mm(dst, query_hi[:, p % 2, qs], key_hi[:, j, ks], start=(t == 0), stop=False, skip_group_check=True)
                        mm(dst, query_hi[:, p % 2, qs], key_lo[:, j, ks], start=False, stop=False, skip_group_check=True)
                    if j == 0:
                        pe.wait_ge(a_qlo, u + 1)
                    for dst, qs, ks in part:
                        last = mm(dst, query_lo[:, p % 2, qs], key_hi[:, j, ks], start=False, stop=True, skip_group_check=True)
                    last.then_inc(a_score, 1)

            def turn_probs(b, p):
                u = NP * b + p
                pe.wait_ge(a_norm, u + 1)
                if later(b, 1) or p >= 1:
                    pe.wait_ge(a_ptlo, 2 * u)
                for j in range(2):
                    for n in range(3):
                        last = nc.tensor.transpose(bank[3 + j][:, n * P:n * P + P], probs[:, p % 2, j, n * P:n * P + P], ident[:, :])
                    last.then_inc(a_ptr, 1)

            def weigh(b, p):
                u = NP * b + p
                if p == 0:
                    pe.wait_ge(l_split, b + 1)
                if later(b, 1) or p >= 1:
                    pe.wait_ge(a_olo, u)
                pe.wait_ge(a_pthi, 2 * (u + 1))
                part = []
                for k, (c0, n) in enumerate(((0, S), (S, P))):
                    part.append((bank[5][0:KL, :].rearrange("p (h q) -> p h q", h=2)[:, :, S - n:S],
                                 slice(k * KL, k * KL + KL), slice(c0, c0 + n)))
                for k, (dst, l, c) in enumerate(part):
                    mm(dst, lat_hi[:, l], pt_hi[:, :, c], start=(k == 0), stop=False, skip_group_check=True)
                    mm(dst, lat_lo[:, l], pt_hi[:, :, c], start=False, stop=False, skip_group_check=True)
                pe.wait_ge(a_ptlo, 2 * (u + 1))
                for dst, l, c in part:
                    last = mm(dst, lat_hi[:, l], pt_lo[:, :, c], start=False, stop=True, skip_group_check=True)
                last.then_inc(a_pv, 1)

            def project(b, p, first=False):
                u = NP * b + p
                pe.wait_ge(a_ohi, u + 1)
                if p == 0 and not first:
                    pe.wait_ge(a_gated, b)
                w = slice(p * D, p * D + D)
                for t in range(NT):
                    dst, rows = bank[7][:, t * D:t * D + D], slice(t * P, t * P + P)
                    mm(dst, o_hi[:, rows], wout_hi[:, w], start=(p == 0 and t == 0), stop=False, skip_group_check=True)
                    mm(dst, o_hi[:, rows], wout_lo[:, w], start=False, stop=False, skip_group_check=True)
                pe.wait_ge(a_olo, u + 1)
                for t in range(NT):
                    last = mm(bank[7][:, t * D:t * D + D], o_lo[:, t * P:t * P + P], wout_hi[:, w], start=False,
                              stop=(p == NP - 1), skip_group_check=True)
                last.then_inc(a_out, 1)

            def before(b, p, lag):
                return (b, p - lag) if p >= lag else (b - 1, p - lag + NP)

            def attention(b, first=False, last=False):
                for p in range(NP):
                    scores(b, p, first and p == 0)
                    if not first or p >= 2:
                        turn_probs(*before(b, p, 2))
                    if p + 2 < NP:
                        queries(b, p + 2)
                    elif not last:
                        queries(b + 1, p + 2 - NP)
                    if not first or p >= 3:
                        project(*before(b, p, 3), first and p == 3)
                    if not first or p >= 2:
                        weigh(*before(b, p, 2))

            queries(0, 0)
            queries(0, 1)
            attention(0, first=True)
            with pe.Fori(1, B - 1) as b:
                attention(b)
            attention(B - 1, last=True)
            for p in (NP - 2, NP - 1):
                turn_probs(B - 1, p)
                project(B - 1, p - 1)
                weigh(B - 1, p)
            project(B - 1, NP - 1)
            leave(pe, "tensor")

            enter(pe, "tensor", 3)

            def turn_h(b, slot):
                pe.wait_ge(f_h2, b + 1)
                for k in range(KD):
                    for t in range(NT):
                        last = nc.tensor.transpose(bank[6][:, k * S + t * P:k * S + t * P + P],
                                                   h2[:, slot, t * D + k * P:t * D + k * P + P], ident[:, :])
                last.then_inc(f_ht, 1)

            def up(b, first=False):
                pe.wait_ge(f_hsplit, b + 1)
                for g in range(NF // 2):
                    if not first:
                        pe.wait_ge(f_act, (b - 1) * (NF // 2) + g + 1)
                    for j in range(2):
                        f = 2 * g + j
                        for k in range(KD):
                            w = slice(k * DFF + f * P, k * DFF + f * P + P)
                            last = three(bank[g][:, j * S:j * S + S], (w1_hi[:, w], w1_lo[:, w]),
                                         (h2_hi[:, k * S:k * S + S], h2_lo[:, k * S:k * S + S]), k == 0, k == KD - 1)
                    last.then_inc(f_up, 1)

            def down(b, slot, first=False, last=False):
                if not first:
                    pe.wait_ge(f_summed, b)
                for g in range(NF // 2):
                    pe.wait_ge(f_lo, (NF // 2) * b + g + 1)
                    for f in (2 * g, 2 * g + 1):
                        for t in range(NT):
                            a = slice(f * S + t * P, f * S + t * P + P)
                            done = three(bank[4 + t][:, 0:D], (act_hi[:, a], act_lo[:, a]),
                                         (w2_hi[:, f * D:f * D + D], w2_lo[:, f * D:f * D + D]), f == 0, f == NF - 1)
                    if g == 1 and not last:
                        turn_h(b + 1, 1 - slot)
                done.then_inc(f_down, 1)

            turn_h(0, 0)
            pe.wait_ge(f_w, 1)
            up(0, True)
            pe.wait_ge(f_w, 2)
            down(0, 0, first=True)
            with pe.Fori(0, (B - 2) // 2) as i:
                for slot in range(2):
                    up(2 * i + 1 + slot)
                    down(2 * i + 1 + slot, 1 - slot)
            up(B - 1)
            down(B - 1, 1, last=True)

        @block.vector
        def _(dve):
            v = nc.vector
            step = [0]
            carried = [0]

            def link(ins):
                step[0] += 1
                ins.then_inc(vec_step, 1)
                dve.wait_ge(vec_step, step[0])

            def carry_wait():
                carried[0] = (carried[0] + 1) % 64
                v.memset(spare[:, carried[0]:carried[0] + 1], 0.0)

            dve.wait_ge(exp_c, 1)
            link(v.tensor_scalar_add(c_nat[:, 2, :], c_nat[:, 1, :], 1.0))
            link(v.reciprocal(c_nat[:, 3, :], c_nat[:, 2, :]))
            v.tensor_tensor(silu[:, :], c_nat[:, 0, :], c_nat[:, 3, :], ALU.mult).then_inc(silu_done, 1)

            def statistics(i):
                dve.wait_ge(ld_x[i], 16)
                for n in range(B * NT // 4 * i, B * NT // 4 * (i + 1)):
                    last = v.bn_stats(bn_raw[:, n, :], x_sb[:, n * D:n * D + D])
                return last

            for k in range(KD):
                dve.wait_ge(s_wa_hi, k + 1)
                w = slice(k * WA, k * WA + WA)
                v.tensor_tensor(wa_lo[:, w], bank[k][:, 0:WA], wa_hi[:, w].bitcast(F32), ALU.subtract)
            dve.wait_ge(s_silu_t, 1)
            v.tensor_copy(silu_t[:, :], bank[2][:, 0:KD * B]).then_inc(s_silu_sb, 1)
            def moments(q):
                c = slice(q * B // 2, (q + 1) * B // 2)
                even, odd = bn_raw[:, c, 0:3], bn_raw[:, c, 3:6]
                v.tensor_tensor(tok_mean[:, c], even[:, :, 1], odd[:, :, 1], ALU.add)
                v.tensor_tensor(tok_gap[:, c], even[:, :, 1], odd[:, :, 1], ALU.subtract)
                link(v.tensor_tensor(tok_m2[:, c], even[:, :, 2], odd[:, :, 2], ALU.add))
                link(v.scalar_tensor_tensor(out=tok_gap2[:, c], in0=tok_gap[:, c], scalar=0.25, in1=tok_gap[:, c],
                                            op0=ALU.mult, op1=ALU.mult))
                link(v.scalar_tensor_tensor(out=tok_shift[:, c], in0=tok_m2[:, c], scalar=1.0 / D, in1=tok_gap2[:, c],
                                            op0=ALU.mult, op1=ALU.add))
                v.tensor_scalar_add(tok_var[:, c], tok_shift[:, c], LN_EPS).then_inc(var_done, 1)

            def shift(q):
                c = slice(q * B // 2, (q + 1) * B // 2)
                dve.wait_ge(rstd_done, q + 1)
                link(v.scalar_tensor_tensor(out=tok_shift[:, c], in0=tok_mean[:, c], scalar=-0.5, in1=tok_rstd[:, c],
                                            op0=ALU.mult, op1=ALU.mult))

            dve.wait_ge(s_mod, 1)
            for n in range(3):
                last = v.tensor_copy(mod_nat[:, n * 512:n * 512 + 512], bank[5 + n][0:B, :])
            last.then_inc(s_mod_sb, 1)
            dve.wait_ge(s_mod_sb, 1)
            dve.wait_ge(s_modt, 1)
            v.tensor_copy(mod_t[:, 0:2 * B], bank[2][:, 0:2 * B])
            v.tensor_scalar_add(mod_t[:, 2 * B:4 * B], bank[2][:, 2 * B:4 * B], 1.0).then_inc(mod_t_done, 1)
            for n, part in enumerate((2, 5)):
                g = mod_nat[:, part * D:part * D + D]
                v.tensor_scalar(gate_sign[:, 0, n * D:n * D + D], g, 0.0, 2.0, ALU.is_ge, ALU.mult)
                last = v.scalar_tensor_tensor(out=gate_sign[:, 1, n * D:n * D + D], in0=g, scalar=-1.0, in1=g,
                                              op0=ALU.mult, op1=ALU.max)
            link(last)
            link(v.tensor_scalar_max(gate_abs[:, :], gate_sign[:, 1, :], 0.25))
            for n, part in enumerate((0, 3)):
                v.scalar_tensor_tensor(out=mod_out[:, part * D:part * D + D], in0=gate_sign[:, 0, n * D:n * D + D],
                                       scalar=-1.0, in1=gate_abs[:, n * D:n * D + D], op0=ALU.add, op1=ALU.mult)
            v.tensor_scalar_add(mod_out[:, D:2 * D], mod_nat[:, 4 * D:5 * D], 1.0)
            v.tensor_copy(mod_out[:, 2 * D:3 * D], mod_nat[:, 3 * D:4 * D]).then_inc(mod_out_done, 1)
            dve.wait_ge(ld_small, 16 * 5)
            for n in range(NP):
                dve.wait_ge(s_wout_hi, n + 1)
                w = slice(n * D, n * D + D)
                v.tensor_tensor(wout_lo[:, w], bank[2 + n % 2][:, 0:D], wout_hi[:, w].bitcast(F32),
                                ALU.subtract).then_inc(s_wout_free, 1)
                dve.wait_ge(s_wq_hi, n + 1)
                q, w = bank[4 + n % 2], slice(n * 256, n * 256 + 256)
                v.scalar_tensor_tensor(out=wq_lo0[:, w], in0=q[:, 0:256], scalar=qw[:, 0:1], in1=wq_hi0[:, w].bitcast(F32),
                                       op0=ALU.mult, op1=ALU.subtract)
                v.scalar_tensor_tensor(out=wq_hl1[KW1:P, w], in0=q[0:KW1, 256:512], scalar=qw[0:KW1, 1:2],
                                       in1=wq_hl1[0:KW1, w].bitcast(F32), op0=ALU.mult, op1=ALU.subtract).then_inc(s_wq_lo, 1)
                if n == 4:
                    link(statistics(0))
                    moments(0)
            shift(0)
            leave(dve, "vector")

            enter(dve, "vector", 1)

            def normed(b, s):
                if not isinstance(b, int) or b >= 2:
                    dve.wait_ge(p_ht, b - 1)
                for t in range(NT):
                    g = b * NT + t
                    last = v.tensor_scalar(xhat[:, s, t * D:t * D + D], x_sb[:, bass.ds(g * D, D)],
                                           tok_rstd[:, bass.ds(g, 1)], tok_shift[:, bass.ds(g, 1)], ALU.mult, ALU.add)
                last.then_inc(p_xhat, 1)
                if not isinstance(b, int) or b >= 2:
                    dve.wait_ge(p_hsb, b - 1)
                v.tensor_copy(mod_col[:, s, :], mod_t[:, :].rearrange("p (n b) -> p n b", b=B)[:, :, bass.ds(b, 1)]
                              .rearrange("p n a -> p (n a)")).then_inc(p_mod, 1)

            def split_x(b, s):
                dve.wait_ge(p_hsb, b + 1)
                if not isinstance(b, int) or b >= 2:
                    dve.wait_ge(p_proj, b - 1)
                v.tensor_tensor(h_lo[:, s, :], h_t[:, s, :], h_hi[:, s, :].bitcast(F32), ALU.subtract).then_inc(p_split, 1)

            def rows(b, s):
                dve.wait_ge(p_rms, b + 1)
                if not isinstance(b, int) or b >= 2:
                    dve.wait_ge(p_t, b - 1)
                for t in range(NT):
                    src = bank[2 + 2 * s + t]
                    rq, rk = rms_r[:, s, 2 * t:2 * t + 1], rms_r[:, s, 2 * t + 1:2 * t + 2]
                    v.tensor_scalar(qn[:, s, t * QL:t * QL + QL], src[:, 0:QL], rq, None, ALU.mult)
                    v.tensor_scalar(keys[:, s, t * P:t * P + KL], src[:, QL:QL + KL], rk, None, ALU.mult)
                    r0, r1, r2 = QL + KL, QL + KL + DR // 2, WA
                    v.tensor_tensor(kr_cos[:, s, t * DR:t * DR + DR], src[:, r0:r2], rope_tok[:, t, 0:DR], ALU.mult)
                    v.tensor_tensor(kr_sin[:, s, t * DR:t * DR + DR // 2], src[:, r1:r2], rope_tok[:, t, DR:DR + DR // 2], ALU.mult)
                    last = v.tensor_tensor(kr_sin[:, s, t * DR + DR // 2:t * DR + DR], src[:, r0:r1],
                                           rope_tok[:, t, DR + DR // 2:2 * DR], ALU.mult)
                last.then_inc(p_rows, 1)

            def two_batches(i):
                for s in range(2):
                    b = 2 * i + s
                    if not last_batches(b, 3):
                        normed(b + 3, 1 - s)
                    rows(b, s)
                    if not last_batches(b, 2):
                        split_x(b + 2, s)

            normed(0, 0)
            normed(1, 1)
            link(statistics(1))
            moments(1)
            split_x(0, 0)
            split_x(1, 1)
            normed(2, 0)
            shift(1)
            two_batches(0)
            link(statistics(2))
            moments(2)
            two_batches(1)
            shift(2)
            link(statistics(3))
            moments(3)
            two_batches(2)
            shift(3)
            with dve.Fori(3, B // 2 - 2) as i:
                two_batches(i)
            two_batches(B // 2 - 2)
            two_batches(B // 2 - 1)
            leave(dve, "vector")

            enter(dve, "vector", 2)

            def split_key(b, part):
                dve.wait_ge(k_hi_done, 3 * b + part + 1)
                src, dst, lo, hi = key_t[:, bass.ds(b * S, S)], bass.ds((b % 2) * S, S), slice(0, 64), slice(64, P)
                rounded = key_hi[:, 0, :].bitcast(F32)
                to, full, less = ((key_lo[:, 0, dst], src, rounded[:, dst]),
                                  (key_lo[lo, 1, dst], src[hi, :], rounded[hi, dst]),
                                  (key_lo[hi, 1, dst], src[lo, :], rounded[lo, dst]))[part]
                v.tensor_tensor(to, full, less, ALU.subtract).then_inc(k_split, 1)

            def split_query(b, p):
                dve.wait_ge(a_qhi, NP * b + p + 1)
                v.tensor_tensor(query_lo[:, p % 2, :], query[:, p % 2, :], query_hi[:, p % 2, :].bitcast(F32),
                                ALU.subtract).then_inc(a_qlo, 1)


            def split_q(b, part):
                dve.wait_ge(q_hi_done, 2 * b + part + 1)
                to, full, rounded = ((q_lo0[:, :], qn_t0[:, bass.ds(b * S, S)], q_hi0[:, :]),
                                     (q_lo1[:, :], qn_t1[0:KW1, bass.ds(b * S, S)], q_hi1[0:KW1, :]))[part]
                v.tensor_tensor(to, full, rounded.bitcast(F32), ALU.subtract).then_inc(q_split, 1)

            def masked(b, p):
                u = NP * b + p
                if not isinstance(b, int) or u >= 2:
                    dve.wait_ge(a_exp, 2 * (u - 1))
                for j in range(2):
                    dve.wait_ge(a_score, 2 * u + j + 1)
                    carry_wait()
                    s, o, m = bank[1 + j], scored[:, p % 2, j, :], row_min[:, p % 2, :]
                    v.tensor_tensor_reduce(out=o[:, 0:P], in0=s[:, 0:P], in1=mask_pad[:, P:2 * P], scale=-SCALE, scalar=3.0e38,
                                           op0=ALU.add, op1=ALU.min, accum_out=m[:, 2 * j:2 * j + 1])
                    v.tensor_tensor_reduce(out=o[:, P:SCORE], in0=s[:, P:SCORE], in1=mask_pad[:, :], scale=-SCALE, scalar=3.0e38,
                                           op0=ALU.add, op1=ALU.min, accum_out=m[:, 2 * j + 1:2 * j + 2]).then_inc(a_masked, 1)

            def rotate(b, p):
                u = NP * b + p
                dve.wait_ge(a_qgen, u + 1)
                if not isinstance(b, int) or u >= 2:
                    dve.wait_ge(a_query, u - 1)
                src = bank[(0, 6)[p % 2]][:, S:2 * S]
                v.tensor_tensor(pe_cos[:, p % 2, :], src, rope[:, 0:S], ALU.mult)
                v.stream_shuffle(pe_rot[:, p % 2, :], src, SWAP16).then_inc(a_rot, 1)

            def split_pt(b, p):
                for j in range(2):
                    dve.wait_ge(a_pthi, 2 * (NP * b + p) + j + 1)
                    v.tensor_tensor(pt_lo[:, j, :], bank[3 + j][:, 0:SCORE], pt_hi[:, j, :].bitcast(F32),
                                    ALU.subtract).then_inc(a_ptlo, 1)

            def split_latent(b):
                dve.wait_ge(l_hi_done, b + 1)
                v.tensor_tensor(lat_lo[:, :], lat[:, bass.ds(b * NT * KL, NT * KL)], lat_hi[:, :].bitcast(F32),
                                ALU.subtract).then_inc(l_split, 1)

            def invert(b, p):
                u = NP * b + p
                dve.wait_ge(a_exp, 2 * (u + 1))
                if not isinstance(b, int) or u >= 2:
                    dve.wait_ge(a_norm, u - 1)
                v.reciprocal(row_inv[:, p % 2, :], row_sum[:, p % 2, :]).then_inc(a_inv, 1)

            def split_o(b, p):
                u = NP * b + p
                dve.wait_ge(a_ohi, u + 1)
                v.tensor_tensor(o_lo[0:64, :], bank[5][0:64, 0:S], o_hi[0:64, :].bitcast(F32), ALU.subtract)
                v.tensor_tensor(o_lo[64:128, :], bank[5][0:64, S:2 * S], o_hi[64:128, :].bitcast(F32), ALU.subtract).then_inc(a_olo, 1)

            def gate(b, t):
                if t == 0:
                    dve.wait_ge(a_out, NP * (b + 1))
                    dve.wait_ge(gate_loaded, 16 * (b + 1))
                    dve.wait_ge(gated_free, b + 1)
                last = v.tensor_tensor(gated[:, t * D:t * D + D], bank[7][:, t * D:t * D + D], gate_a[:, :], ALU.mult)
                if t == NT - 1:
                    last.then_inc(a_gated, 1)

            def before(b, p, lag):
                return (b, p - lag) if p >= lag else (b - 1, p - lag + NP)

            def attention(b, first=False, last=False):
                for p in range(NP):
                    masked(b, p)
                    if not first or p >= 1:
                        invert(*before(b, p, 1))
                    if p == 3 and not first:
                        gate(b - 1, 1)
                    if not first or p >= 3:
                        split_o(*before(b, p, 3))
                    if p == 2 and not first:
                        split_latent(b)
                    if not first or p >= 2:
                        split_pt(*before(b, p, 2))
                    if p + 1 < NP:
                        split_query(b, p + 1)
                    elif not last:
                        split_query(b + 1, 0)
                    if p + 2 < NP:
                        rotate(b, p + 2)
                    elif not last:
                        rotate(b + 1, p + 2 - NP)
                    if last and p == NP - 2:
                        variance(0)
                        normed2(0, True)
                    if last and p == NP - 1:
                        dve.wait_ge(f_hi_w, 1)
                        v.tensor_tensor(w1_lo[:, :], w1_nat, w1_hi[:, :].bitcast(F32), ALU.subtract).then_inc(f_w, 1)
                    if p in (0, 1, 4) and not last:
                        split_key(b + 1, (0, 1, 4).index(p))
                    if p == 2 and not first:
                        gate(b - 1, 0)
                    if p == 5 and not last:
                        split_q(b + 1, 0)
                        split_q(b + 1, 1)

            base = step[0]

            def chain(b, n, ins):
                ins.then_inc(vec_step, 1)
                dve.wait_ge(vec_step, 2 * b + base + n)

            def variance(b):
                for t in range(NT):
                    last = v.bn_stats(f_bn[:, t, :], x_sb[:, bass.ds((b * NT + t) * D, D)])
                chain(b, 1, last)
                carry_wait()
                for t in range(NT):
                    last = v.bn_aggr(f_stat[:, t, :], f_bn[:, t, :])
                chain(b, 2, last)
                v.tensor_scalar_add(f_var[:, :], f_stat[:, :, 1], LN_EPS).then_inc(f_var_done, 1)

            def normed2(b, first=False):
                dve.wait_ge(f_rstd_done, b + 1)
                v.scalar_tensor_tensor(out=f_shift[:, :], in0=f_stat[:, :, 0], scalar=-1.0, in1=f_rstd[:, :],
                                       op0=ALU.mult, op1=ALU.mult).then_inc(f_shifted, 1)
                if not first:
                    dve.wait_ge(f_scaled, b)
                dve.wait_ge(f_shifted, b + 1)
                for t in range(NT):
                    last = v.tensor_scalar(h2_n[:, t * D:t * D + D], x_sb[:, bass.ds((b * NT + t) * D, D)],
                                           f_rstd[:, t:t + 1], f_shift[:, t:t + 1], ALU.mult, ALU.add)
                last.then_inc(f_xhat, 1)

            split_latent(0)
            for part in range(2):
                split_q(0, part)
            for part in range(3):
                split_key(0, part)
            rotate(0, 0)
            rotate(0, 1)
            split_query(0, 0)
            attention(0, first=True)
            with dve.Fori(1, B - 1) as b:
                attention(b)
            attention(B - 1, last=True)
            invert(B - 1, NP - 1)
            split_o(B - 1, NP - 3)
            split_pt(B - 1, NP - 2)
            split_o(B - 1, NP - 2)
            split_pt(B - 1, NP - 1)
            split_o(B - 1, NP - 1)
            for t in range(NT):
                gate(B - 1, t)
            leave(dve, "vector")

            enter(dve, "vector", 3)
            dve.wait_ge(ld_ffn_small, 16 * 4)
            v.tensor_scalar(rb_col[:, 1:2], rb_col[:, 0:1], 0.5, None, ALU.mult)
            def score(b, slot):
                dve.wait_ge(f_h2, b + 1)
                if not isinstance(b, int) or b >= 2:
                    dve.wait_ge(f_tanh, b - 1)
                carry_wait()
                for t in range(NT):
                    last = v.tensor_tensor_reduce(out=rout_junk[:, t, :], in0=h2[:, slot, t * D:t * D + D], in1=rw_row[:, :],
                                                  scale=1.0, scalar=0.0, op0=ALU.mult, op1=ALU.add,
                                                  accum_out=rout[:, slot, t:t + 1])
                last.then_inc(f_rout, 1)

            def split_h(b):
                dve.wait_ge(f_hhi, b + 1)
                v.tensor_tensor(h2_lo[:, :], bank[6][:, :], h2_hi[:, :].bitcast(F32), ALU.subtract).then_inc(f_hsplit, 1)

            def split_act(b, g):
                dve.wait_ge(f_act, (NF // 2) * b + g + 1)
                a = slice(g * 512, g * 512 + 512)
                v.tensor_tensor(act_lo[:, a], act_full[:, a], act_hi[:, a].bitcast(F32), ALU.subtract).then_inc(f_lo, 1)

            def mix(b, slot):
                dve.wait_ge(f_down, b + 1)
                if not isinstance(b, int) or b >= 1:
                    dve.wait_ge(f_gated, b)
                for t in range(NT):
                    v.tensor_tensor(f_sum[:, t * D:t * D + D], bank[4 + t][:, 0:D], b2_row[:, :], ALU.add)
                dve.wait_ge(f_tanh, b + 1)
                last = v.tensor_scalar(rout_w[:, slot, :], rout_t[:, slot, :], 1.0, 0.5, ALU.add, ALU.mult)
                last.then_inc(f_summed, 1)
                dve.wait_ge(f_summed, b + 1)
                for t in range(NT):
                    last = v.scalar_tensor_tensor(out=f_mix[:, t * D:t * D + D], in0=f_sum[:, t * D:t * D + D],
                                                  scalar=rout_w[:, slot, t:t + 1], in1=h2[:, slot, t * D:t * D + D],
                                                  op0=ALU.mult, op1=ALU.add)
                last.then_inc(f_mixed, 1)

            def feed(b, slot, first=False, last=False):
                if not first:
                    mix(b - 1, 1 - slot)
                if not last:
                    variance(b + 1)
                split_act(b, 0)
                if not last:
                    normed2(b + 1)
                split_act(b, 1)
                split_act(b, 2)
                split_act(b, 3)
                if not last:
                    score(b + 1, 1 - slot)
                    split_h(b + 1)

            split_h(0)
            score(0, 0)
            dve.wait_ge(f_hi_w, 2)
            v.tensor_tensor(w2_lo[:, :], w2_nat, w2_hi[:, :].bitcast(F32), ALU.subtract).then_inc(f_w, 1)
            feed(0, 0, first=True)
            feed(1, 1)
            with dve.Fori(1, B // 2 - 1) as i:
                feed(2 * i, 0)
                feed(2 * i + 1, 1)
            feed(B - 2, 0)
            feed(B - 1, 1, last=True)
            mix(B - 1, 1)

        @block.scalar
        def _(act):
            a = nc.scalar.activation
            act.dma_start(c_nat[:, 0, :], c).then_inc(ld_c, 16)
            act.dma_start(mask_pad[:, :], mask_in).then_inc(ld_small, 16)
            act.dma_start(rope[:, :], rope_rows).then_inc(ld_small, 16)
            act.dma_start(rope_tok[:, :, :], rope_tokens.rearrange("(t p) n -> p t n", p=P)).then_inc(ld_small, 16)
            act.dma_start(qw[:, 0:1], q_norm_w[0:P].rearrange("(p a) -> p a", a=1)).then_inc(ld_small, 16)
            act.dma_start(qw[0:KW1, 1:2], q_norm_w[P:QL].rearrange("(p a) -> p a", a=1)).then_inc(ld_small, 16)
            act.wait_ge(ld_c, 16)
            a(c_nat[:, 1, :], c_nat[:, 0, :], ACT.Exp, scale=-1.0).then_inc(exp_c, 1)
            for k in range(KD):
                act.wait_ge(s_wa_t, k + 1)
                a(wa_hi[:, k * WA:k * WA + WA], bank[k][:, 0:WA], ACT.Copy).then_inc(s_wa_hi, 1)
            for n in range(NP):
                act.wait_ge(s_wo_t, n + 1)
                a(wo_t[:, 2 * n:2 * n + 2, :].rearrange("p h o -> p (h o)"), bank[n % 2][:, :], ACT.Copy).then_inc(s_wo_sb, 1)
            act.wait_ge(ld_small, 16 * 5)
            for n in range(NP):
                act.wait_ge(s_wout, n + 1)
                a(wout_hi[:, n * D:n * D + D], bank[2 + n % 2][:, 0:D], ACT.Copy).then_inc(s_wout_hi, 1)
                act.wait_ge(s_wq, n + 1)
                q, w = bank[4 + n % 2], slice(n * 256, n * 256 + 256)
                a(wq_hi0[:, w], q[:, 0:256], ACT.Copy, scale=qw[:, 0:1])
                a(wq_hl1[0:KW1, w], q[0:KW1, 256:512], ACT.Copy, scale=qw[0:KW1, 1:2]).then_inc(s_wq_hi, 1)
            leave(act, "scalar")

            enter(act, "scalar", 1)

            def modulated(b, s):
                act.wait_ge(p_ht, b + 1)
                act.wait_ge(p_mod, b + 1)
                if not isinstance(b, int) or b >= 2:
                    act.wait_ge(p_split, b - 1)
                    act.wait_ge(p_proj, b - 1)
                for dst, k in ((h_hi, 0), (h_hi, 1), (h_t, 0), (h_t, 1)):
                    last = a(dst[:, s, k * S:k * S + S], bank[s][:, k * S:k * S + S], ACT.Identity,
                             bias=mod_col[:, s, k:k + 1], scale=mod_col[:, s, 2 + k:3 + k])
                last.then_inc(p_hsb, 1)

            def squares(b, s):
                act.wait_ge(p_proj, b + 1)
                if not isinstance(b, int) or b >= 2:
                    act.wait_ge(p_rms, b - 1)
                for t in range(NT):
                    src = bank[2 + 2 * s + t]
                    a(sq_junk[:, s, t, 0:QL], src[:, 0:QL], ACT.Square, accum_out=sumsq[:, s, 2 * t:2 * t + 1])
                    last = a(sq_junk[:, s, t, QL:QL + KL], src[:, QL:QL + KL], ACT.Square, accum_out=sumsq[:, s, 2 * t + 1:2 * t + 2])
                last.then_inc(p_sq, 1)

            def keep_rows(b):
                act.wait_ge(p_t, b + 1)
                cols = bass.ds(b * S, S)
                a(qn_t0[:, cols], bank[6][:, 0:S], ACT.Copy)
                a(qn_t1[0:KW1, cols], bank[6][0:KW1, S:2 * S], ACT.Copy)
                a(key_t[:, cols], bank[7][:, 0:S], ACT.Copy).then_inc(p_kept, 1)

            def two_batches(i):
                for s in range(2):
                    b = 2 * i + s
                    if not last_batches(b, 2):
                        modulated(b + 2, s)
                    if not last_batches(b, 1):
                        squares(b + 1, 1 - s)
                    if not isinstance(b, int) or b >= 1:
                        keep_rows(b - 1)

            modulated(0, 0)
            modulated(1, 1)
            squares(0, 0)
            two_batches(0)
            with act.Fori(1, B // 2 - 2) as i:
                two_batches(i)
            two_batches(B // 2 - 2)
            two_batches(B // 2 - 1)
            keep_rows(B - 1)
            leave(act, "scalar")

            enter(act, "scalar", 2)

            def round_q(b, part):
                src = bass.ds(b * S, S)
                if part == 0:
                    if not isinstance(b, int) or b >= 1:
                        act.wait_ge(a_qgen, NP * b)
                    last = a(q_hi0[:, :], qn_t0[:, src], ACT.Copy)
                else:
                    a(q_hi1[0:KW1, :], qn_t1[0:KW1, src], ACT.Copy)
                    last = a(q_hi1[KW1:P, :], qn_t1[0:KW1, src], ACT.Copy)
                last.then_inc(q_hi_done, 1)

            def round_key(b, part):
                if part == 0 and (not isinstance(b, int) or b >= 2):
                    act.wait_ge(a_score, 2 * NP * (b - 1))
                src, dst = bass.ds(b * S, S), bass.ds((b % 2) * S, S)
                to, of = ((key_hi[:, 0, dst], key_t[:, src]),
                          (key_hi[0:64, 1, dst], key_t[64:128, src]),
                          (key_hi[64:128, 1, dst], key_t[0:64, src]))[part]
                a(to, of, ACT.Copy).then_inc(k_hi_done, 1)

            def round_query(b, p):
                u = NP * b + p
                act.wait_ge(a_query, u + 1)
                if not isinstance(b, int) or u >= 2:
                    act.wait_ge(a_score, 2 * (u - 1))
                a(query_hi[:, p % 2, :], query[:, p % 2, :], ACT.Copy).then_inc(a_qhi, 1)

            def latent_rows(b, p):
                u = NP * b + p
                act.wait_ge(a_rot, u + 1)
                if not isinstance(b, int) or u >= 2:
                    act.wait_ge(a_qlo, u - 1)
                src = bank[(0, 6)[p % 2]]
                a(query[0:64, p % 2, 0:S], src[0:64, 0:S], ACT.Copy)
                a(query[64:128, p % 2, S:2 * S], src[64:128, 0:S], ACT.Copy).then_inc(a_latq, 1)

            def exps(b, p, j):
                u = NP * b + p
                if j == 0 and (not isinstance(b, int) or u >= 2):
                    act.wait_ge(a_ptr, 2 * (u - 1))
                    act.wait_ge(a_inv, u - 1)
                act.wait_ge(a_masked, 2 * u + j + 1)
                for t, c in enumerate((slice(0, P), slice(P, SCORE))):
                    n = 2 * j + t
                    last = a(probs[:, p % 2, j, c], scored[:, p % 2, j, c], ACT.Exp, scale=-1.0,
                             bias=row_min[:, p % 2, n:n + 1], accum_out=row_sum[:, p % 2, n:n + 1])
                last.then_inc(a_exp, 1)

            def round_pt(b, p):
                u = NP * b + p
                for j in range(2):
                    act.wait_ge(a_ptr, 2 * u + j + 1)
                    if j == 0 and (not isinstance(b, int) or u >= 1):
                        act.wait_ge(a_pv, u)
                    a(pt_hi[:, j, :], bank[3 + j][:, 0:SCORE], ACT.Copy).then_inc(a_pthi, 1)

            def round_latent(b):
                if not isinstance(b, int) or b >= 1:
                    act.wait_ge(a_pv, NP * b)
                a(lat_hi[:, :], lat[:, bass.ds(b * NT * KL, NT * KL)], ACT.Copy).then_inc(l_hi_done, 1)

            def round_o(b, p):
                u = NP * b + p
                act.wait_ge(a_pv, u + 1)
                if not isinstance(b, int) or u >= 1:
                    act.wait_ge(a_out, u)
                a(o_hi[0:64, :], bank[5][0:64, 0:S], ACT.Copy)
                a(o_hi[64:128, :], bank[5][0:64, S:2 * S], ACT.Copy).then_inc(a_ohi, 1)

            def before(b, p, lag):
                return (b, p - lag) if p >= lag else (b - 1, p - lag + NP)

            def attention(b, first=False, last=False):
                for p in range(NP):
                    if p + 1 < NP:
                        latent_rows(b, p + 1)
                    elif not last:
                        latent_rows(b + 1, 0)
                    if not first or p >= 3:
                        round_o(*before(b, p, 3))
                    if p == 2 and not first:
                        round_latent(b)
                    if not first or p >= 2:
                        round_pt(*before(b, p, 2))
                    if p + 1 < NP:
                        round_query(b, p + 1)
                    elif not last:
                        round_query(b + 1, 0)
                    exps(b, p, 0)
                    if p in (0, 1, 4) and not last:
                        round_key(b + 1, (0, 1, 4).index(p))
                    if p == 5 and not last:
                        round_q(b + 1, 0)
                        round_q(b + 1, 1)
                    exps(b, p, 1)
                    if last and p >= NP - 2:
                        w, (hi, nat) = p - NP + 2, ((w1_hi, w1_nat), (w2_hi, w2_nat))[p - NP + 2]
                        act.wait_ge(a_qgen, NP * B)
                        act.wait_ge(ld_ffn[w], 16)
                        a(hi[:, :], nat, ACT.Copy).then_inc(f_hi_w, 1)

            round_latent(0)
            for part in range(2):
                round_q(0, part)
            for part in range(3):
                round_key(0, part)
            latent_rows(0, 0)
            round_query(0, 0)
            attention(0, first=True)
            with act.Fori(1, B - 1) as b:
                attention(b)
            attention(B - 1, last=True)
            round_o(B - 1, NP - 3)
            round_pt(B - 1, NP - 2)
            round_o(B - 1, NP - 2)
            round_pt(B - 1, NP - 1)
            round_o(B - 1, NP - 1)
            leave(act, "scalar")

            enter(act, "scalar", 3)

            def round_h(b, first=False):
                act.wait_ge(f_ht, b + 1)
                if not first:
                    act.wait_ge(f_up, (NF // 2) * b)
                a(h2_hi[:, :], bank[6][:, :], ACT.Copy).then_inc(f_hhi, 1)

            def gelus(b, first=False):
                if not first:
                    act.wait_ge(f_down, b)
                for g in range(NF // 2):
                    act.wait_ge(f_up, (NF // 2) * b + g + 1)
                    for j in range(2):
                        f = 2 * g + j
                        for dst in (act_hi, act_full):
                            last = a(dst[:, f * S:f * S + S], bank[g][:, j * S:j * S + S], ACT.Gelu_apprx_tanh, bias=b1_col[:, f:f + 1])
                    last.then_inc(f_act, 1)

            def router(b, slot):
                act.wait_ge(f_rout, b + 1)
                if not isinstance(b, int) or b >= 2:
                    act.wait_ge(f_mixed, b - 1)
                a(rout_t[:, slot, :], rout[:, slot, :], ACT.Tanh, bias=rb_col[:, 1:2], scale=0.5).then_inc(f_tanh, 1)

            round_h(0, True)
            router(0, 0)
            gelus(0, True)
            router(1, 1)
            round_h(1)
            with act.Fori(0, (B - 2) // 2) as i:
                for slot in range(2):
                    gelus(2 * i + 1 + slot)
                    router(2 * i + 2 + slot, slot)
                    round_h(2 * i + 2 + slot)
            gelus(B - 1)

        @block.gpsimd
        def _(pool):
            g = nc.gpsimd
            step = [0]

            def link(ins):
                step[0] += 1
                ins.then_inc(pool_step, 1)
                pool.wait_ge(pool_step, step[0])

            pool.dma_start(kw_row[:, :], kv_norm_w.rearrange("(a n) -> a n", a=1).broadcast_to([P, KL])).then_inc(ld_kwr, 16)
            g.memset(half_neg[:, :], -0.5)
            g.memset(rms_eps[:, :], RMS_EPS)
            for t in range(NT):
                g.memset(inv_n[:, 2 * t:2 * t + 1], 1.0 / QL)
                g.memset(inv_n[:, 2 * t + 1:2 * t + 2], 1.0 / KL)
            pool.wait_ge(ld_kwr, 16)
            pool.wait_ge(ld_kv, 16)
            g.tensor_tensor(wkv_nat[:, :, :], wkv_nat[:, :, :],
                            kw_row[:, :].rearrange("p (a c) -> p a c", a=1).broadcast_to([P, 2 * NH, KL]), ALU.mult).then_inc(kv_scaled, 1)

            def token_rstd(q):
                c = slice(q * B // 2, (q + 1) * B // 2)
                pool.wait_ge(var_done, q + 1)
                g.tensor_tensor(tok_rstd[:, c], tok_var[:, c], half_neg[:, c], ALU.pow).then_inc(rstd_done, 1)

            token_rstd(0)
            pool.wait_ge(rstd_done, 1)
            leave(pool, "gpsimd")

            enter(pool, "gpsimd", 1)
            base = step[0]

            def rms(b, s):
                pool.wait_ge(p_sq, b + 1)
                g.tensor_tensor(rms_mid[:, s, :], sumsq[:, s, :], inv_n[:, :], ALU.mult).then_inc(pool_step, 1)
                pool.wait_ge(pool_step, 2 * b + base + 1)
                g.tensor_tensor(rms_var[:, s, :], rms_mid[:, s, :], rms_eps[:, :], ALU.add).then_inc(pool_step, 1)
                pool.wait_ge(pool_step, 2 * b + base + 2)
                if not isinstance(b, int) or b >= 2:
                    pool.wait_ge(p_rows, b - 1)
                g.tensor_tensor(rms_r[:, s, :], rms_var[:, s, :], half_neg[:, 0:2 * NT], ALU.pow).then_inc(p_rms, 1)

            def finish_keys(b, s):
                pool.wait_ge(p_rows, b + 1)
                g.tensor_copy(lat[:, bass.ds(b * NT * KL, NT * KL)].rearrange("p (t c) -> p t c", t=NT),
                              keys[:, s, :].rearrange("p (t c) -> p t c", t=NT)[:, :, 0:KL])
                for t in range(NT):
                    def runs(a):
                        return a.rearrange("p (h g j) -> p h g j", h=2, g=2)
                    dst = keys[:, s, t * P + KL:t * P + P].rearrange("p (g h j) -> p h g j", g=2, h=2)
                    last = g.tensor_tensor(dst, runs(kr_cos[:, s, t * DR:t * DR + DR]), runs(kr_sin[:, s, t * DR:t * DR + DR]), ALU.add)
                last.then_inc(p_norm, 1)

            def two_batches(i):
                for s in range(2):
                    b = 2 * i + s
                    if not last_batches(b, 1):
                        rms(b + 1, 1 - s)
                    finish_keys(b, s)

            token_rstd(1)
            rms(0, 0)
            two_batches(0)
            token_rstd(2)
            two_batches(1)
            token_rstd(3)
            with pool.Fori(2, B // 2 - 2) as i:
                two_batches(i)
            two_batches(B // 2 - 2)
            two_batches(B // 2 - 1)
            step[0] += 2 * B
            pool.wait_ge(p_norm, B)
            leave(pool, "gpsimd")

            enter(pool, "gpsimd", 2)
            pool.sem_inc(gated_free, 1)
            base_u = step[0]

            def finish_rope(b, p):
                u = NP * b + p
                pool.wait_ge(a_rot, u + 1)
                g.tensor_tensor(pe_rot[:, p % 2, :], pe_rot[:, p % 2, :], rope[:, S:2 * S], ALU.mult).then_inc(pool_step, 1)
                pool.wait_ge(pool_step, 2 * u + base_u + 1)
                pool.wait_ge(a_latq, u + 1)
                g.tensor_tensor(query[0:64, p % 2, S:2 * S], pe_rot[0:64, p % 2, :], pe_cos[0:64, p % 2, :], ALU.add).then_inc(pool_step, 1)
                pool.wait_ge(pool_step, 2 * u + base_u + 2)
                g.tensor_tensor(query[64:128, p % 2, 0:S], pe_rot[64:128, p % 2, :], pe_cos[64:128, p % 2, :], ALU.add).then_inc(a_query, 1)
                pool.wait_ge(a_query, u + 1)

            def normalise(b, p):
                u = NP * b + p
                pool.wait_ge(a_inv, u + 1)
                inv = row_inv[:, p % 2, :].rearrange("p (h t) -> p h t", h=2)
                for t, (c0, n) in enumerate(((0, P), (P, S))):
                    part = probs[:, p % 2, :, c0:c0 + n]
                    last = g.tensor_tensor(part, part, inv[:, :, t:t + 1].broadcast_to([P, 2, n]), ALU.mult)
                last.then_inc(a_norm, 1)

            def rstd(b):
                pool.wait_ge(f_var_done, b + 1)
                g.tensor_tensor(f_rstd[:, :], f_var[:, :], half_neg[:, 0:NT], ALU.pow).then_inc(f_rstd_done, 1)

            def modulate(b, slot, nth):
                pool.wait_ge(ld_modh[slot], 16 * nth)
                pool.wait_ge(f_xhat, b + 1)
                for t in range(NT):
                    last = g.tensor_tensor(h2_m[:, t * D:t * D + D], h2_n[:, t * D:t * D + D], mod_h[:, slot, 0:D], ALU.mult)
                last.then_inc(f_scaled, 1)
                pool.wait_ge(f_scaled, b + 1)
                if not isinstance(b, int) or b >= 2:
                    pool.wait_ge(f_mixed, b - 1)
                for t in range(NT):
                    last = g.tensor_tensor(h2[:, slot, t * D:t * D + D], h2_m[:, t * D:t * D + D], mod_h[:, slot, D:2 * D], ALU.add)
                last.then_inc(f_h2, 1)
                pool.wait_ge(f_h2, b + 1)

            def add_out(b):
                pool.wait_ge(a_gated, b + 1)
                rows = x_sb[:, bass.ds(b * NT * D, NT * D)]
                g.tensor_tensor(rows, rows, gated[:, :], ALU.add).then_inc(gated_free, 1)
                pool.wait_ge(gated_free, b + 2)

            def attention(b, first=False, last=False):
                for p in range(NP):
                    if p + 1 < NP:
                        finish_rope(b, p + 1)
                    elif not last:
                        finish_rope(b + 1, 0)
                    if not first or p >= 1:
                        normalise(b, p - 1) if p else normalise(b - 1, NP - 1)
                    if p == 4 and not first:
                        add_out(b - 1)
                    if last and p == NP - 2:
                        rstd(0)

            finish_rope(0, 0)
            attention(0, first=True)
            with pool.Fori(1, B - 1) as b:
                attention(b)
            attention(B - 1, last=True)
            normalise(B - 1, NP - 1)
            modulate(0, 0, 1)
            add_out(B - 1)
            leave(pool, "gpsimd")

            enter(pool, "gpsimd", 3)

            def finish(b, slot, before):
                pool.wait_ge(f_mixed, b + 1)
                pool.wait_ge(ld_modg[slot], 16 * (before + 1))
                if not isinstance(before, int) or before:
                    pool.wait_ge(stored[slot], 16 * before)
                for t in range(NT):
                    last = g.tensor_tensor(f_gate[:, t * D:t * D + D], f_mix[:, t * D:t * D + D], mod_g[:, slot, :], ALU.mult)
                last.then_inc(f_gated, 1)
                pool.wait_ge(f_gated, b + 1)
                g.tensor_tensor(f_out[:, slot, :], f_gate[:, :], x_sb[:, bass.ds(b * NT * D, NT * D)], ALU.add).then_inc(f_done, 1)
                pool.wait_ge(f_done, b + 1)

            def feed(i, slot, last=False):
                b = 2 * i + slot
                if not last:
                    rstd(b + 2)
                    modulate(b + 2, slot, i + 2)
                finish(b, slot, i)

            rstd(1)
            modulate(1, 1, 1)
            feed(0, 0)
            feed(0, 1)
            with pool.Fori(1, B // 2 - 1) as i:
                feed(i, 0)
                feed(i, 1)
            feed(B // 2 - 1, 0, last=True)
            feed(B // 2 - 1, 1, last=True)


INS = ['L0_attn_hidden_states', 'L0_attn_wq_a', 'L0_attn_q_norm_w', 'L0_attn_wq_b', 'L0_attn_wkv_a', 'L0_attn_kv_norm_w',
       'L0_attn_wkv_b', 'L0_attn_wo', 'L0_ffn_router_weight', 'L0_ffn_router_bias', 'L0_ffn_w1', 'L0_ffn_b1', 'L0_ffn_w2',
       'L0_ffn_b2', 'L0_c', 'L0_wmod']


def shape_constants():
    f = np.float32
    inv = (f(1.0) / np.power(f(10000.0), np.arange(0, DR, 2, dtype=f) / f(DR))).astype(f)
    angle = (np.arange(S, dtype=f)[:, None] * inv[None, :]).astype(f)
    cos, sin = np.cos(angle).astype(f), np.sin(angle).astype(f)
    tokens = np.concatenate([cos, cos, -sin, sin], axis=1)
    row = [(half, g * 16 + j) for half, g in RUNS for j in range(16)] * 2
    rows = np.stack([np.concatenate([cos[:, d], sin[:, d] if half else -sin[:, d]]) for half, d in row])
    masks = np.zeros((P, 2 * P), f)
    masks[:, P:] = np.where(np.tril(np.ones((P, P), bool)), f(0), f(MASKED))
    return {"ident": np.eye(P, dtype=f), "mask": masks, "rope_rows": rows.astype(f), "rope_tokens": tokens.astype(f)}


def kernel(**inputs):
    import concourse.bacc as _bacc
    from concourse.bass_utils import run_bass_kernel_spmd as _run

    nc = _bacc.Bacc("TRN2", target_bir_lowering=False, num_devices=1)
    arrays, args = {}, []
    given = {n: np.asarray(inputs[n]) for n in INS}
    given["L0_ffn_b1"] = given["L0_ffn_b1"].reshape(NF, P).T
    given = [(n, np.ascontiguousarray(a)) for n, a in given.items()] + list(shape_constants().items())
    for name, a in given:
        arrays[f"in_{name}"] = a
        args.append(nc.dram_tensor(f"in_{name}", a.shape, mybir.dt.from_np(a.dtype), kind="ExternalInput").ap())
    result = nc.dram_tensor("out_x", (B, S, D), F32, kind="ExternalOutput").ap()
    adaln_layer(nc, *args, result)
    return _run(nc, [arrays], core_ids=[0]).results[0]["out_x"]
```
